# Optimizing a Trainium2 kernel written in Bass

```python
import numpy as np
import jax
import jax.numpy as jnp

def _softmax(x, axis=-1):
    return jax.nn.softmax(x, axis=axis)

def _gelu(x):
    return jax.nn.gelu(x, approximate=True)

def _silu(x):
    return jax.nn.silu(x)

def _sigmoid(x):
    return jax.nn.sigmoid(x)

def _layernorm(x, axis=-1, eps=1e-05):
    m = jnp.mean(x, axis=axis, keepdims=True)
    v = jnp.var(x, axis=axis, keepdims=True)
    return (x - m) / jnp.sqrt(v + eps)

def _scatter_add(tgt, idx, src, axis=0):
    return tgt.at[idx].add(src)

def _segment_sum(src, seg, n):
    return jax.ops.segment_sum(src, seg, n)
kernel_name = 'mk_gnn_resnorm_d2_gnn_r8_f70c3b'

def setup_inputs(seed: int=0):
    np.random.seed(seed)
    _w = jnp.asarray

    def _rec_inputs():
        import jax
        import jax.numpy as jnp
        _gk = jax.random.key(seed)
        x = -8.776e-05 + 1 * jax.random.normal(jax.random.fold_in(_gk, 1), (1250, 512), jnp.float32)
        _s = jax.random.randint(jax.random.fold_in(_gk, 2), (10000,), 0, 1250, jnp.int32)
        _d = jax.random.randint(jax.random.fold_in(_gk, 3), (10000,), 0, 1250, jnp.int32)
        _loop = jnp.arange(1250, dtype=jnp.int32)
        src = jnp.concatenate([_s, _d, _loop])
        dst = jnp.concatenate([_d, _s, _loop])
        _o = jnp.argsort(dst, stable=True)
        src = src[_o]
        dst = dst[_o]
        node_vec1 = jax.random.uniform(jax.random.fold_in(_gk, 13), (1250, 1), jnp.float32, 0.0, 0.999957)
        return (x, src, dst, node_vec1)
    x, src, dst, node_vec1 = _rec_inputs()

    def _L0_gnn_setup():
        import jax, jax.numpy as jnp
        import numpy as np
        N_NODES = 1250
        N_EDGES = 20000
        D_IN = 512
        D_HID = 1024
        key = jax.random.key(seed)
        ks = jax.random.split(key, 8)
        feat = jax.random.normal(ks[0], (N_NODES, D_IN), dtype=jnp.float32)
        W1 = jax.random.normal(ks[1], (D_IN, D_HID), dtype=jnp.float32) * (1.0 / np.sqrt(D_IN))
        b1 = jnp.zeros((D_HID,), dtype=jnp.float32)
        W2 = jax.random.normal(ks[2], (D_HID, D_IN), dtype=jnp.float32) * (1.0 / np.sqrt(D_HID))
        b2 = jnp.zeros((D_IN,), dtype=jnp.float32)
        eps = jnp.zeros((1,), dtype=jnp.float32)
        src = jax.random.randint(ks[3], (N_EDGES,), 0, N_NODES, dtype=jnp.int32)
        dst = jax.random.randint(ks[4], (N_EDGES,), 0, N_NODES, dtype=jnp.int32)
        return {'feat': feat, 'W1': W1, 'b1': b1, 'W2': W2, 'b2': b2, 'eps': eps, 'src': src, 'dst': dst}
    _L0_gnn_all = _L0_gnn_setup()
    _L0_gnn_in = {k: v for k, v in _L0_gnn_all.items() if k in ('W1', 'b1', 'W2', 'b2', 'eps')}
    del _L0_gnn_all

    def _L1_gnn_setup():
        import jax, jax.numpy as jnp
        import numpy as np
        N_NODES = 40962
        LATENT_DIM = 512
        N_EDGES = 81924
        NUM_BLOCKS = 4
        NUM_HEADS = 4
        NUM_FREQ = 32
        BASE_PERIOD = 16
        NOISE_EMB_DIM = 16
        EPS = 1e-05

        def _cond_layer_norm(x, cond, sw, sb, bw, bb):
            mu = jnp.mean(x, axis=-1, keepdims=True)
            var = jnp.var(x, axis=-1, keepdims=True)
            xn = (x - mu) * jax.lax.rsqrt(var + EPS)
            scale = cond @ sw + sb
            bias = cond @ bw + bb
            return xn * (1.0 + scale) + bias

        def _sparse_attention(x, src, dst, wq, bq, wk, bk, wv, bv, wo, bo):
            N, D = x.shape
            H, Dh = (NUM_HEADS, D // NUM_HEADS)
            q = (x @ wq + bq).reshape(N, H, Dh) * Dh ** (-0.5)
            k = (x @ wk + bk).reshape(N, H, Dh)
            v = (x @ wv + bv).reshape(N, H, Dh)
            scores = jnp.einsum('ehd,ehd->eh', q[src], k[dst])
            smax = jax.ops.segment_max(scores, src, num_segments=N)
            ex = jnp.exp(scores - smax[src])
            denom = jax.ops.segment_sum(ex, src, num_segments=N)
            attn = ex / denom[src]
            out = jax.ops.segment_sum(attn[:, :, None] * v[dst], src, num_segments=N)
            return out.reshape(N, D) @ wo + bo

        def _forward(x, edge_index, noise_levels, f_w1, f_b1, f_w2, f_b2, s1_w, s1_b, b1_w, b1_b, wq, bq, wk, bk, wv, bv, wo, bo, s2_w, s2_b, b2_w, b2_b, m_w1, m_b1, m_w2, m_b2):
            src, dst = (edge_index[0], edge_index[1])
            freqs = jnp.arange(1, NUM_FREQ + 1, dtype=x.dtype) * (2.0 * np.pi / BASE_PERIOD)
            ph = noise_levels * freqs
            emb = jnp.concatenate([jnp.sin(ph), jnp.cos(ph)], axis=-1)
            cond = jax.nn.silu(emb @ f_w1 + f_b1) @ f_w2 + f_b2
            for i in range(NUM_BLOCKS):
                y = _cond_layer_norm(x, cond, s1_w[i], s1_b[i], b1_w[i], b1_b[i])
                y = _sparse_attention(y, src, dst, wq[i], bq[i], wk[i], bk[i], wv[i], bv[i], wo[i], bo[i])
                x = x + y
                y = _cond_layer_norm(x, cond, s2_w[i], s2_b[i], b2_w[i], b2_b[i])
                y = jax.nn.relu(y @ m_w1[i] + m_b1[i]) @ m_w2[i] + m_b2[i]
                x = x + y
            return x
        key = jax.random.key(seed)
        ks = jax.random.split(key, 20)

        def w(k, shape, s=0.02):
            return jax.random.normal(k, shape, dtype=jnp.float32) * s
        D, B, C = (LATENT_DIM, NUM_BLOCKS, NOISE_EMB_DIM)
        z = lambda *s: jnp.zeros(s, jnp.float32)
        return {'latent_mesh_nodes': jax.random.normal(ks[0], (N_NODES, D), dtype=jnp.float32), 'edge_index': jax.random.randint(ks[1], (2, N_EDGES), 0, N_NODES, dtype=jnp.int32), 'noise_levels': jax.random.uniform(ks[2], (N_NODES, 1), dtype=jnp.float32), 'f_w1': w(ks[3], (2 * NUM_FREQ, C)), 'f_b1': z(C), 'f_w2': w(ks[4], (C, C)), 'f_b2': z(C), 's1_w': w(ks[5], (B, C, D)), 's1_b': z(B, D), 'b1_w': w(ks[6], (B, C, D)), 'b1_b': z(B, D), 'wq': w(ks[7], (B, D, D)), 'bq': z(B, D), 'wk': w(ks[8], (B, D, D)), 'bk': z(B, D), 'wv': w(ks[9], (B, D, D)), 'bv': z(B, D), 'wo': w(ks[10], (B, D, D)), 'bo': z(B, D), 's2_w': w(ks[11], (B, C, D)), 's2_b': z(B, D), 'b2_w': w(ks[12], (B, C, D)), 'b2_b': z(B, D), 'm_w1': w(ks[13], (B, D, D)), 'm_b1': z(B, D), 'm_w2': w(ks[14], (B, D, D)), 'm_b2': z(B, D)}
    _L1_gnn_all = _L1_gnn_setup()
    _L1_gnn_in = {k: v for k, v in _L1_gnn_all.items() if k in ('f_w1', 'f_b1', 'f_w2', 'f_b2', 's1_w', 's1_b', 'b1_w', 'b1_b', 'wq', 'bq', 'wk', 'bk', 'wv', 'bv', 'wo', 'bo', 's2_w', 's2_b', 'b2_w', 'b2_b', 'm_w1', 'm_b1', 'm_w2', 'm_b2')}
    del _L1_gnn_all
    return {'x': x, 'src': src, 'dst': dst, 'node_vec1': node_vec1, 'L0_gnn_W1': _L0_gnn_in['W1'], 'L0_gnn_b1': _L0_gnn_in['b1'], 'L0_gnn_W2': _L0_gnn_in['W2'], 'L0_gnn_b2': _L0_gnn_in['b2'], 'L0_gnn_eps': _L0_gnn_in['eps'], 'L1_gnn_f_w1': _L1_gnn_in['f_w1'], 'L1_gnn_f_b1': _L1_gnn_in['f_b1'], 'L1_gnn_f_w2': _L1_gnn_in['f_w2'], 'L1_gnn_f_b2': _L1_gnn_in['f_b2'], 'L1_gnn_s1_w': _L1_gnn_in['s1_w'], 'L1_gnn_s1_b': _L1_gnn_in['s1_b'], 'L1_gnn_b1_w': _L1_gnn_in['b1_w'], 'L1_gnn_b1_b': _L1_gnn_in['b1_b'], 'L1_gnn_wq': _L1_gnn_in['wq'], 'L1_gnn_bq': _L1_gnn_in['bq'], 'L1_gnn_wk': _L1_gnn_in['wk'], 'L1_gnn_bk': _L1_gnn_in['bk'], 'L1_gnn_wv': _L1_gnn_in['wv'], 'L1_gnn_bv': _L1_gnn_in['bv'], 'L1_gnn_wo': _L1_gnn_in['wo'], 'L1_gnn_bo': _L1_gnn_in['bo'], 'L1_gnn_s2_w': _L1_gnn_in['s2_w'], 'L1_gnn_s2_b': _L1_gnn_in['s2_b'], 'L1_gnn_b2_w': _L1_gnn_in['b2_w'], 'L1_gnn_b2_b': _L1_gnn_in['b2_b'], 'L1_gnn_m_w1': _L1_gnn_in['m_w1'], 'L1_gnn_m_b1': _L1_gnn_in['m_b1'], 'L1_gnn_m_w2': _L1_gnn_in['m_w2'], 'L1_gnn_m_b2': _L1_gnn_in['m_b2']}

def reference(x, src, dst, node_vec1, L0_gnn_W1, L0_gnn_b1, L0_gnn_W2, L0_gnn_b2, L0_gnn_eps, L1_gnn_f_w1, L1_gnn_f_b1, L1_gnn_f_w2, L1_gnn_f_b2, L1_gnn_s1_w, L1_gnn_s1_b, L1_gnn_b1_w, L1_gnn_b1_b, L1_gnn_wq, L1_gnn_bq, L1_gnn_wk, L1_gnn_bk, L1_gnn_wv, L1_gnn_bv, L1_gnn_wo, L1_gnn_bo, L1_gnn_s2_w, L1_gnn_s2_b, L1_gnn_b2_w, L1_gnn_b2_b, L1_gnn_m_w1, L1_gnn_m_b1, L1_gnn_m_w2, L1_gnn_m_b2):
    import jax
    import jax.numpy as jnp

    def _L0_gnn_ref(feat, W1, b1, W2, b2, eps, src, dst):
        import jax, jax.numpy as jnp
        import numpy as np
        N_NODES = 1250
        N_EDGES = 20000
        D_IN = 512
        D_HID = 1024
        msgs = feat[src]
        neigh = jax.ops.segment_sum(msgs, dst, num_segments=feat.shape[0])
        rst = (1.0 + eps[0]) * feat + neigh
        h = jnp.maximum(rst @ W1 + b1, 0.0)
        h = h @ W2 + b2
        return h + feat

    def _L1_gnn_ref(latent_mesh_nodes, edge_index, noise_levels, f_w1, f_b1, f_w2, f_b2, s1_w, s1_b, b1_w, b1_b, wq, bq, wk, bk, wv, bv, wo, bo, s2_w, s2_b, b2_w, b2_b, m_w1, m_b1, m_w2, m_b2):
        import jax, jax.numpy as jnp
        import numpy as np
        N_NODES = 40962
        LATENT_DIM = 512
        N_EDGES = 81924
        NUM_BLOCKS = 4
        NUM_HEADS = 4
        NUM_FREQ = 32
        BASE_PERIOD = 16
        NOISE_EMB_DIM = 16
        EPS = 1e-05

        def _cond_layer_norm(x, cond, sw, sb, bw, bb):
            mu = jnp.mean(x, axis=-1, keepdims=True)
            var = jnp.var(x, axis=-1, keepdims=True)
            xn = (x - mu) * jax.lax.rsqrt(var + EPS)
            scale = cond @ sw + sb
            bias = cond @ bw + bb
            return xn * (1.0 + scale) + bias

        def _sparse_attention(x, src, dst, wq, bq, wk, bk, wv, bv, wo, bo):
            N, D = x.shape
            H, Dh = (NUM_HEADS, D // NUM_HEADS)
            q = (x @ wq + bq).reshape(N, H, Dh) * Dh ** (-0.5)
            k = (x @ wk + bk).reshape(N, H, Dh)
            v = (x @ wv + bv).reshape(N, H, Dh)
            scores = jnp.einsum('ehd,ehd->eh', q[src], k[dst])
            smax = jax.ops.segment_max(scores, src, num_segments=N)
            ex = jnp.exp(scores - smax[src])
            denom = jax.ops.segment_sum(ex, src, num_segments=N)
            attn = ex / denom[src]
            out = jax.ops.segment_sum(attn[:, :, None] * v[dst], src, num_segments=N)
            return out.reshape(N, D) @ wo + bo

        def _forward(x, edge_index, noise_levels, f_w1, f_b1, f_w2, f_b2, s1_w, s1_b, b1_w, b1_b, wq, bq, wk, bk, wv, bv, wo, bo, s2_w, s2_b, b2_w, b2_b, m_w1, m_b1, m_w2, m_b2):
            src, dst = (edge_index[0], edge_index[1])
            freqs = jnp.arange(1, NUM_FREQ + 1, dtype=x.dtype) * (2.0 * np.pi / BASE_PERIOD)
            ph = noise_levels * freqs
            emb = jnp.concatenate([jnp.sin(ph), jnp.cos(ph)], axis=-1)
            cond = jax.nn.silu(emb @ f_w1 + f_b1) @ f_w2 + f_b2
            for i in range(NUM_BLOCKS):
                y = _cond_layer_norm(x, cond, s1_w[i], s1_b[i], b1_w[i], b1_b[i])
                y = _sparse_attention(y, src, dst, wq[i], bq[i], wk[i], bk[i], wv[i], bv[i], wo[i], bo[i])
                x = x + y
                y = _cond_layer_norm(x, cond, s2_w[i], s2_b[i], b2_w[i], b2_b[i])
                y = jax.nn.relu(y @ m_w1[i] + m_b1[i]) @ m_w2[i] + m_b2[i]
                x = x + y
            return x
        return _forward(latent_mesh_nodes, edge_index, noise_levels, f_w1, f_b1, f_w2, f_b2, s1_w, s1_b, b1_w, b1_b, wq, bq, wk, bk, wv, bv, wo, bo, s2_w, s2_b, b2_w, b2_b, m_w1, m_b1, m_w2, m_b2)
    edge_index = jnp.stack([src, dst])
    x = _layernorm(x + _L0_gnn_ref(x, L0_gnn_W1, L0_gnn_b1, L0_gnn_W2, L0_gnn_b2, L0_gnn_eps, src, dst), axis=-1)
    x = _layernorm(x + _L1_gnn_ref(x, edge_index, node_vec1, L1_gnn_f_w1, L1_gnn_f_b1, L1_gnn_f_w2, L1_gnn_f_b2, L1_gnn_s1_w, L1_gnn_s1_b, L1_gnn_b1_w, L1_gnn_b1_b, L1_gnn_wq, L1_gnn_bq, L1_gnn_wk, L1_gnn_bk, L1_gnn_wv, L1_gnn_bv, L1_gnn_wo, L1_gnn_bo, L1_gnn_s2_w, L1_gnn_s2_b, L1_gnn_b2_w, L1_gnn_b2_b, L1_gnn_m_w1, L1_gnn_m_b1, L1_gnn_m_w2, L1_gnn_m_b2), axis=-1)
    return x

_drawn_inputs = setup_inputs


def setup_inputs(seed=0):
    import zlib

    import numpy as np

    out = dict(_drawn_inputs(seed))
    spreads = {'L0_gnn_b1': (0.0, 0.419),
     'L0_gnn_b2': (0.0, 0.287),
     'L1_gnn_f_b1': (0.0, 0.8),
     'L1_gnn_f_b2': (0.0, 0.8),
     'L1_gnn_s1_b': (0.0, 0.682),
     'L1_gnn_b1_b': (0.0, 0.39),
     'L1_gnn_bq': (0.0, 0.8),
     'L1_gnn_bk': (0.0, 0.8),
     'L1_gnn_bv': (0.0, 0.1),
     'L1_gnn_bo': (0.0, 0.1),
     'L1_gnn_s2_b': (0.0, 0.552),
     'L1_gnn_b2_b': (0.0, 0.578),
     'L1_gnn_m_b1': (0.0, 0.1),
     'L1_gnn_m_b2': (0.0, 0.1)}
    factors = {'node_vec1': 8.0,
     'L1_gnn_f_w1': 8.0,
     'L1_gnn_f_w2': 8.0,
     'L1_gnn_s1_w': 8.0,
     'L1_gnn_b1_w': 8.0,
     'L1_gnn_wq': 7.564,
     'L1_gnn_wk': 7.442,
     'L1_gnn_s2_w': 8.0,
     'L1_gnn_b2_w': 8.0}
    for name, (base, spread) in spreads.items():
        noise = np.random.default_rng([zlib.crc32(name.encode()), seed]).standard_normal(out[name].shape)
        drawn = base * np.exp(spread * noise) if base else spread * noise
        out[name] = jnp.asarray(drawn.astype(out[name].dtype))
    for name, factor in factors.items():
        out[name] = (out[name] * factor).astype(out[name].dtype)
    return out
```

```python
from contextlib import ExitStack

import numpy as np

import concourse.bass as bass
from concourse import mybir

ALU = mybir.AluOpType
ACT = mybir.ActivationFunctionType
AX = mybir.AxisListType
F32 = mybir.dt.float32
F32R = mybir.dt.float32r
BF16 = mybir.dt.bfloat16
F16 = mybir.dt.float16
I32 = mybir.dt.int32

P = 128
N = 1250
D = 512
E = 21250
H1 = 1024
L = 4
H = 4
KD = D // P
NT = -(-N // P)
NP = NT * P
ET = 125
NE = E // ET
NEP = 2 * NE
NOTHING = -1e30
LOWEST = -1e29
EPS = 1e-5
BANK = 512
ROUND = 12582912.0
TWO_PI = (6.28125, 0.0019353071693331003, 1.0253131677018246e-11)
GROUPS = [(0, 512), (512, 512), (1024, N - 1024)]
TILES_OF = [range(0, 4), range(4, 8), range(8, NT)]
NG = NT // 2
UNITS = [(g, h, s) for g in range(NG) for h in range(H) for s in range(2)]


def rows(t):
    return min(P, N - t * P)


def l0_jobs():
    jobs = [("XT", t, 0, "act") for t in range(NT)]
    jobs += [("NB", m, g, "dve") for g in range(3) for m in range(KD)]
    jobs += [("H", m, g, "act") for g in range(3) for m in range(H1 // P)]
    jobs += [("Y", t, 0, "dve") for t in range(NT)]
    return jobs


def qkv_jobs():
    jobs = []
    for i in range(NT + 1):
        if i < NT:
            jobs += [("FS", i, 0, "dve"), ("FB", i, 0, "dve")]
        if i >= 1:
            jobs.append(("T", i - 1, 0, "act"))
            for g, tiles in enumerate(TILES_OF):
                if i - 1 == tiles[-1]:
                    jobs += [("Q", m, g, "dve") for m in range(KD)]
                    jobs += [("K", m, g, "act") for m in range(KD)]
    return jobs + [("V", t, 0, "dve") for t in range(NT)]


def mlp_jobs():
    jobs = []
    for i in range(NT + 2):
        if i < NT:
            jobs.append(("WO", i, 0, "dve"))
        if 1 <= i <= NT:
            jobs += [("FS", i - 1, 0, "dve"), ("FB", i - 1, 0, "dve")]
        if i >= 2:
            jobs.append(("T", i - 2, 0, "act"))
            for g, tiles in enumerate(TILES_OF):
                if i - 2 == tiles[-1]:
                    jobs += [("M1", m, g, "act") for m in range(KD)]
    return jobs + [("M2", t, 0, "dve") for t in range(NT)]


class Jobs:

    def __init__(self, jobs, made=0, act=0, dve=0):
        self.jobs = jobs
        self.start = {"made": made, "act": act, "dve": dve}
        self.made, self.out, self.engine = {}, {}, {}
        n = dict(self.start)
        for kind, a, b, engine in jobs:
            n["made"] += 1
            n[engine] += 1
            self.made[kind, a, b] = n["made"]
            self.out[kind, a, b] = n[engine]
            self.engine[kind, a, b] = engine
        self.end = n

    def bank(self, j):
        return j % 8


def gnn_kernel(nc, x_in, src, dst, noise, W1, b1, W2, b2, eps0, f_w1, f_b1, f_w2, f_b2, s1_w, s1_b,
               b1_w, b1_b, wq, bq, wk, bk, wv, bv, wo, bo, s2_w, s2_b, b2_w, b2_b, m_w1, m_b1,
               m_w2, m_b2, out):
    l0 = Jobs(l0_jobs())
    qkv = Jobs(qkv_jobs())
    mlp = Jobs(mlp_jobs(), **{k: qkv.end[k] for k in ("made", "act", "dve")})
    made0, act0, dve0 = l0.end["made"], l0.end["act"], l0.end["dve"]
    made_n, act_n, dve_n = mlp.end["made"], mlp.end["act"], mlp.end["dve"]
    x_first = nc.dram_tensor("x_first", (NT * P, D), F32, kind="Internal").ap()

    with ExitStack() as ctx:
        def sb(name, shape, dt=F32):
            return ctx.enter_context(nc.sbuf_tensor(name, shape, dt))

        def sem(name):
            return ctx.enter_context(nc.semaphore(name))

        counts = sb("counts", [P, NT, NP])
        x = sb("x", [P, NT, D])
        qT = sb("qT", [P, KD, N])
        kv = sb("kv", [P, 2 * KD, NP])
        pT = sb("pT", [P, 2, NT + 1, 2 * P])
        w = sb("w", [P, 2, KD, D])
        s = sb("s", [P, 2, NP])
        y = sb("y", [P, 2, D])
        row_bias = sb("row_bias", [P, 3, D])
        col_bias = sb("col_bias", [P, 3, KD])
        film_raw = sb("film_raw", [96, 2 * D])
        film = sb("film", [96, 2 * D], F32R)
        cond = sb("cond", [96, N], F32R)
        ident = sb("ident", [P, P])
        ones = sb("ones", [P, P])
        rep = sb("rep", [P, P])
        stat6 = sb("stat6", [P, NT, 6])
        mv = sb("mv", [P, NT, 2])
        rstd = sb("rstd", [P, NT])
        ve = sb("ve", [P, NT])
        half = sb("half", [P, 1])
        small = sb("small", [P, 2, 4])
        edge = sb("edge", [ET, 2, NEP])
        eps1 = sb("eps1", [P, 1])
        table = sb("table", [1, 3, NT], I32)
        ps = ctx.enter_context(nc.psum_tensor("ps", [P, 8, BANK], F32))

        keys = kv[:, 0:KD, :]
        vals = kv[:, KD:2 * KD, :].rearrange("p a b -> p (a b)").rearrange("p (t d) -> p t d", d=D)
        pT_flat = pT[:].rearrange("p a b c -> p (a b c)")
        yT = pT_flat[:, 0:KD * N].rearrange("p (k n) -> p k n", n=N)
        w2_l0 = pT_flat[:, 0:8 * D].rearrange("p (k n) -> p k n", n=D)
        w1_l0 = w[:].rearrange("p a b c -> p (a b c)").rearrange("p (k n) -> p k n", n=H1)
        x1 = kv[:].rearrange("p a b -> p (a b)")[:, 0:NT * D].rearrange("p (t d) -> p t d", d=D)
        iota_n = pT_flat[:, 0:NP // 2].bitcast(F16)
        hot = pT_flat[:, NP // 2:NP // 2 + NP + P].bitcast(BF16).rearrange("p (s n) -> p s n", s=2)
        zero = pT_flat[0:1, 2500:2500 + 256].bitcast(BF16)
        idx_rows = pT_flat[:, 3000:3000 + 4 * ET].bitcast(I32).rearrange("p (a e) -> p a e", e=ET)
        idx_f = pT_flat[:, 3500:3500 + 4 * ET].rearrange("p (a e) -> p a e", e=ET)
        span = pT_flat[:, 4000:4004]
        tl = pT_flat[0:1, 4010:4010 + 2 * NE].rearrange("p (a t) -> p a t", t=NE)
        tl_iota = pT_flat[0:1, 4400:4400 + NE]
        tl_i32 = pT_flat[0:1, 4600:4600 + NE].bitcast(I32)
        rel = kv[0:1].rearrange("p a b -> p (a b)")[:, 0:3 * NT * NE].rearrange("p (a j t) -> p a j t", a=3, t=NE)
        bounds = pT_flat[0:1, 4800:4800 + 3 * NT].rearrange("p (a j) -> p a j", j=NT)

        idx_in, x_in_s, small_in, noise_in = sem("idx_in"), sem("x_loaded"), sem("small_in"), sem("noise_in")
        w1_in, w2_in, b2_in = sem("w1_in"), sem("w2_in"), sem("b2_in")
        consts = sem("consts")
        idx_t, tiles_s = sem("idx_transposed"), sem("edge_tables")
        dv = sem("dve_step")
        hot_ready, hot_used = sem("hot_ready"), sem("hot_used")
        block_counted, counts_out = sem("block_counted"), sem("counts_out")
        cond_mm, cond_dve, cond_act = sem("cond_mm"), sem("cond_dve"), sem("cond_act")
        made = sem("product_made")
        act_out, dve_out = sem("act_read_product"), sem("dve_read_product")
        stat_s, mv_ready, rstd_ready, ve_s = sem("stats_made"), sem("mean_var_ready"), sem("rstd_ready"), sem("ve")
        xn_done, biased = sem("normed"), sem("bias_added")
        l0_twice = sem("x_twice")
        mask_ln, mask_dve, mask_ready = sem("mask_ln"), sem("mask_dve"), sem("mask_ready")
        padded, tails_clear = sem("padding_cleared"), sem("tails_clear")
        w_in = [sem("w_in_even"), sem("w_in_odd")]
        colb_in, film_in = sem("col_bias_in"), sem("film_in")
        rowb_in = [sem("bv_in"), sem("bo_in"), sem("mb2_in")]
        film_hi, film_ready = sem("film_high"), sem("film_ready")
        scored, masked, negm_s, exp_done = sem("scored"), sem("masked"), sem("neg_max"), sem("exp_done")
        den_s, rep_ready = sem("denominator"), sem("reciprocal_spread")
        turned, pT_out, summed, head_out = sem("turned"), sem("weights_out"), sem("summed"), sem("head_out")
        x1_saved, x1_in, added, y_out, out_s = sem("x1_saved"), sem("x1_in"), sem("x1_added"), sem("y_out"), sem("out_written")
        l0_ready = sem("l0_normed")
        passed = sem("passed_waits")
        block = ctx.enter_context(nc.Block())

        W_OF_BLOCK = [(wq, "Q"), (wk, "K"), (wv, "V"), (wo, "WO"), (m_w1, "M1"), (m_w2, "M2")]
        LAST_OF = {"Q": (KD - 1, 2), "K": (KD - 1, 2), "V": (NT - 1, 0), "WO": (NT - 1, 0), "M1": (KD - 1, 2),
                   "M2": (NT - 1, 0)}

        def jobs_of(kind):
            return qkv if kind in ("Q", "K", "V") else mlp

        @block.sync
        def _(sp):
            for a, ind in enumerate((src, dst)):
                r = ind.rearrange("(t e) -> t e", e=ET)
                sp.dma_start(idx_rows[:, 2 * a, :], r[0:P]).then_inc(idx_in, 16)
                sp.dma_start(idx_rows[0:NE - P, 2 * a + 1, :], r[P:NE]).then_inc(idx_in, 16)
            sp.dma_start(s[0:32, 0, 0:N], noise.rearrange("n o -> o n").broadcast_to([32, N])).then_inc(noise_in, 16)
            sp.dma_start(x[:, 0:NT - 1, :], x_in[0:(NT - 1) * P].rearrange("(t p) d -> p t d", p=P)).then_inc(x_in_s, 16)
            sp.dma_start(x[0:rows(NT - 1), NT - 1, :], x_in[(NT - 1) * P:N]).then_inc(x_in_s, 16)
            sp.dma_start(eps1[:], eps0.rearrange("(o n) -> o n", o=1).broadcast_to([P, 1])).then_inc(small_in, 16)
            sp.dma_start(film_raw[0:64, 0:16], f_w1[:, :]).then_inc(small_in, 16)
            sp.dma_start(film_raw[0:16, 16:32], f_w2[:, :]).then_inc(small_in, 16)
            sp.dma_start(film_raw[0:16, 32:33], f_b1.rearrange("(p o) -> p o", o=1)).then_inc(small_in, 16)
            sp.dma_start(film_raw[0:16, 33:34], f_b2.rearrange("(p o) -> p o", o=1)).then_inc(small_in, 16)
            sp.dma_start(row_bias[:, 2, 0:8], b1.rearrange("(m p) -> p m", p=P), allow_slow_non_contiguous=True).then_inc(small_in, 16)
            sp.dma_start(row_bias[:, 0, :], b2.rearrange("(o n) -> o n", o=1).broadcast_to([P, D])).then_inc(b2_in, 16)
            sp.dma_start(w1_l0, W1.rearrange("(k p) n -> p k n", p=P)).then_inc(w1_in, 16)
            sp.wait_ge(dve_out, l0.out["NB", KD - 1, 2])
            sp.dma_start(w2_l0, W2.rearrange("(k p) n -> p k n", p=P)).then_inc(w2_in, 16)
            sp.wait_ge(l0_ready, NT)
            sp.dma_start(x_first[0:(NT - 1) * P].rearrange("(t p) d -> p t d", p=P), x[:, 0:NT - 1, :]).then_inc(x1_saved, 16)
            sp.dma_start(x_first[(NT - 1) * P:N], x[0:rows(NT - 1), NT - 1, :]).then_inc(x1_saved, 16)
            with sp.Fori(0, L) as i:
                sp.wait_ge(act_out, i * act_n + act0)
                sp.wait_ge(dve_out, i * dve_n + dve0)
                for n, b in enumerate((bq, bk, m_b1)):
                    sp.dma_start(col_bias[:, n, :], b[i].rearrange("(m p) -> p m", p=P), allow_slow_non_contiguous=True).then_inc(colb_in, 16)
                for n, b in enumerate((bv, bo, m_b2)):
                    sp.dma_start(row_bias[:, n, :], b[bass.ds(i, 1)].broadcast_to([P, D])).then_inc(rowb_in[n], 16)

                def load_film(n, sw, sb_, bw, bb):
                    for c, (wt, bt) in enumerate(((sw, sb_), (bw, bb))):
                        for r in range(3):
                            sp.dma_start(film_raw[32 * r:32 * r + 16, c * D:(c + 1) * D], wt[i]).then_inc(film_in, 16)
                            sp.dma_start(film_raw[32 * r + 16:32 * r + 17, c * D:(c + 1) * D], bt[bass.ds(i, 1)]).then_inc(film_in, 16)

                def load_w(n):
                    wt, kind = W_OF_BLOCK[n]
                    if n >= 2:
                        k = W_OF_BLOCK[n - 2][1]
                        sp.wait_ge(made, i * made_n + made0 + jobs_of(k).made[(k, *LAST_OF[k])])
                    else:
                        sp.wait_ge(made, i * made_n + made0)
                    sp.dma_start(w[:, n % 2, :, :], wt[i].rearrange("(k p) n -> p k n", p=P)).then_inc(w_in[n % 2], 16)

                sp.wait_ge(film_ready, 2 * i + 1)
                sp.wait_ge(padded, 1)
                load_film(0, s1_w, s1_b, b1_w, b1_b)
                load_w(0)
                load_w(1)
                sp.wait_ge(film_ready, 2 * i + 2)
                load_film(1, s2_w, s2_b, b2_w, b2_b)
                for n in range(2, 6):
                    load_w(n)
            sp.wait_ge(dve_out, L * dve_n + dve0)
            sp.wait_ge(made, L * made_n + made0)
            sp.wait_ge(x1_saved, 32)
            sp.dma_start(x1[:, 0:NT - 1, :], x_first[0:(NT - 1) * P].rearrange("(t p) d -> p t d", p=P)).then_inc(x1_in, 16)
            sp.dma_start(x1[0:rows(NT - 1), NT - 1, :], x_first[(NT - 1) * P:N]).then_inc(x1_in, 16)
            for t in range(NT):
                sp.wait_ge(y_out, t + 1)
                sp.dma_start(out[t * P:t * P + rows(t)], x[0:rows(t), t, :]).then_inc(out_s, 16)
            sp.wait_ge(out_s, 16 * NT)

        @block.gpsimd
        def _(pool):
            nc.gpsimd.memset(ident[:], 0.0).then_inc(consts, 1)
            nc.gpsimd.memset(ones[:], 1.0).then_inc(consts, 1)
            nc.gpsimd.memset(zero, 0.0).then_inc(consts, 1)
            nc.gpsimd.memset(half[:], -0.5).then_inc(consts, 1)
            nc.gpsimd.memset(edge[:], -1.0).then_inc(consts, 1)
            pool.wait_ge(consts, 5)
            nc.gpsimd.affine_select(out=ident[:], in_=ident[:], compare_op=ALU.not_equal, fill=1.0, base=0,
                                    pattern=[[-1, P]], channel_multiplier=1).then_inc(consts, 1)
            nc.gpsimd.iota(iota_n, [[1, NP]], base=0, channel_multiplier=0,
                           allow_small_or_imprecise_dtypes=True).then_inc(consts, 1)
            nc.gpsimd.iota(tl_i32, [[1, NE]], base=0, channel_multiplier=0).then_inc(consts, 1)
            nc.gpsimd.iota(rep[0:32, 0:1].bitcast(I32), [[0, 1]], base=1, channel_multiplier=1).then_inc(consts, 1)

            def rstd_of(t, n):
                R = rows(t)
                pool.wait_ge(mv_ready, n + 1)
                pool.sem_inc(passed)
                nc.gpsimd.tensor_scalar(ve[0:R, t:t + 1], mv[0:R, t, 1:2], EPS, None, ALU.add).then_inc(ve_s, 1)
                pool.wait_ge(ve_s, n + 1)
                nc.gpsimd.tensor_tensor(rstd[0:R, t:t + 1], ve[0:R, t:t + 1], half[0:R, :], ALU.pow).then_inc(rstd_ready, 1)

            pool.wait_ge(dve_out, l0.out["NB", KD - 1, 2])
            pool.wait_ge(x_in_s, 32)
            pool.wait_ge(b2_in, 16)
            for t in range(NT):
                xt = x[0:rows(t), t, :]
                nc.gpsimd.tensor_tensor(xt, xt, xt, ALU.add).then_inc(l0_twice, 1)
                pool.wait_ge(l0_twice, 2 * t + 1)
                nc.gpsimd.tensor_tensor(xt, xt, row_bias[0:rows(t), 0, :], ALU.add).then_inc(l0_twice, 1)
            for t in range(NT):
                rstd_of(t, t)
            pool.wait_ge(cond_dve, 7)
            pool.wait_ge(cond_mm, 6)
            nc.gpsimd.memset(film_raw[:], 0.0).then_inc(padded, 1)
            pool.sem_inc(film_ready)
            with pool.Fori(0, L) as i:
                def split_film(n):
                    pool.wait_ge(film_in, (2 * i + n + 1) * 12 * 16)
                    kind = (qkv, mlp)[n]
                    if n == 1:
                        pool.wait_ge(made, i * made_n + made0 + qkv.made["FB", NT - 1, 0])
                    else:
                        pool.wait_ge(made, i * made_n + made0)
                    pool.sem_inc(passed)
                    nc.gpsimd.tensor_copy(film[:], film_raw[:]).then_inc(film_hi, 1)
                    pool.wait_ge(film_hi, 2 * i + n + 1)
                    nc.gpsimd.tensor_tensor(film[64:96, :], film_raw[64:96, :], film[64:96, :].bitcast(F32),
                                            ALU.subtract).then_inc(film_ready, 1)
                    pool.wait_ge(film_ready, 2 * i + n + 2)

                for n in range(2):
                    split_film(n)
                    before = i * 2 * NT + n * NT
                    for t in range(NT + 1):
                        if t < NT:
                            rstd_of(t, before + NT + t)
                        if t >= 1:
                            R = rows(t - 1)
                            if t == 1:
                                pool.wait_ge(rowb_in[n + 1], i * 16 + 16)
                            pool.wait_ge(xn_done, before + t)
                            nc.gpsimd.tensor_tensor(x[0:R, t - 1, :], x[0:R, t - 1, :], row_bias[0:R, n + 1, :],
                                                    ALU.add).then_inc(biased, 1)
            for t in range(NT):
                rstd_of(t, (2 * L + 1) * NT + t)

        @block.scalar
        def _(act):
            cps = ps[:].rearrange("p b c -> p (b c)")[:, 0:NP].rearrange("p (i d) -> p i d", d=P)
            act.sem_inc(counts_out)
            with act.Fori(0, NT) as j:
                act.wait_ge(block_counted, j + 1)
                nc.scalar.copy(counts[:, :, bass.ds(j * P, P)], cps).then_inc(counts_out, 1)
            act.wait_ge(cond_dve, 2)
            nc.scalar.activation(s[0:32, 0, 0:N], qT[0:32, 0, :], ACT.Sin).then_inc(cond_act, 1)
            nc.scalar.activation(s[32:64, 0, 0:N], qT[0:32, 1, :], ACT.Sin).then_inc(cond_act, 1)
            act.wait_ge(cond_dve, 3)
            nc.scalar.activation(qT[0:16, 1, :], qT[0:16, 0, :], ACT.Exp, scale=-1.0).then_inc(cond_act, 1)
            for j, (kind, a, b, engine) in enumerate(l0.jobs):
                if engine != "act":
                    continue
                act.wait_ge(made, l0.made[kind, a, b])
                bank = ps[:, l0.bank(j), :]
                if kind == "XT":
                    R = rows(a)
                    nc.scalar.copy(yT[:, :, a * P:a * P + R],
                                   bank.rearrange("p (k r) -> p k r", r=P)[:, :, 0:R]).then_inc(act_out, 1)
                else:
                    c0, cn = GROUPS[b]
                    nc.scalar.activation(kv[:, a, c0:c0 + cn], bank[:, 0:cn], ACT.Relu,
                                         bias=row_bias[:, 2, a:a + 1]).then_inc(act_out, 1)
            for t in range(NT):
                act.wait_ge(mask_dve, 2 * t + 1)
                nc.scalar.activation(s[:, t % 2, :], s[:, t % 2, :], ACT.Ln).then_inc(mask_ln, 1)
            with act.Fori(0, L) as i:
                def read_products(jl):
                    for j, (kind, a, b, engine) in enumerate(jl.jobs):
                        if engine != "act":
                            continue
                        act.wait_ge(made, i * made_n + made0 + jl.made[kind, a, b])
                        bank = ps[:, jl.bank(j), :]
                        if kind == "T":
                            R = rows(a)
                            nc.scalar.copy(yT[:, :, a * P:a * P + R],
                                           bank.rearrange("p (k r) -> p k r", r=P)[:, :, 0:R]).then_inc(act_out, 1)
                            continue
                        if (a, b) == (0, 0):
                            act.wait_ge(colb_in, i * 48 + 48)
                        c0, cn = GROUPS[b]
                        n, f = {"K": (1, ACT.Identity), "M1": (2, ACT.Relu)}[kind]
                        nc.scalar.activation(keys[:, a, c0:c0 + cn], bank[:, 0:cn], f,
                                             bias=col_bias[:, n, a:a + 1]).then_inc(act_out, 1)

                read_products(qkv)
                U = len(UNITS)

                def exp(u):
                    g, h, k = UNITS[u]
                    R = rows(2 * g + k)
                    act.wait_ge(negm_s, i * U + u + 1)
                    nc.scalar.activation(s[0:R, u % 2, :], s[0:R, u % 2, :], ACT.Exp, bias=small[0:R, u % 2, 1:2],
                                         accum_out=small[0:R, u % 2, 2:3]).then_inc(exp_done, 1)

                exp(0)
                for u, (g, h, k) in enumerate(UNITS):
                    if u + 1 < U:
                        exp(u + 1)
                    R = rows(2 * g + k)
                    gh = u // 2
                    act.wait_ge(turned, i * U + u + 1)
                    if gh >= 2 and k == 0:
                        act.wait_ge(head_out, i * NG * H + gh - 1)
                    src_ps = ps[:].rearrange("p b c -> p (b c)")[:, 3 * BANK:3 * BANK + (NT + 1) * P]
                    nc.scalar.copy(pT[:, gh % 2, :, k * P:k * P + R],
                                   src_ps.rearrange("p (t r) -> p t r", r=P)[:, :, 0:R]).then_inc(pT_out, 1)
                read_products(mlp)

        @block.vector
        def _(dve):
            step = [0]

            def chain(ins):
                step[0] += 1
                ins.then_inc(dv, 1)
                dve.wait_ge(dv, step[0])

            dve.wait_ge(idx_in, 64)
            for a in range(2):
                nc.vector.tensor_copy(idx_f[:, 2 * a, :], idx_rows[:, 2 * a, :]).then_inc(tiles_s, 1)
                nc.vector.tensor_copy(idx_f[0:NE - P, 2 * a + 1, :], idx_rows[0:NE - P, 2 * a + 1, :]).then_inc(tiles_s, 1)
            dve.wait_ge(tiles_s, 4)
            for a, R in ((0, P), (1, NE - P)):
                nc.vector.tensor_reduce(span[0:R, 2 * a:2 * a + 1], idx_f[0:R, 2 + a, :], AX.X, ALU.min).then_inc(tiles_s, 1)
                nc.vector.tensor_reduce(span[0:R, 2 * a + 1:2 * a + 2], idx_f[0:R, 2 + a, :], AX.X, ALU.max).then_inc(tiles_s, 1)
            dve.wait_ge(idx_t, 1)
            dve.wait_ge(consts, 9)
            nc.vector.tensor_copy(edge[:, 0, 0:NE], ps[0:ET, 0, 0:NE]).then_inc(tiles_s, 1)
            nc.vector.tensor_copy(edge[:, 1, 0:NE], ps[0:ET, 1, 0:NE]).then_inc(tiles_s, 1)
            for a in range(2):
                nc.vector.tensor_copy(tl[:, a, :], ps[0:1, 2 + a, 0:NE]).then_inc(tiles_s, 1)
            chain(nc.vector.tensor_copy(tl_iota, tl_i32))
            dve.wait_ge(tiles_s, 12)
            for j in range(NT):
                chain(nc.vector.tensor_scalar(rel[:, 0, j, :], tl[:, 1, :], float(j * P), None, ALU.is_ge))
                chain(nc.vector.tensor_scalar(rel[:, 1, j, :], tl[:, 0, :], float((j + 1) * P), None, ALU.is_lt))
            chain(nc.vector.tensor_tensor(rel[:, 0], rel[:, 0], rel[:, 1], ALU.mult))
            for j in range(NT):
                chain(nc.vector.scalar_tensor_tensor(rel[:, 1, j, :], tl_iota, 1.0, rel[:, 0, j, :], ALU.add, ALU.mult))
                chain(nc.vector.tensor_scalar(rel[:, 2, j, :], rel[:, 0, j, :], -1024.0, 1024.0, ALU.mult, ALU.add))
                chain(nc.vector.tensor_tensor(rel[:, 2, j, :], rel[:, 2, j, :], tl_iota, ALU.add))
            chain(nc.vector.tensor_reduce(bounds[:, 1, :], rel[:, 1], AX.X, ALU.max))
            chain(nc.vector.tensor_reduce(bounds[:, 0, :], rel[:, 2], AX.X, ALU.min))
            chain(nc.vector.tensor_scalar(bounds[:, 1, :], bounds[:, 1, :], 1.0, None, ALU.max))
            chain(nc.vector.scalar_tensor_tensor(bounds[:, 0, :], bounds[:, 1, :], -1.0, bounds[:, 0, :], ALU.add, ALU.min))
            chain(nc.vector.tensor_tensor(bounds[:, 1, :], bounds[:, 1, :], bounds[:, 0, :], ALU.subtract))
            chain(nc.vector.tensor_scalar(bounds[:, 1, :], bounds[:, 1, :], 0.5, 0.25, ALU.mult, ALU.add))
            chain(nc.vector.tensor_scalar(bounds[:, 1, :], bounds[:, 1, :], ROUND, ROUND, ALU.add, ALU.subtract))
            chain(nc.vector.memset(bounds[:, 2, 0:1], 0.0))
            for j in range(1, NT):
                chain(nc.vector.tensor_tensor(bounds[:, 2, j:j + 1], bounds[:, 2, j - 1:j], bounds[:, 1, j - 1:j], ALU.add))
            nc.vector.tensor_copy(table[:], bounds).then_inc(tiles_s, 1)
            dve.wait_ge(tiles_s, 13)
            dve.sem_inc(hot_used)
            with dve.Fori(0, NT) as j:
                first = dve.value_load(table[0:1, 0, bass.ds(j, 1)], min_val=0, max_val=NE - 1)
                pairs = dve.value_load(table[0:1, 1, bass.ds(j, 1)], min_val=1, max_val=NE // 2)
                before = dve.value_load(table[0:1, 2, bass.ds(j, 1)], min_val=0, max_val=NT * NE // 2)
                with dve.Fori(0, pairs) as k:
                    for m in range(2):
                        t = first + k * 2 + m
                        dve.wait_ge(hot_used, (before + k) * 2 + m + 1)
                        nc.vector.tensor_scalar(hot[0:ET, m, 0:NP], iota_n[0:ET], edge[:, 0, bass.ds(t, 1)], None,
                                                ALU.is_equal)
                        nc.vector.tensor_scalar(hot[0:ET, m, NP:NP + P], iota_n[0:ET, bass.ds(j * P, P)],
                                                edge[:, 1, bass.ds(t, 1)], None, ALU.is_equal).then_inc(hot_ready, 1)
            freq = rep[0:32, 1:2]
            chain(nc.vector.tensor_copy(freq, rep[0:32, 0:1].bitcast(I32)))
            chain(nc.vector.tensor_scalar(freq, freq, float(np.float32(2.0 * np.pi / 16)), None, ALU.mult))
            dve.wait_ge(noise_in, 16)
            ph, kk = s[0:32, 0, 0:N], s[0:32, 1, 0:N]
            chain(nc.vector.tensor_scalar(ph, ph, freq, None, ALU.mult))
            chain(nc.vector.tensor_scalar(kk, ph, float(1.0 / (2.0 * np.pi)), ROUND, ALU.mult, ALU.add))
            chain(nc.vector.tensor_scalar(kk, kk, ROUND, None, ALU.subtract))
            for part in TWO_PI:
                chain(nc.vector.scalar_tensor_tensor(ph, kk, -part, ph, ALU.mult, ALU.add))
            nc.vector.tensor_scalar(qT[0:32, 0, :], ph, 3.1415925, -3.1415925, ALU.min, ALU.max).then_inc(cond_dve, 1)
            dve.wait_ge(cond_dve, 1)
            chain(nc.vector.scalar_tensor_tensor(kk, qT[0:32, 0, :], -1.0, qT[0:32, 0, :], ALU.mult, ALU.max))
            nc.vector.tensor_scalar(qT[0:32, 1, :], kk, -1.0, float(np.pi / 2), ALU.mult, ALU.add).then_inc(cond_dve, 1)
            dve.wait_ge(cond_mm, 3)
            dve.wait_ge(small_in, 16 * 6)
            dve.wait_ge(cond_act, 2)
            c_ps = ps[0:16].rearrange("p b c -> p (b c)")[:, 0:N]
            nc.vector.tensor_scalar(qT[0:16, 0, :], c_ps, film_raw[0:16, 32:33], None, ALU.add).then_inc(cond_dve, 1)
            dve.wait_ge(cond_act, 3)
            chain(nc.vector.tensor_scalar(qT[0:16, 1, :], qT[0:16, 1, :], 1.0, None, ALU.add))
            chain(nc.vector.reciprocal(qT[0:16, 1, :], qT[0:16, 1, :]))
            nc.vector.tensor_tensor(qT[0:16, 2, :], qT[0:16, 0, :], qT[0:16, 1, :], ALU.mult).then_inc(cond_dve, 1)
            chain(nc.vector.memset(qT[0:32, 3, :], 1.0))
            dve.wait_ge(cond_mm, 6)
            c2_ps = ps[0:16].rearrange("p b c -> p (b c)")[:, 4 * BANK:4 * BANK + N]
            chain(nc.vector.tensor_scalar(qT[0:16, 3, :], c2_ps, film_raw[0:16, 33:34], None, ALU.add))
            nc.vector.tensor_copy(cond[0:32, :], qT[0:32, 3, :]).then_inc(cond_dve, 1)
            dve.wait_ge(cond_dve, 5)
            nc.vector.tensor_copy(cond[64:96, :], qT[0:32, 3, :]).then_inc(cond_dve, 1)
            nc.vector.tensor_tensor(cond[32:64, :], qT[0:32, 3, :], cond[0:32, :].bitcast(F32),
                                    ALU.subtract).then_inc(cond_dve, 1)
            dve.wait_ge(cond_dve, 7)
            dve.wait_ge(small_in, 16 * 6)
            chain(nc.vector.tensor_scalar(eps1[:], eps1[:], 1.0, None, ALU.add))

            def stats(t, n):
                R = rows(t)
                nc.vector.bn_stats(stat6[0:R, t, :], x[0:R, t, :]).then_inc(stat_s, 1)
                dve.wait_ge(stat_s, n + 1)
                dve.sem_inc(passed)
                nc.vector.bn_aggr(mv[0:R, t, :], stat6[0:R, t, :]).then_inc(mv_ready, 1)

            for j, (kind, a, b, engine) in enumerate(l0.jobs):
                if engine != "dve":
                    continue
                dve.wait_ge(made, l0.made[kind, a, b])
                bank = ps[:, l0.bank(j), :]
                if kind == "NB":
                    if (a, b) == (0, 0):
                        dve.wait_ge(act_out, l0.out["XT", NT - 1, 0])
                    c0, cn = GROUPS[b]
                    nc.vector.scalar_tensor_tensor(qT[:, a, c0:c0 + cn], yT[:, a, c0:c0 + cn], eps1[:, 0:1],
                                                   bank[:, 0:cn], ALU.mult, ALU.add).then_inc(dve_out, 1)
                else:
                    R = rows(a)
                    dve.wait_ge(l0_twice, 2 * a + 2)
                    nc.vector.tensor_tensor(x[0:R, a, :], bank[0:R, :], x[0:R, a, :], ALU.add).then_inc(dve_out, 1)
                    dve.wait_ge(dve_out, l0.out[kind, a, b])
                    stats(a, a)
            for t in range(NT):
                R = rows(t)
                dve.wait_ge(rstd_ready, t + 1)
                nc.vector.tensor_scalar(x[0:R, t, :], x[0:R, t, :], mv[0:R, t, 0:1], rstd[0:R, t:t + 1],
                                        ALU.subtract, ALU.mult).then_inc(l0_ready, 1)
            for t in range(NT):
                if t >= 2:
                    dve.wait_ge(mask_ready, t - 1)
                nc.vector.tensor_scalar(s[:, t % 2, :], counts[:, t, :], 1.0, None, ALU.max).then_inc(mask_dve, 1)
                nc.vector.tensor_scalar(counts[:, t, :], counts[:, t, :], 0.5, NOTHING, ALU.is_lt,
                                        ALU.mult).then_inc(mask_dve, 1)
                dve.wait_ge(mask_dve, 2 * t + 2)
                dve.wait_ge(mask_ln, t + 1)
                nc.vector.tensor_tensor(counts[:, t, :], counts[:, t, :], s[:, t % 2, :], ALU.add).then_inc(mask_ready, 1)
            dve.wait_ge(made, l0.end["made"])
            nc.vector.memset(kv[:, 0:KD, N:NP], 0.0).then_inc(tails_clear, 1)
            nc.vector.memset(vals[:, NT - 1, :], 0.0).then_inc(tails_clear, 1)
            dve.wait_ge(l0_ready, NT)
            dve.wait_ge(x1_saved, 32)
            with dve.Fori(0, L) as i:
                U = len(UNITS)

                def read_products(jl, norm):
                    before = i * 2 * NT + norm * NT
                    for j, (kind, a, b, engine) in enumerate(jl.jobs):
                        if engine != "dve":
                            continue
                        if kind == "FS":
                            R = rows(a)
                            if norm == 0 and a == 0:
                                stats(0, before + NT)
                                stats(1, before + NT + 1)
                            dve.wait_ge(rstd_ready, before + NT + a + 1)
                            if a >= 2:
                                dve.wait_ge(made, i * made_n + made0 + jl.made["T", a - 2, 0])
                            nc.vector.tensor_scalar(y[0:R, a % 2, :], x[0:R, a, :], mv[0:R, a, 0:1],
                                                    rstd[0:R, a:a + 1], ALU.subtract, ALU.mult).then_inc(xn_done, 1)
                            dve.wait_ge(xn_done, before + a + 1)
                        dve.wait_ge(made, i * made_n + made0 + jl.made[kind, a, b])
                        bank = ps[:, jl.bank(j), :]
                        mine = i * dve_n + dve0 + jl.out[kind, a, b]
                        if kind == "FS":
                            nc.vector.scalar_tensor_tensor(y[0:R, a % 2, :], bank[0:R, :], 1.0, y[0:R, a % 2, :],
                                                           ALU.add, ALU.mult).then_inc(dve_out, 1)
                            dve.wait_ge(dve_out, mine)
                        elif kind == "FB":
                            R = rows(a)
                            nc.vector.tensor_tensor(y[0:R, a % 2, :], bank[0:R, :], y[0:R, a % 2, :],
                                                    ALU.add).then_inc(dve_out, 1)
                            if norm == 0 and a + 2 < NT:
                                stats(a + 2, before + NT + a + 2)
                        elif kind == "Q":
                            c0, cn = GROUPS[b]
                            if (a, b) == (0, 0):
                                dve.wait_ge(colb_in, i * 48 + 48)
                            nc.vector.tensor_scalar(qT[:, a, c0:c0 + cn], bank[:, 0:cn], col_bias[:, 0, a:a + 1],
                                                    float(P ** -0.5), ALU.add, ALU.mult).then_inc(dve_out, 1)
                        elif kind == "V":
                            R = rows(a)
                            if a == 0:
                                dve.wait_ge(rowb_in[0], i * 16 + 16)
                            nc.vector.tensor_tensor(vals[0:R, a, :], bank[0:R, :], row_bias[0:R, 0, :],
                                                    ALU.add).then_inc(dve_out, 1)
                        else:
                            R = rows(a)
                            dve.wait_ge(biased, before + a + 1 - (NT if kind == "WO" else 0))
                            nc.vector.tensor_tensor(x[0:R, a, :], bank[0:R, :], x[0:R, a, :], ALU.add).then_inc(dve_out, 1)
                            dve.wait_ge(dve_out, mine)
                            if kind == "WO":
                                stats(a, before + NT + a)

                def mask(u):
                    g, h, k = UNITS[u]
                    t = 2 * g + k
                    R = rows(t)
                    dve.wait_ge(scored, i * U + u + 1)
                    if u >= 2:
                        dve.wait_ge(turned, i * U + u - 1)
                    dve.sem_inc(passed)
                    nc.vector.tensor_tensor_reduce(s[0:R, u % 2, :], ps[:].rearrange("p b c -> p (b c)")[0:R, 0:NP],
                                                   counts[0:R, t, :], 1.0, LOWEST, ALU.add, ALU.max,
                                                   small[0:R, u % 2, 0:1]).then_inc(masked, 1)
                    dve.wait_ge(masked, i * U + u + 1)
                    nc.vector.tensor_scalar(small[0:R, u % 2, 1:2], small[0:R, u % 2, 0:1], -1.0, None,
                                            ALU.mult).then_inc(negm_s, 1)

                read_products(qkv, 0)
                mask(0)
                for u, (g, h, k) in enumerate(UNITS):
                    if u + 1 < U:
                        mask(u + 1)
                    R = rows(2 * g + k)
                    dve.wait_ge(exp_done, i * U + u + 1)
                    nc.vector.tensor_scalar(small[0:R, u % 2, 2:3], small[0:R, u % 2, 2:3], 0.5, None,
                                            ALU.max).then_inc(den_s, 1)
                    dve.wait_ge(den_s, (i * U + u) * 2 + 1)
                    nc.vector.reciprocal(small[0:R, u % 2, 3:4], small[0:R, u % 2, 2:3]).then_inc(den_s, 1)
                    dve.wait_ge(den_s, (i * U + u) * 2 + 2)
                    if u >= 1:
                        dve.wait_ge(turned, i * U + u)
                    nc.vector.tensor_scalar(rep[0:R, :], ones[0:R, :], small[0:R, u % 2, 3:4], None,
                                            ALU.mult).then_inc(rep_ready, 1)
                    for gh in [u // 2 - 1] * (k == 1 and u >= 2) + [u // 2] * (u == U - 1):
                        gg, hh = gh // H, gh % H
                        wd = rows(2 * gg) + rows(2 * gg + 1)
                        dve.wait_ge(summed, i * NG * H + gh + 1)
                        dve.wait_ge(pT_out, i * U + 2 * gh + 2)
                        nc.vector.tensor_tensor(qT[:, hh, gg * 2 * P:gg * 2 * P + wd], ps[:, 6 + gh % 2, 0:wd],
                                                pT[:, gh % 2, NT, 0:wd], ALU.mult).then_inc(head_out, 1)
                read_products(mlp, 1)
            dve.wait_ge(x1_in, 32)
            for t in range(NT):
                R = rows(t)
                nc.vector.tensor_tensor(x[0:R, t, :], x[0:R, t, :], x1[0:R, t, :], ALU.add).then_inc(added, 1)
                dve.wait_ge(added, t + 1)
                stats(t, (2 * L + 1) * NT + t)
            for t in range(NT):
                R = rows(t)
                dve.wait_ge(rstd_ready, (2 * L + 1) * NT + t + 1)
                nc.vector.tensor_scalar(x[0:R, t, :], x[0:R, t, :], mv[0:R, t, 0:1], rstd[0:R, t:t + 1],
                                        ALU.subtract, ALU.mult).then_inc(y_out, 1)

        @block.tensor
        def _(pe):
            mm = nc.tensor.matmul
            pe.wait_ge(consts, 6)
            pe.wait_ge(tiles_s, 8)
            for a in range(2):
                nc.tensor.transpose(ps[0:ET, a, 0:P], idx_f[:, 2 * a, :], ident[:])
                nc.tensor.transpose(ps[0:ET, a, P:NE], idx_f[0:NE - P, 2 * a + 1, :], ident[0:NE - P, 0:NE - P])
            for a in range(2):
                nc.tensor.transpose(ps[0:1, 2 + a, 0:P], span[:, a:a + 1], ident[:])
                last = nc.tensor.transpose(ps[0:1, 2 + a, P:NE], span[0:NE - P, 2 + a:3 + a], ident[0:NE - P, 0:NE - P])
            last.then_inc(idx_t, 1)
            pe.wait_ge(tiles_s, 13)
            cps = ps[:].rearrange("p b c -> p (b c)")
            with pe.Fori(0, NT) as j:
                pairs = pe.value_load(table[0:1, 1, bass.ds(j, 1)], min_val=1, max_val=NE // 2)
                before = pe.value_load(table[0:1, 2, bass.ds(j, 1)], min_val=0, max_val=NT * NE // 2)
                pe.wait_ge(counts_out, j + 1)
                for b in range(3):
                    mm(cps[:, b * BANK:(b + 1) * BANK], zero[:, 0:P], zero[:, 0:BANK], start=True, stop=False,
                       skip_group_check=True)
                with pe.Fori(0, pairs) as k:
                    for m in range(2):
                        pe.wait_ge(hot_ready, (before + k) * 2 + m + 1)
                        for i in range(NT):
                            last = mm(cps[:, i * P:(i + 1) * P], hot[0:ET, m, i * P:(i + 1) * P],
                                      hot[0:ET, m, NP:NP + P], start=False, stop=False, skip_group_check=True)
                        last.then_inc(hot_used, 1)
                for b in range(3):
                    last = mm(cps[:, b * BANK:(b + 1) * BANK], zero[:, 0:P], zero[:, 0:BANK], start=False, stop=True,
                              skip_group_check=True)
                last.then_inc(block_counted, 1)
            pe.wait_ge(counts_out, NT + 1)
            pe.wait_ge(cond_act, 2)
            pe.wait_ge(small_in, 16 * 6)
            for g, (c0, cn) in enumerate(GROUPS):
                mm(ps[0:16, g, 0:cn], film_raw[0:64, 0:16], s[0:64, 0, c0:c0 + cn], start=True, stop=True).then_inc(cond_mm, 1)
            pe.wait_ge(cond_dve, 4)
            for g, (c0, cn) in enumerate(GROUPS):
                mm(ps[0:16, 4 + g, 0:cn], film_raw[0:16, 16:32], qT[0:16, 2, c0:c0 + cn], start=True, stop=True).then_inc(cond_mm, 1)
            pe.wait_ge(cond_dve, 7)
            pe.wait_ge(x_in_s, 32)

            def bank_free(jl, j, base_act, base_dve):
                if j >= 8:
                    key = jl.jobs[j - 8][:3]
                    if jl.engine[key] == "act":
                        pe.wait_ge(act_out, base_act + jl.out[key])
                    else:
                        pe.wait_ge(dve_out, base_dve + jl.out[key])

            for j, (kind, a, b, engine) in enumerate(l0.jobs):
                bank_free(l0, j, 0, 0)
                bank = ps[:, l0.bank(j), :]
                if kind == "XT":
                    R = rows(a)
                    for k in range(KD):
                        last = nc.tensor.transpose(bank[:, k * P:k * P + R], x[0:R, a, k * P:(k + 1) * P], ident[0:R, 0:R])
                elif kind == "NB":
                    c0, cn = GROUPS[b]
                    for k in range(NT):
                        R = rows(k)
                        last = mm(bank[:, 0:cn], x[0:R, k, a * P:(a + 1) * P], counts[0:R, k, c0:c0 + cn],
                                  start=(k == 0), stop=(k == NT - 1))
                elif kind == "H":
                    c0, cn = GROUPS[b]
                    if a == 0:
                        pe.wait_ge(w1_in, 16)
                        pe.wait_ge(dve_out, l0.out["NB", KD - 1, b])
                    for k in range(KD):
                        last = mm(bank[:, 0:cn], w1_l0[:, k, a * P:(a + 1) * P], qT[:, k, c0:c0 + cn],
                                  start=(k == 0), stop=(k == KD - 1))
                else:
                    R = rows(a)
                    if a == 0:
                        pe.wait_ge(w2_in, 16)
                    pe.wait_ge(act_out, l0.out["H", H1 // P - 1, min(a // 4, 2)])
                    for k in range(H1 // P):
                        last = mm(bank[0:R, :], kv[:, k, a * P:a * P + R], w2_l0[:, k, :], start=(k == 0),
                                  stop=(k == H1 // P - 1))
                last.then_inc(made, 1)
            pe.wait_ge(tails_clear, 2)
            with pe.Fori(0, L) as i:
                U = len(UNITS)

                def products(jl, norm):
                    for j, (kind, a, b, engine) in enumerate(jl.jobs):
                        bank_free(jl, j, i * act_n + act0, i * dve_n + dve0)
                        bank = ps[:, jl.bank(j), :]
                        if kind in ("FS", "FB"):
                            R = rows(a)
                            if a == 0 and kind == "FS":
                                pe.wait_ge(film_ready, 2 * i + norm + 2)
                            c0 = 0 if kind == "FS" else D
                            last = mm(bank[0:R, :], cond[:, a * P:a * P + R], film[:, c0:c0 + D], start=True, stop=True)
                        elif kind == "T":
                            R = rows(a)
                            pe.wait_ge(dve_out, i * dve_n + dve0 + jl.out["FB", a, 0])
                            for k in range(KD):
                                last = nc.tensor.transpose(bank[:, k * P:k * P + R], y[0:R, a % 2, k * P:(k + 1) * P],
                                                           ident[0:R, 0:R])
                        elif kind in ("Q", "K", "M1"):
                            c0, cn = GROUPS[b]
                            wn = {"Q": 0, "K": 1, "M1": 4}[kind]
                            if (a, b) == (0, 0):
                                pe.wait_ge(w_in[wn % 2], i * 48 + (wn // 2 + 1) * 16)
                            if a == 0:
                                pe.wait_ge(act_out, i * act_n + act0 + jl.out["T", TILES_OF[b][-1], 0])
                            for k in range(KD):
                                last = mm(bank[:, 0:cn], w[:, wn % 2, k, a * P:(a + 1) * P], yT[:, k, c0:c0 + cn],
                                          start=(k == 0), stop=(k == KD - 1))
                        else:
                            R = rows(a)
                            wn = {"V": 2, "WO": 3, "M2": 5}[kind]
                            left = {"V": yT, "WO": qT, "M2": keys}[kind]
                            if a == 0:
                                pe.wait_ge(w_in[wn % 2], i * 48 + (wn // 2 + 1) * 16)
                            if kind == "WO":
                                pe.wait_ge(head_out, i * NG * H + (a // 2 + 1) * H)
                            if kind == "M2":
                                pe.wait_ge(act_out, i * act_n + act0 + jl.out["M1", KD - 1, min(a // 4, 2)])
                            for k in range(KD):
                                last = mm(bank[0:R, :], left[:, k, a * P:a * P + R], w[:, wn % 2, k, :],
                                          start=(k == 0), stop=(k == KD - 1))
                        last.then_inc(made, 1)

                def scores(u):
                    g, h, k = UNITS[u]
                    t = 2 * g + k
                    R = rows(t)
                    if u >= 1:
                        pe.wait_ge(masked, i * U + u)
                    for b, (c0, cn) in enumerate(((0, 512), (512, 512), (1024, 256))):
                        last = mm(ps[0:R, b, 0:cn], qT[:, h, t * P:t * P + R], keys[:, h, c0:c0 + cn], start=True, stop=True)
                    last.then_inc(scored, 1)

                def weigh(gh, part):
                    g, h = gh // H, gh % H
                    wd = rows(2 * g) + rows(2 * g + 1)
                    if part == 0:
                        pe.wait_ge(pT_out, i * U + 2 * gh + 2)
                        if gh >= 2:
                            pe.wait_ge(head_out, i * NG * H + gh - 1)
                    for t in range(5 * part, 5 * part + 5):
                        last = mm(ps[:, 6 + gh % 2, 0:wd], vals[:, t, h * P:(h + 1) * P], pT[:, gh % 2, t, 0:wd],
                                  start=(t == 0), stop=(t == NT - 1))
                    if part == 1:
                        last.then_inc(summed, 1)

                pe.wait_ge(act_out, i * act_n + act0)
                pe.wait_ge(dve_out, i * dve_n + dve0)
                products(qkv, 0)
                pe.wait_ge(act_out, i * act_n + act0 + qkv.end["act"])
                pe.wait_ge(dve_out, i * dve_n + dve0 + qkv.end["dve"])
                scores(0)
                for u, (g, h, k) in enumerate(UNITS):
                    R = rows(2 * g + k)
                    if u + 1 < U:
                        scores(u + 1)
                    if u >= 2:
                        weigh(u // 2 - 1, k)
                    pe.wait_ge(exp_done, i * U + u + 1)
                    pe.wait_ge(rep_ready, i * U + u + 1)
                    if u >= 1:
                        pe.wait_ge(pT_out, i * U + u)
                    turn = ps[:].rearrange("p b c -> p (b c)")[:, 3 * BANK:]
                    for t in range(NT):
                        nc.tensor.transpose(turn[:, t * P:t * P + R], s[0:R, u % 2, t * P:(t + 1) * P], ident[0:R, 0:R])
                    nc.tensor.transpose(turn[:, NT * P:NT * P + R], rep[0:R, :], ident[0:R, 0:R]).then_inc(turned, 1)
                for part in range(2):
                    weigh(U // 2 - 1, part)
                pe.wait_ge(pT_out, i * U + U)
                pe.wait_ge(head_out, (i + 1) * NG * H)
                products(mlp, 1)


_INS = ['x', 'src', 'dst', 'node_vec1', 'L0_gnn_W1', 'L0_gnn_b1', 'L0_gnn_W2', 'L0_gnn_b2', 'L0_gnn_eps',
        'L1_gnn_f_w1', 'L1_gnn_f_b1', 'L1_gnn_f_w2', 'L1_gnn_f_b2', 'L1_gnn_s1_w', 'L1_gnn_s1_b', 'L1_gnn_b1_w',
        'L1_gnn_b1_b', 'L1_gnn_wq', 'L1_gnn_bq', 'L1_gnn_wk', 'L1_gnn_bk', 'L1_gnn_wv', 'L1_gnn_bv', 'L1_gnn_wo',
        'L1_gnn_bo', 'L1_gnn_s2_w', 'L1_gnn_s2_b', 'L1_gnn_b2_w', 'L1_gnn_b2_b', 'L1_gnn_m_w1', 'L1_gnn_m_b1',
        'L1_gnn_m_w2', 'L1_gnn_m_b2']


def kernel(**inputs):
    import numpy as _np
    import concourse.bacc as _bacc
    from concourse import mybir as _mybir
    from concourse.bass_utils import run_bass_kernel_spmd as _run

    nc = _bacc.Bacc("TRN2", target_bir_lowering=False, num_devices=1)
    arrays, args = {}, []
    for name in _INS:
        a = _np.ascontiguousarray(inputs[name])
        arrays[f"in_{name}_dram"] = a
        args.append(nc.dram_tensor(f"in_{name}_dram", a.shape, _mybir.dt.from_np(a.dtype), kind="ExternalInput").ap())
    args.append(nc.dram_tensor("out_dram", (N, D), F32, kind="ExternalOutput").ap())
    gnn_kernel(nc, *args)
    r = _run(nc, [arrays], core_ids=[0])
    return r.results[0]["out_dram"]
```

```python
from contextlib import ExitStack

import numpy as np

import concourse.bass as bass
from concourse import mybir

ALU = mybir.AluOpType
ACT = mybir.ActivationFunctionType
AX = mybir.AxisListType
F32 = mybir.dt.float32
F32R = mybir.dt.float32r
BF16 = mybir.dt.bfloat16
F16 = mybir.dt.float16
I32 = mybir.dt.int32

P = 128
N = 1250
D = 512
E = 21250
H1 = 1024
L = 4
H = 4
KD = D // P
NT = -(-N // P)
NP = NT * P
ET = 125
NE = E // ET
BATCH = 2
NEP = 2 * NE + 4
NOTHING = -1e30
LOWEST = -1e29
EPS = 1e-5
BANK = 512
ROUND = 12582912.0
TWO_PI = (6.28125, 0.0019353071693331003, 1.0253131677018246e-11)
GROUPS = [(0, 512), (512, 512), (1024, N - 1024)]
TILES_OF = [range(0, 4), range(4, 8), range(8, NT)]
NG = NT // 2
UNITS = [(g, h, s) for g in range(NG) for h in range(H) for s in range(2)]


def rows(t):
    return min(P, N - t * P)


ON_SCALAR = ("XT", "H", "M1", "T", "K")
ON_VECTOR = ("NB", "Y", "WO", "FS", "FB", "T", "M2", "Q", "K", "V")


def l0_jobs():
    jobs = [("XT", t, 0) for t in range(NT)]
    jobs += [("NB", m, g) for g in range(3) for m in range(KD)]
    jobs += [("H", m, g) for g in range(3) for m in range(H1 // P)]
    jobs += [("Y", t, 0) for t in range(NT)]
    return jobs


def wo_m1_jobs():
    jobs = []
    for i in range(NT + 2):
        ahead = 2
        if i == 0:
            jobs += [("OS", t, 0) for t in range(ahead)]
        if i + ahead < NT:
            jobs.append(("OS", i + ahead, 0))
        if i < NT:
            jobs.append(("WO", i, 0))
        if 1 <= i <= NT:
            jobs += [("FS", i - 1, 0), ("FB", i - 1, 0)]
        if i == 3:
            jobs.append(("W", "M1", 0))
        if i >= 2:
            jobs.append(("T", i - 2, 0))
            for g, tiles in enumerate(TILES_OF):
                if i - 2 == tiles[-1]:
                    jobs += [("M1", m, g) for m in range(KD)]
    at = max(n for n, job in enumerate(jobs) if job[:3] == ("M1", KD - 1, 1)) + 1
    return jobs[:at] + [("W", "M2", 0)] + jobs[at:]


def m2_qkv_jobs(m2=True, qkv=True):
    jobs = []
    for i in range(NT + 2):
        if m2 and i < NT:
            jobs.append(("M2", i, 0))
        if not qkv:
            continue
        if 1 <= i <= NT:
            jobs += [("FS", i - 1, 0), ("FB", i - 1, 0)]
        if i == 3:
            jobs.append(("W", "Q", 0))
        if i >= 2:
            jobs.append(("T", i - 2, 0))
            for g, tiles in enumerate(TILES_OF):
                if i - 2 == tiles[-1]:
                    jobs += [("Q", m, g) for m in range(KD)]
    if qkv:
        jobs.append(("W", "K", 0))
        jobs += [("K", m, g) for g in range(3) for m in range(KD)]
        at = max(n for n, job in enumerate(jobs) if job[:3] == ("K", KD - 1, 1)) + 1
        jobs = jobs[:at] + [("W", "V", 0)] + jobs[at:]
        jobs += [("V", t, 0) for t in range(NT)]
    return jobs


class Counts:

    def __init__(self, jobs, before=None):
        self.jobs, self.products = jobs, []
        self.made, self.act_out, self.dve_out, self.bank = {}, {}, {}, {}
        made, act, dve = before.end if before else (0, 0, 0)
        for kind, a, b in jobs:
            if kind in ON_SCALAR:
                act += 1
                self.act_out[kind, a, b] = act
            if kind in ON_VECTOR:
                dve += 1
                self.dve_out[kind, a, b] = dve
            if kind in ON_SCALAR or kind in ON_VECTOR:
                made += 1
                self.made[kind, a, b] = made
                self.bank[kind, a, b] = len(self.products) % 8
                self.products.append((kind, a, b))
        self.end = (made, act, dve)


class Now:

    def __init__(self, made, act, dve, block):
        self.made, self.act, self.dve, self.block = made, act, dve, block


def gnn_kernel(nc, x_in, src, dst, noise, W1, b1, W2, b2, eps0, f_w1, f_b1, f_w2, f_b2, s1_w, s1_b,
               b1_w, b1_b, wq, bq, wk, bk, wv, bv, wo, bo, s2_w, s2_b, b2_w, b2_b, m_w1, m_b1,
               m_w2, m_b2, out):
    l0 = Counts(l0_jobs())
    qkv0 = Counts(m2_qkv_jobs(m2=False), l0)
    wo_m1 = Counts(wo_m1_jobs())
    m2_qkv = Counts(m2_qkv_jobs(), wo_m1)
    m2_last = Counts(m2_qkv_jobs(qkv=False), wo_m1)
    start, per = qkv0.end, m2_qkv.end
    U = len(UNITS)
    GH = NG * H

    def now(i, eng=None):
        values = [i * per[n] + start[n] for n in range(3)]
        if eng is not None:
            values = [eng.snap(value) for value in values]
        return Now(*values, i)

    zero_now = Now(0, 0, 0, -1)
    last = now(L - 1)

    W_IN_BLOCK = {"WO": 3, "M1": 4, "M2": 5, "Q": 6, "K": 7, "V": 8}

    def w_index(kind, block):
        return 6 * block + W_IN_BLOCK[kind]

    def w_place(kind):
        return (W_IN_BLOCK[kind] + 1) % 2

    def w_loads(kind, block):
        c = W_IN_BLOCK[kind]
        return 3 * block + ((c + 1) // 2 if c % 2 else c // 2 + 1)

    x_first = nc.dram_tensor("x_first", (NT * P, D), F32, kind="Internal").ap()
    mask_dram = nc.dram_tensor("mask_dram", (NT, P, NP), F32, kind="Internal").ap()

    with ExitStack() as ctx:
        def sb(name, shape, dt=F32):
            return ctx.enter_context(nc.sbuf_tensor(name, shape, dt))

        def sem(name):
            return ctx.enter_context(nc.semaphore(name))

        ident = sb("ident", [P, P])
        ones = sb("ones", [P, P])
        rep = sb("rep", [P, P])
        stat6 = sb("stat6", [P, NT, 6])
        mv = sb("mv", [P, NT, 2])
        rstd = sb("rstd", [P, NT])
        ve = sb("ve", [P, NT])
        shift = sb("shift", [P, NT])
        half = sb("half", [P, 1])
        small = sb("small", [P, 2, 4])
        edge = sb("edge", [ET, 2, NEP])
        eps1 = sb("eps1", [P, 1])
        table = sb("table", [1, 3, NT], I32)
        col_bias = sb("col_bias", [P, 3, KD])
        l0_bias = sb("l0_bias", [P, H1 // P])
        f_bias = sb("f_bias", [16, 2])

        SLAB = [("x", 20480), ("cond", 5120), ("q", 20480), ("kh", 40960), ("v", 20480), ("yp", 43008),
                ("w", 32768), ("y", 4096), ("film", 4096), ("film_raw", 4096), ("row_bias", 6144)]
        base = -(-nc.sbuf_base // 32) * 32
        sb("slab", [P, sum(n for _, n in SLAB) // 4 + 8])
        offset = {}
        for name, size in SLAB:
            offset[name] = base
            base += size

        def at(part, plus, name, shape, dt=F32):
            return nc.alloc_sbuf_tensor_at(name, shape, dt, offset=offset[part] + plus)

        x = at("x", 0, "x", [P, NT, D])
        cond = at("cond", 0, "cond", [96, N], F32R)
        q = at("q", 0, "q", [P, KD, N])
        kh = at("kh", 0, "kh", [P, 2, KD, NP], F32R)
        v = at("v", 0, "v", [P, NT, D])
        yT = at("yp", 0, "yT", [P, 2, KD, N], F32R)
        pT = at("yp", 0, "pT", [P, 2, NT + 1, 2 * P])
        masks = at("yp", 22528, "masks", [P, 3, NP])
        q_parts = at("yp", 37888, "q_parts", [P, 2, 2, 2 * P], F32R)
        w = at("w", 0, "w", [P, 2, 2, KD, D], F32R)
        w_raw = at("w", 0, "w_raw", [P, 2, 2, KD, D])
        s = at("w", 16384, "s", [P, 2, NP])
        y = at("y", 0, "y", [P, 2, D])
        film = at("film", 0, "film", [96, 2 * D], F32R)
        film_raw = at("film_raw", 0, "film_raw_t", [96, 2 * D])
        row_bias = at("row_bias", 0, "row_bias_t", [P, 3, D])
        relu_out = v[:, 0:2, :]
        counts = at("kh", 0, "counts", [P, NT, NP])
        phase = at("kh", 0, "phase", [64, 2, N])
        xT = at("yp", 0, "xT", [P, KD, N])
        mask_out = at("yp", 20480, "mask_out", [P, 2, NP])
        mask_log = at("yp", 30720, "mask_log", [P, 2, NP])
        hidden = at("kh", 0, "hidden", [P, H1 // P, N])
        w1_l0 = at("w", 0, "w1_l0", [P, KD, H1])
        w2_l0 = at("w", 16384, "w2_l0", [P, H1 // P, D])
        x1 = at("kh", 0, "x1", [P, NT, D])
        iota_n = at("yp", 0, "iota_n", [P, NP], F16)
        hot = at("yp", 2560, "hot", [P, 2 * BATCH, NP + P], BF16)
        zero = at("yp", 13824, "zero", [1, BANK], BF16)
        idx_rows = at("yp", 14848, "idx_rows", [P, 4, ET], I32)
        idx_f = at("yp", 16896, "idx_f", [P, 4, ET])
        span = at("yp", 18944, "span", [P, 4])
        tl = at("yp", 19008, "tl", [1, 2, NE])
        tl_iota = at("yp", 20480, "tl_iota", [1, NE])
        tl_i32 = at("yp", 21504, "tl_i32", [1, NE], I32)
        bounds = at("yp", 22528, "bounds", [1, 3, NT])
        rel = at("v", 0, "rel_t", [1, 3, NT, NE])
        emb = at("q", 0, "emb", [64, KD, N])
        f_mats = at("film_raw", 0, "f_mats", [64, 32])
        ps = ctx.enter_context(nc.psum_tensor("ps", [P, 8, BANK], F32))
        ps_flat = ps[:].rearrange("p b c -> p (b c)")

        idx_in, x_in_s, small_in, noise_in = sem("idx_in"), sem("x_loaded"), sem("small_in"), sem("noise_in")
        w1_in, w2_in, b2_in = sem("w1_in"), sem("w2_in"), sem("b2_in")
        consts = sem("consts")
        idx_t, tiles_s = sem("idx_transposed"), sem("edge_tables")
        dv = sem("dve_step")
        hot_ready, hot_used = sem("hot_ready"), sem("hot_used")
        block_counted, counts_out = sem("block_counted"), sem("counts_out")
        cond_mm, cond_dve, cond_act = sem("cond_mm"), sem("cond_dve"), sem("cond_act")
        made = sem("product_made")
        act_out, dve_out = sem("copied_by_scalar"), sem("copied_by_vector")
        stat_s, mv_ready, rstd_done, rstd_ready, ve_s = (
            sem("stats_made"), sem("mean_var_ready"), sem("rstd_done"), sem("rstd_ready"), sem("ve"))
        xn_done, biased = sem("normed"), sem("bias_added")
        l0_twice, l0_ready = sem("x_twice"), sem("l0_normed")
        mask_ln, mask_dve, mask_ready, mask_saved = sem("mask_ln"), sem("mask_dve"), sem("mask_ready"), [sem(f"mask_saved_{n}") for n in range(2)]
        mask_in = [sem(f"mask_in_{n}") for n in range(3)]
        padded, tails_clear = sem("padding_cleared"), sem("tails_clear")
        w_in = [sem("w_in_first"), sem("w_in_second")]
        w_high, w_ready = sem("w_high"), sem("w_ready")
        bqk_in, mb1_in, film_in = sem("bq_bk_in"), sem("m_b1_in"), sem("film_in")
        bv_in, bo_in, mb2_in = sem("bv_in"), sem("bo_in"), sem("m_b2_in")
        film_hi, film_ready = sem("film_high"), sem("film_ready")
        q_high, q_ready = sem("q_high"), sem("q_ready")
        o_high, o_ready = sem("o_high"), sem("o_ready")
        h_high, h_ready = sem("h_high"), sem("h_ready")
        scored, masked, negm_s, exp_done = sem("scored"), sem("masked"), sem("neg_max"), sem("exp_done")
        den_s, rep_ready = sem("denominator"), sem("reciprocal_spread")
        turned, pT_out, summed, head_out = sem("turned"), sem("weights_out"), sem("summed"), sem("head_out")
        x1_saved, x1_in, added, y_out, out_s = sem("x1_saved"), sem("x1_in"), sem("x1_added"), sem("y_out"), sem("out_written")
        passed = sem("passed_waits")
        block = ctx.enter_context(nc.Block())

        @block.sync
        def _(sp):
            for a, ind in enumerate((src, dst)):
                r = ind.rearrange("(t e) -> t e", e=ET)
                sp.dma_start(idx_rows[:, 2 * a, :], r[0:P]).then_inc(idx_in, 16)
                sp.dma_start(idx_rows[0:NE - P, 2 * a + 1, :], r[P:NE]).then_inc(idx_in, 16)
            sp.dma_start(phase[0:32, 0, :], noise.rearrange("n o -> o n").broadcast_to([32, N])).then_inc(noise_in, 16)
            sp.dma_start(f_mats[0:64, 0:16], f_w1[:, :]).then_inc(small_in, 16)
            sp.dma_start(f_mats[0:16, 16:32], f_w2[:, :]).then_inc(small_in, 16)
            sp.dma_start(f_bias[:, 0:1], f_b1.rearrange("(p o) -> p o", o=1)).then_inc(small_in, 16)
            sp.dma_start(f_bias[:, 1:2], f_b2.rearrange("(p o) -> p o", o=1)).then_inc(small_in, 16)
            sp.dma_start(eps1[:], eps0.rearrange("(o n) -> o n", o=1).broadcast_to([P, 1])).then_inc(small_in, 16)
            sp.dma_start(l0_bias[:], b1.rearrange("(m p) -> p m", p=P), allow_slow_non_contiguous=True).then_inc(small_in, 16)
            sp.dma_start(x[:, 0:NT - 1, :], x_in[0:(NT - 1) * P].rearrange("(t p) d -> p t d", p=P)).then_inc(x_in_s, 16)
            sp.dma_start(x[0:rows(NT - 1), NT - 1, :], x_in[(NT - 1) * P:N]).then_inc(x_in_s, 16)
            sp.dma_start(w1_l0[:], W1.rearrange("(k p) n -> p k n", p=P)).then_inc(w1_in, 16)
            sp.dma_start(w2_l0[:], W2.rearrange("(k p) n -> p k n", p=P)).then_inc(w2_in, 16)
            sp.dma_start(row_bias[:, 2, :], b2.rearrange("(o n) -> o n", o=1).broadcast_to([P, D])).then_inc(b2_in, 16)

            def load_col(n, b, i, s_):
                sp.dma_start(col_bias[:, n, :], b[i].rearrange("(m p) -> p m", p=P),
                             allow_slow_non_contiguous=True).then_inc(s_, 16)

            def load_row(n, b, i, s_):
                sp.dma_start(row_bias[:, n, :], b[bass.ds(i, 1)].broadcast_to([P, D])).then_inc(s_, 16)

            def load_film(i, sw, sb_, bw, bb):
                for c, (wt, bt) in enumerate(((sw, sb_), (bw, bb))):
                    for r in range(3):
                        sp.dma_start(film_raw[32 * r:32 * r + 16, c * D:(c + 1) * D], wt[i]).then_inc(film_in, 16)
                        sp.dma_start(film_raw[32 * r + 16:32 * r + 17, c * D:(c + 1) * D], bt[bass.ds(i, 1)]).then_inc(film_in, 16)

            def load_w(kind, wt, i):
                p = w_place(kind)
                sp.dma_start(w_raw[:, p, 1, :, :], wt[i].rearrange("(k p) n -> p k n", p=P)).then_inc(w_in[p], 16)

            load_col(0, bq, 0, bqk_in)
            load_col(1, bk, 0, bqk_in)
            load_col(2, m_b1, 0, mb1_in)
            load_row(0, bv, 0, bv_in)
            load_row(1, bo, 0, bo_in)
            for t in range(NT):
                sp.wait_ge(mask_ready, t + 1)
                sp.dma_start(mask_dram[t], mask_out[:, t % 2, :]).then_inc(mask_saved[t % 2], 16)
            sp.wait_ge(padded, 1)
            load_film(0, s1_w, s1_b, b1_w, b1_b)
            sp.wait_ge(made, l0.end[0])
            load_w("Q", wq, 0)
            load_w("K", wk, 0)
            sp.wait_ge(l0_twice, 2 * NT)
            load_row(2, m_b2, 0, mb2_in)
            for t in range(NT):
                sp.wait_ge(l0_ready, t + 1)
                sp.dma_start(x_first[t * P:t * P + rows(t)], x[0:rows(t), t, :]).then_inc(x1_saved, 16)
            sp.wait_ge(made, qkv0.made["Q", KD - 1, 2])
            load_w("V", wv, 0)

            def block_loads(c, more):
                i = c.block
                sp.wait_ge(film_ready, 2 * i + 1)
                load_film(i, s2_w, s2_b, b2_w, b2_b)
                sp.wait_ge(made, c.made)
                load_w("WO", wo, i)
                for t in range(NT):
                    if t >= 3:
                        sp.wait_ge(masked, i * U + UNITS.index(((t - 3) // 2, H - 1, (t - 3) % 2)) + 1)
                    elif t == 0:
                        for n in range(2):
                            sp.wait_ge(mask_saved[n], 16 * NT // 2)
                    sp.dma_start(masks[:, t % 3, :], mask_dram[t]).then_inc(mask_in[t % 3], 16)
                sp.wait_ge(turned, i * U + U)
                load_w("M1", m_w1, i)
                if more:
                    sp.wait_ge(biased, i * 2 * NT + NT)
                    load_row(0, bv, i + 1, bv_in)
                    load_row(1, bo, i + 1, bo_in)
                    load_col(0, bq, i + 1, bqk_in)
                    load_col(1, bk, i + 1, bqk_in)
                    sp.wait_ge(film_ready, 2 * i + 2)
                    load_film(i + 1, s1_w, s1_b, b1_w, b1_b)
                sp.wait_ge(made, c.made + wo_m1.made["WO", NT - 1, 0])
                load_w("M2", m_w2, i)
                if more:
                    sp.wait_ge(made, c.made + wo_m1.made["M1", KD - 1, 2])
                    load_w("Q", wq, i + 1)
                    sp.wait_ge(biased, i * 2 * NT + 2 * NT)
                    sp.wait_ge(h_ready, (i + 1) * 3 * KD)
                    load_row(2, m_b2, i + 1, mb2_in)
                    load_col(2, m_b1, i + 1, mb1_in)
                    sp.wait_ge(made, c.made + m2_qkv.made["M2", NT - 1, 0])
                    load_w("K", wk, i + 1)
                    sp.wait_ge(made, c.made + m2_qkv.made["Q", KD - 1, 2])
                    load_w("V", wv, i + 1)

            with sp.Fori(0, L - 1) as i:
                block_loads(now(i, sp), True)
            block_loads(last, False)
            sp.wait_ge(made, last.made + m2_last.end[0])
            sp.wait_ge(x1_saved, 16 * NT)
            sp.dma_start(x1[:, 0:NT - 1, :], x_first[0:(NT - 1) * P].rearrange("(t p) d -> p t d", p=P)).then_inc(x1_in, 16)
            sp.dma_start(x1[0:rows(NT - 1), NT - 1, :], x_first[(NT - 1) * P:N]).then_inc(x1_in, 16)
            for t in range(NT):
                sp.wait_ge(y_out, t + 1)
                sp.dma_start(out[t * P:t * P + rows(t)], x[0:rows(t), t, :]).then_inc(out_s, 16)
            sp.wait_ge(out_s, 16 * NT)

        @block.gpsimd
        def _(pool):
            nc.gpsimd.memset(ident[:], 0.0).then_inc(consts, 1)
            nc.gpsimd.memset(ones[:], 1.0).then_inc(consts, 1)
            nc.gpsimd.memset(zero[:], 0.0).then_inc(consts, 1)
            nc.gpsimd.memset(half[:], -0.5).then_inc(consts, 1)
            nc.gpsimd.memset(edge[:], -1.0).then_inc(consts, 1)
            pool.wait_ge(consts, 5)
            nc.gpsimd.affine_select(out=ident[:], in_=ident[:], compare_op=ALU.not_equal, fill=1.0, base=0,
                                    pattern=[[-1, P]], channel_multiplier=1).then_inc(consts, 1)
            nc.gpsimd.iota(iota_n[:], [[1, NP]], base=0, channel_multiplier=0,
                           allow_small_or_imprecise_dtypes=True).then_inc(consts, 1)
            nc.gpsimd.iota(tl_i32[:], [[1, NE]], base=0, channel_multiplier=0).then_inc(consts, 1)
            nc.gpsimd.iota(rep[0:32, 0:1].bitcast(I32), [[0, 1]], base=1, channel_multiplier=1).then_inc(consts, 1)

            def rstd_of(t, n):
                R = rows(t)
                pool.wait_ge(mv_ready, n + 1)
                pool.sem_inc(passed)
                nc.gpsimd.tensor_scalar(ve[0:R, t:t + 1], mv[0:R, t, 1:2], EPS, None, ALU.add).then_inc(ve_s, 1)
                pool.wait_ge(ve_s, n + 1)
                nc.gpsimd.tensor_tensor(rstd[0:R, t:t + 1], ve[0:R, t:t + 1], half[0:R, :], ALU.pow).then_inc(rstd_done, 1)
                pool.wait_ge(rstd_done, n + 1)
                pool.sem_inc(passed)
                nc.gpsimd.tensor_scalar(shift[0:R, t:t + 1], mv[0:R, t, 0:1], -1.0, rstd[0:R, t:t + 1], ALU.mult,
                                        ALU.mult).then_inc(rstd_ready, 1)

            pool.wait_ge(cond_mm, 6)
            nc.gpsimd.memset(film_raw[:], 0.0).then_inc(padded, 1)

            def split_film(n):
                pool.wait_ge(film_in, (n + 1) * 12 * 16)
                pool.sem_inc(passed)
                nc.gpsimd.tensor_copy(film[:], film_raw[:]).then_inc(film_hi, 1)
                pool.wait_ge(film_hi, n + 1)
                nc.gpsimd.tensor_tensor(film[64:96, :], film_raw[64:96, :], film[64:96, :].bitcast(F32),
                                        ALU.subtract).then_inc(film_ready, 1)
                pool.wait_ge(film_ready, n + 1)

            pool.wait_ge(made, l0.made["NB", KD - 1, 2])
            pool.wait_ge(x_in_s, 32)
            pool.wait_ge(b2_in, 16)
            for t in range(NT):
                xt = x[0:rows(t), t, :]
                nc.gpsimd.tensor_tensor(xt, xt, xt, ALU.add).then_inc(l0_twice, 1)
                pool.wait_ge(l0_twice, 2 * t + 1)
                nc.gpsimd.tensor_tensor(xt, xt, row_bias[0:rows(t), 2, :], ALU.add).then_inc(l0_twice, 1)
            split_film(0)
            for t in range(NT):
                rstd_of(t, t)

            def norm(n, bias_row, bias_in, value):
                for t in range(NT + 1):
                    if t < NT:
                        rstd_of(t, (n + 1) * NT + t)
                    if t >= 1:
                        R = rows(t - 1)
                        if t == 1:
                            pool.wait_ge(bias_in, value)
                        pool.wait_ge(xn_done, n * NT + t)
                        nc.gpsimd.tensor_tensor(x[0:R, t - 1, :], x[0:R, t - 1, :], row_bias[0:R, bias_row, :],
                                                ALU.add).then_inc(biased, 1)

            pool.wait_ge(x1_saved, 16 * NT)
            norm(0, 1, bo_in, 16)

            def pool_block(c, more):
                i = c.block
                pool.wait_ge(made, c.made)
                split_film(2 * i + 1)
                norm(2 * i + 1, 2, mb2_in, i * 16 + 16)
                if more:
                    pool.wait_ge(made, c.made + wo_m1.made["FB", NT - 1, 0])
                    split_film(2 * i + 2)
                    norm(2 * i + 2, 1, bo_in, i * 16 + 32)

            with pool.Fori(0, L - 1) as i:
                pool_block(now(i, pool), True)
            pool_block(last, False)
            for t in range(NT):
                rstd_of(t, (2 * L + 1) * NT + t)

        @block.scalar
        def _(act):
            act.wait_ge(cond_dve, 2)
            nc.scalar.activation(phase[0:32, 0, :], emb[0:32, 0, :], ACT.Sin).then_inc(cond_act, 1)
            nc.scalar.activation(phase[32:64, 0, :], emb[0:32, 1, :], ACT.Sin).then_inc(cond_act, 1)
            act.wait_ge(cond_dve, 3)
            nc.scalar.activation(emb[0:16, 1, :], emb[0:16, 0, :], ACT.Exp, scale=-1.0).then_inc(cond_act, 1)
            cps = ps_flat[:, 0:NP].rearrange("p (i d) -> p i d", d=P)
            act.sem_inc(counts_out)
            act.wait_ge(cond_mm, 3)
            with act.Fori(0, NT) as j:
                act.wait_ge(block_counted, j + 1)
                nc.scalar.copy(counts[:, :, bass.ds(j * P, P)], cps).then_inc(counts_out, 1)
            for t in range(NT):
                R = rows(t)
                act.wait_ge(made, l0.made["XT", t, 0])
                nc.scalar.copy(xT[:, :, t * P:t * P + R],
                               ps[:, l0.bank["XT", t, 0], :].rearrange("p (k r) -> p k r", r=P)[:, :, 0:R]).then_inc(act_out, 1)
            for t in range(NT):
                act.wait_ge(mask_dve, 2 * t + 1)
                nc.scalar.activation(mask_log[:, t % 2, :], mask_log[:, t % 2, :], ACT.Ln).then_inc(mask_ln, 1)
            for kind, a, b in l0.jobs:
                if kind != "H":
                    continue
                if (a, b) == (0, 0):
                    act.wait_ge(mask_ready, NT)
                act.wait_ge(made, l0.made[kind, a, b])
                c0, cn = GROUPS[b]
                nc.scalar.activation(hidden[:, a, c0:c0 + cn], ps[:, l0.bank[kind, a, b], 0:cn], ACT.Relu,
                                     bias=l0_bias[:, a:a + 1]).then_inc(act_out, 1)

            def products(jl, c, norm):
                for kind, a, b in jl.jobs:
                    if kind == "FS":
                        R = rows(a)
                        act.wait_ge(rstd_ready, (norm + 1) * NT + a + 1)
                        if a >= 2:
                            act.wait_ge(made, c.made + jl.made["T", a - 2, 0])
                        nc.scalar.activation(y[0:R, a % 2, :], x[0:R, a, :], ACT.Identity, bias=shift[0:R, a:a + 1],
                                             scale=rstd[0:R, a:a + 1]).then_inc(xn_done, 1)
                    elif kind == "W":
                        p = w_place(a)
                        n = w_index(a, c.block)
                        act.wait_ge(w_in[p], w_loads(a, c.block) * 16)
                        nc.scalar.copy(w[:, p, 0, :, :], w_raw[:, p, 1, :, :]).then_inc(w_high, 1)
                    elif kind == "OS":
                        R = rows(a)
                        if a == 0:
                            act.wait_ge(head_out, c.block * GH + GH)
                        nc.scalar.copy(yT[:, 0, :, a * P:a * P + R], q[:, :, a * P:a * P + R]).then_inc(o_high, 1)
                    elif kind in ON_SCALAR:
                        act.wait_ge(made, c.made + jl.made[kind, a, b])
                        bank = ps[:, jl.bank[kind, a, b], :]
                        if kind == "T":
                            R = rows(a)
                            nc.scalar.copy(yT[:, 0, :, a * P:a * P + R],
                                           bank.rearrange("p (k r) -> p k r", r=P)[:, :, 0:R]).then_inc(act_out, 1)
                        elif kind == "K":
                            c0, cn = GROUPS[b]
                            if (a, b) == (0, 0):
                                act.wait_ge(bqk_in, c.block * 32 + 64)
                            nc.scalar.activation(kh[:, 0, a, c0:c0 + cn], bank[:, 0:cn], ACT.Identity,
                                                 bias=col_bias[:, 1, a:a + 1]).then_inc(act_out, 1)
                        else:
                            c0, cn = GROUPS[b]
                            n = b * KD + a
                            if n == 0:
                                act.wait_ge(mb1_in, c.block * 16 + 16)
                            if n >= 2:
                                act.wait_ge(h_ready, c.block * 3 * KD + n - 1)
                            nc.scalar.activation(relu_out[:, n % 2, 0:cn], bank[:, 0:cn], ACT.Relu,
                                                 bias=col_bias[:, 2, a:a + 1]).then_inc(act_out, 1)
                            act.wait_ge(act_out, c.act + jl.act_out[kind, a, b])
                            nc.scalar.copy(kh[:, 0, a, c0:c0 + cn], relu_out[:, n % 2, 0:cn]).then_inc(h_high, 1)

            def q_part(gh, i):
                g, h = gh // H, gh % H
                wd = rows(2 * g) + rows(2 * g + 1)
                if gh >= 2:
                    act.wait_ge(scored, i * U + 2 * gh - 2)
                nc.scalar.copy(q_parts[:, gh % 2, 0, 0:wd], q[:, h, g * 2 * P:g * 2 * P + wd]).then_inc(q_high, 1)

            def attention(c):
                i = c.block

                def exp(u):
                    g, h, k = UNITS[u]
                    R = rows(2 * g + k)
                    act.wait_ge(negm_s, i * U + u + 1)
                    nc.scalar.activation(s[0:R, u % 2, :], s[0:R, u % 2, :], ACT.Exp, bias=small[0:R, u % 2, 1:2],
                                         accum_out=small[0:R, u % 2, 2:3]).then_inc(exp_done, 1)

                act.wait_ge(made, c.made)
                act.wait_ge(dve_out, c.dve)
                q_part(0, i)
                q_part(1, i)
                exp(0)
                for u, (g, h, k) in enumerate(UNITS):
                    gh = u // 2
                    if k == 1 and gh + 2 < GH:
                        q_part(gh + 2, i)
                    if u + 1 < U:
                        exp(u + 1)
                    R = rows(2 * g + k)
                    act.wait_ge(turned, i * U + u + 1)
                    if gh >= 2 and k == 0:
                        act.wait_ge(head_out, i * GH + gh - 1)
                    turn = ps_flat[:, 3 * BANK:3 * BANK + (NT + 1) * P].rearrange("p (t r) -> p t r", r=P)
                    nc.scalar.copy(pT[:, gh % 2, :, k * P:k * P + R], turn[:, :, 0:R]).then_inc(pT_out, 1)
                    if u == U // 2:
                        act.wait_ge(w_in[w_place("WO")], w_loads("WO", i) * 16)
                        nc.scalar.copy(w[:, w_place("WO"), 0, :, :], w_raw[:, w_place("WO"), 1, :, :]).then_inc(w_high, 1)

            products(qkv0, zero_now, 0)
            with act.Fori(0, L - 1) as i:
                c = now(i, act)
                attention(c)
                products(wo_m1, c, 2 * i + 1)
                products(m2_qkv, c, 2 * i + 2)
            attention(last)
            products(wo_m1, last, 2 * L - 1)

        @block.vector
        def _(dve):
            step = [0]

            def chain(ins):
                step[0] += 1
                ins.then_inc(dv, 1)
                dve.wait_ge(dv, step[0])

            dve.wait_ge(consts, 9)
            freq = rep[0:32, 1:2]
            chain(nc.vector.tensor_copy(freq, rep[0:32, 0:1].bitcast(I32)))
            chain(nc.vector.tensor_scalar(freq, freq, float(np.float32(2.0 * np.pi / 16)), None, ALU.mult))
            dve.wait_ge(noise_in, 16)
            ph, kk = phase[0:32, 0, :], phase[0:32, 1, :]
            chain(nc.vector.tensor_scalar(ph, ph, freq, None, ALU.mult))
            chain(nc.vector.tensor_scalar(kk, ph, float(1.0 / (2.0 * np.pi)), ROUND, ALU.mult, ALU.add))
            chain(nc.vector.tensor_scalar(kk, kk, ROUND, None, ALU.subtract))
            for part in TWO_PI:
                chain(nc.vector.scalar_tensor_tensor(ph, kk, -part, ph, ALU.mult, ALU.add))
            nc.vector.tensor_scalar(emb[0:32, 0, :], ph, 3.1415925, -3.1415925, ALU.min, ALU.max).then_inc(cond_dve, 1)
            dve.wait_ge(cond_dve, 1)
            chain(nc.vector.scalar_tensor_tensor(kk, emb[0:32, 0, :], -1.0, emb[0:32, 0, :], ALU.mult, ALU.max))
            nc.vector.tensor_scalar(emb[0:32, 1, :], kk, -1.0, float(np.pi / 2), ALU.mult, ALU.add).then_inc(cond_dve, 1)
            dve.wait_ge(idx_in, 64)
            for a in range(2):
                nc.vector.tensor_copy(idx_f[:, 2 * a, :], idx_rows[:, 2 * a, :]).then_inc(tiles_s, 1)
                nc.vector.tensor_copy(idx_f[0:NE - P, 2 * a + 1, :], idx_rows[0:NE - P, 2 * a + 1, :]).then_inc(tiles_s, 1)
            dve.wait_ge(tiles_s, 4)
            for a, R in ((0, P), (1, NE - P)):
                nc.vector.tensor_reduce(span[0:R, 2 * a:2 * a + 1], idx_f[0:R, 2 + a, :], AX.X, ALU.min).then_inc(tiles_s, 1)
                nc.vector.tensor_reduce(span[0:R, 2 * a + 1:2 * a + 2], idx_f[0:R, 2 + a, :], AX.X, ALU.max).then_inc(tiles_s, 1)
            dve.wait_ge(idx_t, 1)
            nc.vector.tensor_copy(edge[:, 0, 0:NE], ps[0:ET, 0, 0:NE]).then_inc(tiles_s, 1)
            nc.vector.tensor_copy(edge[:, 1, 0:NE], ps[0:ET, 1, 0:NE]).then_inc(tiles_s, 1)
            for a in range(2):
                nc.vector.tensor_copy(tl[:, a, :], ps[0:1, 2 + a, 0:NE]).then_inc(tiles_s, 1)
            chain(nc.vector.tensor_copy(tl_iota[:], tl_i32[:]))
            dve.wait_ge(tiles_s, 12)
            for j in range(NT):
                nc.vector.tensor_scalar(rel[:, 0, j, :], tl[:, 1, :], float(j * P), None, ALU.is_ge)
                chain(nc.vector.tensor_scalar(rel[:, 1, j, :], tl[:, 0, :], float((j + 1) * P), None, ALU.is_lt))
            chain(nc.vector.tensor_tensor(rel[:, 0], rel[:, 0], rel[:, 1], ALU.mult))
            tiles_b = tl_iota[:].rearrange("p (o t) -> p o t", o=1).broadcast_to([1, NT, NE])
            chain(nc.vector.scalar_tensor_tensor(rel[:, 2], rel[:, 0], -1024.0, tiles_b, ALU.mult, ALU.add))
            chain(nc.vector.scalar_tensor_tensor(rel[:, 1], tiles_b, 1.0, rel[:, 0], ALU.add, ALU.mult))
            chain(nc.vector.tensor_reduce(bounds[:, 1, :], rel[:, 1], AX.X, ALU.max))
            chain(nc.vector.tensor_reduce(bounds[:, 0, :], rel[:, 2], AX.X, ALU.min))
            chain(nc.vector.tensor_scalar(rel[:, 0, 0, 0:NT], bounds[:, 0, :], 0.0, 1024.0, ALU.is_lt, ALU.mult))
            chain(nc.vector.tensor_tensor(bounds[:, 0, :], bounds[:, 0, :], rel[:, 0, 0, 0:NT], ALU.add))
            chain(nc.vector.tensor_scalar(bounds[:, 1, :], bounds[:, 1, :], 1.0, None, ALU.max))
            chain(nc.vector.scalar_tensor_tensor(bounds[:, 0, :], bounds[:, 1, :], -1.0, bounds[:, 0, :], ALU.add, ALU.min))
            chain(nc.vector.tensor_tensor(bounds[:, 1, :], bounds[:, 1, :], bounds[:, 0, :], ALU.subtract))
            chain(nc.vector.tensor_scalar(bounds[:, 1, :], bounds[:, 1, :], 0.25, 0.375, ALU.mult, ALU.add))
            chain(nc.vector.tensor_scalar(bounds[:, 1, :], bounds[:, 1, :], ROUND, ROUND, ALU.add, ALU.subtract))
            chain(nc.vector.memset(bounds[:, 2, 0:1], 0.0))
            for j in range(1, NT):
                chain(nc.vector.tensor_tensor(bounds[:, 2, j:j + 1], bounds[:, 2, j - 1:j], bounds[:, 1, j - 1:j], ALU.add))
            nc.vector.tensor_copy(table[:], bounds[:]).then_inc(tiles_s, 1)
            dve.wait_ge(cond_mm, 3)
            dve.wait_ge(small_in, 16 * 6)
            dve.wait_ge(cond_act, 2)
            nc.vector.tensor_scalar(emb[0:16, 0, :], ps_flat[0:16, 4 * BANK:4 * BANK + N], f_bias[:, 0:1], None,
                                    ALU.add).then_inc(cond_dve, 1)
            dve.wait_ge(cond_act, 3)
            chain(nc.vector.tensor_scalar(emb[0:16, 1, :], emb[0:16, 1, :], 1.0, None, ALU.add))
            chain(nc.vector.reciprocal(emb[0:16, 1, :], emb[0:16, 1, :]))
            nc.vector.tensor_tensor(emb[0:16, 2, :], emb[0:16, 0, :], emb[0:16, 1, :], ALU.mult).then_inc(cond_dve, 1)
            chain(nc.vector.memset(emb[0:32, 3, :], 1.0))
            dve.wait_ge(cond_mm, 6)
            chain(nc.vector.tensor_scalar(emb[0:16, 3, :], ps_flat[0:16, 4 * BANK:4 * BANK + N], f_bias[:, 1:2], None, ALU.add))
            nc.vector.tensor_copy(cond[0:32, :], emb[0:32, 3, :]).then_inc(cond_dve, 1)
            dve.wait_ge(cond_dve, 5)
            nc.vector.tensor_copy(cond[64:96, :], emb[0:32, 3, :]).then_inc(cond_dve, 1)
            nc.vector.tensor_tensor(cond[32:64, :], emb[0:32, 3, :], cond[0:32, :].bitcast(F32),
                                    ALU.subtract).then_inc(cond_dve, 1)
            dve.wait_ge(cond_dve, 7)
            chain(nc.vector.tensor_scalar(eps1[:], eps1[:], 1.0, None, ALU.add))
            dve.wait_ge(tiles_s, 13)
            dve.sem_inc(hot_used, 2)
            with dve.Fori(0, NT) as j:
                first = dve.value_load(table[0:1, 0, bass.ds(j, 1)], min_val=0, max_val=NE - 1)
                quads = dve.value_load(table[0:1, 1, bass.ds(j, 1)], min_val=1, max_val=NE // 4 + 1)
                before = dve.value_load(table[0:1, 2, bass.ds(j, 1)], min_val=0, max_val=NT * (NE // 4 + 1))
                block_start = dve.snap(j * P)
                with dve.Fori(0, quads) as k:
                    t = dve.snap(first + k * 4)
                    n = dve.snap((before + k) * 2)
                    for m in range(2 * BATCH):
                        if m % BATCH == 0:
                            dve.wait_ge(hot_used, n + m // BATCH + 1)
                        nc.vector.tensor_scalar(hot[0:ET, m, 0:NP], iota_n[0:ET], edge[:, 0, bass.ds(t + m, 1)], None,
                                                ALU.is_equal)
                        ins = nc.vector.tensor_scalar(hot[0:ET, m, NP:NP + P], iota_n[0:ET, bass.ds(block_start, P)],
                                                      edge[:, 1, bass.ds(t + m, 1)], None, ALU.is_equal)
                        if m % BATCH == BATCH - 1:
                            ins.then_inc(hot_ready, 1)

            def stats(t, n):
                R = rows(t)
                nc.vector.bn_stats(stat6[0:R, t, :], x[0:R, t, :]).then_inc(stat_s, 1)
                dve.wait_ge(stat_s, n + 1)
                dve.sem_inc(passed)
                nc.vector.bn_aggr(mv[0:R, t, :], stat6[0:R, t, :]).then_inc(mv_ready, 1)

            def mask_tile(t):
                if t == 0:
                    dve.wait_ge(counts_out, NT + 1)
                if t >= 2:
                    dve.wait_ge(mask_saved[t % 2], 16 * (t // 2))
                nc.vector.tensor_scalar(mask_log[:, t % 2, :], counts[:, t, :], 1.0, None, ALU.max).then_inc(mask_dve, 1)
                nc.vector.tensor_scalar(mask_out[:, t % 2, :], counts[:, t, :], 0.5, NOTHING, ALU.is_lt,
                                        ALU.mult).then_inc(mask_dve, 1)
                dve.wait_ge(mask_dve, 2 * t + 2)
                dve.wait_ge(mask_ln, t + 1)
                nc.vector.tensor_tensor(mask_out[:, t % 2, :], mask_out[:, t % 2, :], mask_log[:, t % 2, :],
                                        ALU.add).then_inc(mask_ready, 1)

            for kind, a, b in l0.jobs:
                if kind not in ON_VECTOR:
                    continue
                if kind == "NB":
                    if b * KD + a < NT:
                        mask_tile(b * KD + a)
                    dve.wait_ge(made, l0.made[kind, a, b])
                    bank = ps[:, l0.bank[kind, a, b], :]
                    if (a, b) == (0, 0):
                        dve.wait_ge(act_out, l0.act_out["XT", NT - 1, 0])
                    c0, cn = GROUPS[b]
                    nc.vector.scalar_tensor_tensor(q[:, a, c0:c0 + cn], xT[:, a, c0:c0 + cn], eps1[:, 0:1],
                                                   bank[:, 0:cn], ALU.mult, ALU.add).then_inc(dve_out, 1)
                else:
                    R = rows(a)
                    dve.wait_ge(made, l0.made[kind, a, b])
                    bank = ps[:, l0.bank[kind, a, b], :]
                    dve.wait_ge(l0_twice, 2 * a + 2)
                    nc.vector.tensor_tensor(x[0:R, a, :], bank[0:R, :], x[0:R, a, :], ALU.add).then_inc(dve_out, 1)
                    dve.wait_ge(dve_out, l0.dve_out[kind, a, b])
                    stats(a, a)
            for t in range(NT):
                R = rows(t)
                dve.wait_ge(rstd_ready, t + 1)
                nc.vector.tensor_scalar(x[0:R, t, :], x[0:R, t, :], mv[0:R, t, 0:1], rstd[0:R, t:t + 1],
                                        ALU.subtract, ALU.mult).then_inc(l0_ready, 1)
                dve.wait_ge(l0_ready, t + 1)
                stats(t, NT + t)
            nc.vector.memset(kh[:, :, :, N:NP].bitcast(F32), 0.0).then_inc(tails_clear, 1)
            nc.vector.memset(v[:, NT - 1, :], 0.0).then_inc(tails_clear, 1)
            dve.wait_ge(tails_clear, 2)

            def products(jl, c, norm):
                before = norm * NT
                for kind, a, b in jl.jobs:
                    R = rows(a) if kind not in ("Q", "K", "M1", "W") else P
                    if kind == "W":
                        p = w_place(a)
                        n = w_index(a, c.block)
                        dve.wait_ge(w_high, n + 1)
                        nc.vector.tensor_tensor(w[:, p, 1, :, :], w_raw[:, p, 1, :, :], w[:, p, 0, :, :].bitcast(F32),
                                                ALU.subtract).then_inc(w_ready, 1)
                        continue
                    if kind == "OS":
                        dve.wait_ge(o_high, c.block * NT + a + 1)
                        tile = slice(a * P, a * P + R)
                        nc.vector.tensor_tensor(yT[:, 1, :, tile], q[:, :, tile], yT[:, 0, :, tile].bitcast(F32),
                                                ALU.subtract).then_inc(o_ready, 1)
                        continue
                    if kind == "M1":
                        c0, cn = GROUPS[b]
                        n = b * KD + a
                        dve.wait_ge(h_high, c.block * 3 * KD + n + 1)
                        nc.vector.tensor_tensor(kh[:, 1, a, c0:c0 + cn], relu_out[:, n % 2, 0:cn],
                                                kh[:, 0, a, c0:c0 + cn].bitcast(F32), ALU.subtract).then_inc(h_ready, 1)
                        continue
                    if kind == "FS":
                        norm_tile(jl, c, before, a)
                        continue
                    if kind == "FB":
                        continue
                    dve.wait_ge(made, c.made + jl.made[kind, a, b])
                    if kind in ("T", "K"):
                        dve.wait_ge(act_out, c.act + jl.act_out[kind, a, b])
                    bank = ps[:, jl.bank[kind, a, b], :]
                    mine = c.dve + jl.dve_out[kind, a, b]
                    if kind == "T":
                        turned_tile = bank.rearrange("p (k r) -> p k r", r=P)[:, :, 0:R]
                        high = yT[:, 0, :, a * P:a * P + R].bitcast(F32)
                        nc.vector.tensor_tensor(yT[:, 1, :, a * P:a * P + R], turned_tile, high,
                                                ALU.subtract).then_inc(dve_out, 1)
                    elif kind == "Q":
                        c0, cn = GROUPS[b]
                        if (a, b) == (0, 0):
                            dve.wait_ge(bqk_in, c.block * 32 + 64)
                        nc.vector.tensor_scalar(q[:, a, c0:c0 + cn], bank[:, 0:cn], col_bias[:, 0, a:a + 1],
                                                float(P ** -0.5), ALU.add, ALU.mult).then_inc(dve_out, 1)
                    elif kind == "K":
                        c0, cn = GROUPS[b]
                        nc.vector.scalar_tensor_tensor(kh[:, 1, a, c0:c0 + cn], bank[:, 0:cn], col_bias[:, 1, a:a + 1],
                                                       kh[:, 0, a, c0:c0 + cn].bitcast(F32), ALU.add,
                                                       ALU.subtract).then_inc(dve_out, 1)
                    elif kind == "V":
                        if a == 0:
                            dve.wait_ge(bv_in, c.block * 16 + 32)
                        nc.vector.tensor_tensor(v[0:R, a, :], bank[0:R, :], row_bias[0:R, 0, :],
                                                ALU.add).then_inc(dve_out, 1)
                    else:
                        done = before if kind == "WO" else norm_before_m2(jl, c)
                        dve.wait_ge(biased, done + a + 1 - (NT if kind == "WO" else 0))
                        nc.vector.tensor_tensor(x[0:R, a, :], bank[0:R, :], x[0:R, a, :], ALU.add).then_inc(dve_out, 1)
                        dve.wait_ge(dve_out, mine)
                        if kind == "WO" or jl is m2_qkv:
                            stats(a, before + NT + a)

            def norm_before_m2(jl, c):
                return (2 * c.block + 1) * NT

            def norm_tile(jl, c, before, a):
                R = rows(a)
                dve.wait_ge(xn_done, before + a + 1)
                dve.wait_ge(made, c.made + jl.made["FS", a, 0])
                nc.vector.scalar_tensor_tensor(y[0:R, a % 2, :], ps[0:R, jl.bank["FS", a, 0], :], 1.0, y[0:R, a % 2, :],
                                               ALU.add, ALU.mult).then_inc(dve_out, 1)
                dve.wait_ge(dve_out, c.dve + jl.dve_out["FS", a, 0])
                dve.wait_ge(made, c.made + jl.made["FB", a, 0])
                nc.vector.tensor_tensor(y[0:R, a % 2, :], ps[0:R, jl.bank["FB", a, 0], :], y[0:R, a % 2, :],
                                        ALU.add).then_inc(dve_out, 1)

            def attention(c):
                i = c.block

                def q_part(gh):
                    g, h = gh // H, gh % H
                    wd = rows(2 * g) + rows(2 * g + 1)
                    dve.wait_ge(q_high, i * GH + gh + 1)
                    nc.vector.tensor_tensor(q_parts[:, gh % 2, 1, 0:wd], q[:, h, g * 2 * P:g * 2 * P + wd],
                                            q_parts[:, gh % 2, 0, 0:wd].bitcast(F32), ALU.subtract).then_inc(q_ready, 1)

                def mask(u):
                    g, h, k = UNITS[u]
                    t = 2 * g + k
                    R = rows(t)
                    if h == 0:
                        loads = len(range(t % 3, NT, 3))
                        dve.wait_ge(mask_in[t % 3], i * 16 * loads + 16 * (t // 3 + 1))
                    dve.wait_ge(scored, i * U + u + 1)
                    if u >= 2:
                        dve.wait_ge(turned, i * U + u - 1)
                    dve.sem_inc(passed)
                    nc.vector.tensor_tensor_reduce(s[0:R, u % 2, :], ps_flat[0:R, 0:NP], masks[0:R, t % 3, :],
                                                   1.0, LOWEST, ALU.add, ALU.max, small[0:R, u % 2, 0:1]).then_inc(masked, 1)
                    dve.wait_ge(masked, i * U + u + 1)
                    nc.vector.tensor_scalar(small[0:R, u % 2, 1:2], small[0:R, u % 2, 0:1], -1.0, None,
                                            ALU.mult).then_inc(negm_s, 1)

                q_part(0)
                q_part(1)
                mask(0)
                for u, (g, h, k) in enumerate(UNITS):
                    R = rows(2 * g + k)
                    dve.wait_ge(exp_done, i * U + u + 1)
                    nc.vector.tensor_scalar(small[0:R, u % 2, 2:3], small[0:R, u % 2, 2:3], 0.5, None,
                                            ALU.max).then_inc(den_s, 1)
                    dve.wait_ge(den_s, (i * U + u) * 2 + 1)
                    nc.vector.reciprocal(small[0:R, u % 2, 3:4], small[0:R, u % 2, 2:3]).then_inc(den_s, 1)
                    dve.wait_ge(den_s, (i * U + u) * 2 + 2)
                    if u >= 1:
                        dve.wait_ge(turned, i * U + u)
                    nc.vector.tensor_scalar(rep[0:R, :], ones[0:R, :], small[0:R, u % 2, 3:4], None,
                                            ALU.mult).then_inc(rep_ready, 1)
                    if u + 1 < U:
                        mask(u + 1)
                    if k == 1 and u // 2 + 2 < GH:
                        q_part(u // 2 + 2)
                    for gh in [u // 2 - 1] * (k == 1 and u >= 2) + [u // 2] * (u == U - 1):
                        gg, hh = gh // H, gh % H
                        wd = rows(2 * gg) + rows(2 * gg + 1)
                        dve.wait_ge(summed, i * GH + gh + 1)
                        dve.wait_ge(pT_out, i * U + 2 * gh + 2)
                        nc.vector.tensor_tensor(q[:, hh, gg * 2 * P:gg * 2 * P + wd], ps[:, 6 + gh % 2, 0:wd],
                                                pT[:, gh % 2, NT, 0:wd], ALU.mult).then_inc(head_out, 1)
                    if u == U // 2:
                        p = w_place("WO")
                        dve.wait_ge(w_high, w_index("WO", i) + 1)
                        nc.vector.tensor_tensor(w[:, p, 1, :, :], w_raw[:, p, 1, :, :], w[:, p, 0, :, :].bitcast(F32),
                                                ALU.subtract).then_inc(w_ready, 1)

            products(qkv0, zero_now, 0)
            with dve.Fori(0, L - 1) as i:
                c = now(i, dve)
                attention(c)
                products(wo_m1, c, 2 * i + 1)
                products(m2_qkv, c, 2 * i + 2)
            attention(last)
            products(wo_m1, last, 2 * L - 1)
            products(m2_last, last, 2 * L)
            dve.wait_ge(x1_in, 32)
            for t in range(NT):
                R = rows(t)
                nc.vector.tensor_tensor(x[0:R, t, :], x[0:R, t, :], x1[0:R, t, :], ALU.add).then_inc(added, 1)
                dve.wait_ge(added, t + 1)
                stats(t, (2 * L + 1) * NT + t)
            for t in range(NT):
                R = rows(t)
                dve.wait_ge(rstd_ready, (2 * L + 1) * NT + t + 1)
                nc.vector.tensor_scalar(x[0:R, t, :], x[0:R, t, :], mv[0:R, t, 0:1], rstd[0:R, t:t + 1],
                                        ALU.subtract, ALU.mult).then_inc(y_out, 1)

        @block.tensor
        def _(pe):
            mm = nc.tensor.matmul
            pe.wait_ge(consts, 6)
            pe.wait_ge(tiles_s, 8)
            for a in range(2):
                nc.tensor.transpose(ps[0:ET, a, 0:P], idx_f[:, 2 * a, :], ident[:])
                nc.tensor.transpose(ps[0:ET, a, P:NE], idx_f[0:NE - P, 2 * a + 1, :], ident[0:NE - P, 0:NE - P])
            for a in range(2):
                nc.tensor.transpose(ps[0:1, 2 + a, 0:P], span[:, a:a + 1], ident[:])
                mine = nc.tensor.transpose(ps[0:1, 2 + a, P:NE], span[0:NE - P, 2 + a:3 + a], ident[0:NE - P, 0:NE - P])
            mine.then_inc(idx_t, 1)
            pe.wait_ge(cond_act, 2)
            pe.wait_ge(small_in, 16 * 6)
            for g, (c0, cn) in enumerate(GROUPS):
                mm(ps[0:16, 4 + g, 0:cn], f_mats[0:64, 0:16], phase[0:64, 0, c0:c0 + cn], start=True, stop=True).then_inc(cond_mm, 1)
            pe.wait_ge(cond_dve, 4)
            for g, (c0, cn) in enumerate(GROUPS):
                mm(ps[0:16, 4 + g, 0:cn], f_mats[0:16, 16:32], emb[0:16, 2, c0:c0 + cn], start=True, stop=True).then_inc(cond_mm, 1)
            pe.wait_ge(tiles_s, 13)
            with pe.Fori(0, NT) as j:
                quads = pe.value_load(table[0:1, 1, bass.ds(j, 1)], min_val=1, max_val=NE // 4 + 1)
                before = pe.value_load(table[0:1, 2, bass.ds(j, 1)], min_val=0, max_val=NT * (NE // 4 + 1))
                pe.wait_ge(counts_out, j + 1)
                for b in range(3):
                    mm(ps[:, b, :], zero[:, 0:P], zero[:, 0:BANK], start=True, stop=False, skip_group_check=True)
                with pe.Fori(0, quads) as k:
                    n = pe.snap((before + k) * 2)
                    for m in range(2 * BATCH):
                        if m % BATCH == 0:
                            pe.wait_ge(hot_ready, n + m // BATCH + 1)
                        for i in range(NT):
                            mine = mm(ps_flat[:, i * P:(i + 1) * P], hot[0:ET, m, i * P:(i + 1) * P],
                                      hot[0:ET, m, NP:NP + P], start=False, stop=False, skip_group_check=True)
                        if m % BATCH == BATCH - 1:
                            mine.then_inc(hot_used, 1)
                for b in range(3):
                    mine = mm(ps[:, b, :], zero[:, 0:P], zero[:, 0:BANK], start=False, stop=True, skip_group_check=True)
                mine.then_inc(block_counted, 1)
            pe.wait_ge(counts_out, NT + 1)
            pe.wait_ge(x_in_s, 32)

            def bank_of(jl, key, c):
                n = jl.products.index(key)
                if n >= 8 and jl.products[n - 8] in jl.dve_out:
                    pe.wait_ge(dve_out, c.dve + jl.dve_out[jl.products[n - 8]])
                elif n >= 8:
                    pe.wait_ge(act_out, c.act + jl.act_out[jl.products[n - 8]])
                return ps[:, jl.bank[key], :]

            for kind, a, b in l0.jobs:
                bank = bank_of(l0, (kind, a, b), zero_now)
                if kind == "XT":
                    R = rows(a)
                    for k in range(KD):
                        mine = nc.tensor.transpose(bank[:, k * P:k * P + R], x[0:R, a, k * P:(k + 1) * P], ident[0:R, 0:R])
                elif kind == "NB":
                    c0, cn = GROUPS[b]
                    for k in range(NT):
                        R = rows(k)
                        mine = mm(bank[:, 0:cn], x[0:R, k, a * P:(a + 1) * P], counts[0:R, k, c0:c0 + cn],
                                  start=(k == 0), stop=(k == NT - 1))
                elif kind == "H":
                    c0, cn = GROUPS[b]
                    if a == 0:
                        pe.wait_ge(w1_in, 16)
                        pe.wait_ge(dve_out, l0.dve_out["NB", KD - 1, b])
                    for k in range(KD):
                        mine = mm(bank[:, 0:cn], w1_l0[:, k, a * P:(a + 1) * P], q[:, k, c0:c0 + cn],
                                  start=(k == 0), stop=(k == KD - 1))
                else:
                    R = rows(a)
                    if a == 0:
                        pe.wait_ge(w2_in, 16)
                    pe.wait_ge(act_out, l0.act_out["H", H1 // P - 1, min(a // 4, 2)])
                    for k in range(H1 // P):
                        mine = mm(bank[0:R, :], hidden[:, k, a * P:a * P + R], w2_l0[:, k, :], start=(k == 0),
                                  stop=(k == H1 // P - 1))
                mine.then_inc(made, 1)

            PARTS = ((1, 0), (0, 1), (0, 0))

            def three_passes(to, left, right, first=True, final=True):
                for n, (a, b) in enumerate(PARTS):
                    mine = mm(to, left(a), right(b), start=first and n == 0, stop=final and n == 2)
                return mine

            def products(jl, c, norm):
                for kind, a, b in jl.jobs:
                    if kind in ("W", "OS"):
                        continue
                    bank = bank_of(jl, (kind, a, b), c)
                    if kind in ("FS", "FB"):
                        R = rows(a)
                        if a == 0 and kind == "FS":
                            pe.wait_ge(film_ready, norm + 1)
                        c0 = 0 if kind == "FS" else D
                        mine = mm(bank[0:R, :], cond[:, a * P:a * P + R], film[:, c0:c0 + D], start=True, stop=True)
                    elif kind == "T":
                        R = rows(a)
                        pe.wait_ge(dve_out, c.dve + jl.dve_out["FB", a, 0])
                        for k in range(KD):
                            mine = nc.tensor.transpose(bank[:, k * P:k * P + R], y[0:R, a % 2, k * P:(k + 1) * P],
                                                       ident[0:R, 0:R])
                    elif kind in ("Q", "K", "M1"):
                        c0, cn = GROUPS[b]
                        p = w_place(kind)
                        if (a, b) == (0, 0):
                            pe.wait_ge(w_ready, w_index(kind, c.block) + 1)
                        if a == 0 and kind != "K":
                            pe.wait_ge(dve_out, c.dve + jl.dve_out["T", TILES_OF[b][-1], 0])
                        for k in range(KD):
                            mine = three_passes(bank[:, 0:cn], lambda n: w[:, p, n, k, a * P:(a + 1) * P],
                                                lambda n: yT[:, n, k, c0:c0 + cn], k == 0, k == KD - 1)
                    else:
                        R = rows(a)
                        p = w_place(kind)
                        left = kh if kind == "M2" else yT
                        if a == 0:
                            pe.wait_ge(w_ready, w_index(kind, c.block) + 1)
                        if kind == "WO":
                            pe.wait_ge(o_ready, c.block * NT + a + 1)
                        if kind == "M2":
                            pe.wait_ge(h_ready, c.block * 3 * KD + KD * (min(a // 4, 2) + 1))
                        for k in range(KD):
                            mine = three_passes(bank[0:R, :], lambda n: left[:, n, k, a * P:a * P + R],
                                                lambda n: w[:, p, n, k, :], k == 0, k == KD - 1)
                    mine.then_inc(made, 1)

            def attention(c):
                i = c.block

                def scores(u):
                    g, h, k = UNITS[u]
                    R = rows(2 * g + k)
                    gh = u // 2
                    if k == 0:
                        pe.wait_ge(q_ready, i * GH + gh + 1)
                    if u >= 1:
                        pe.wait_ge(masked, i * U + u)
                    for b, (c0, cn) in enumerate(((0, 512), (512, 512), (1024, 256))):
                        mine = three_passes(ps[0:R, b, 0:cn], lambda n: q_parts[:, gh % 2, n, k * P:k * P + R],
                                            lambda n: kh[:, n, h, c0:c0 + cn])
                    mine.then_inc(scored, 1)

                def weigh(gh, part):
                    g, h = gh // H, gh % H
                    wd = rows(2 * g) + rows(2 * g + 1)
                    if part == 0:
                        pe.wait_ge(pT_out, i * U + 2 * gh + 2)
                        if gh >= 2:
                            pe.wait_ge(head_out, i * GH + gh - 1)
                    for t in range(5 * part, 5 * part + 5):
                        mine = mm(ps[:, 6 + gh % 2, 0:wd], v[:, t, h * P:(h + 1) * P], pT[:, gh % 2, t, 0:wd],
                                  start=(t == 0), stop=(t == NT - 1))
                    if part == 1:
                        mine.then_inc(summed, 1)

                pe.wait_ge(act_out, c.act)
                pe.wait_ge(dve_out, c.dve)
                scores(0)
                for u, (g, h, k) in enumerate(UNITS):
                    R = rows(2 * g + k)
                    if u + 1 < U:
                        scores(u + 1)
                    if u >= 2:
                        weigh(u // 2 - 1, k)
                    pe.wait_ge(exp_done, i * U + u + 1)
                    pe.wait_ge(rep_ready, i * U + u + 1)
                    if u >= 1:
                        pe.wait_ge(pT_out, i * U + u)
                    turn = ps_flat[:, 3 * BANK:]
                    for t in range(NT):
                        nc.tensor.transpose(turn[:, t * P:t * P + R], s[0:R, u % 2, t * P:(t + 1) * P], ident[0:R, 0:R])
                    nc.tensor.transpose(turn[:, NT * P:NT * P + R], rep[0:R, :], ident[0:R, 0:R]).then_inc(turned, 1)
                for part in range(2):
                    weigh(GH - 1, part)
                pe.wait_ge(pT_out, i * U + U)

            pe.wait_ge(tails_clear, 2)
            pe.wait_ge(act_out, l0.end[1])
            pe.wait_ge(dve_out, l0.end[2])
            products(qkv0, zero_now, 0)
            with pe.Fori(0, L - 1) as i:
                c = now(i, pe)
                attention(c)
                products(wo_m1, c, 2 * i + 1)
                pe.wait_ge(act_out, c.act + wo_m1.end[1])
                pe.wait_ge(dve_out, c.dve + wo_m1.end[2])
                products(m2_qkv, c, 2 * i + 2)
            attention(last)
            products(wo_m1, last, 2 * L - 1)
            pe.wait_ge(act_out, last.act + wo_m1.end[1])
            pe.wait_ge(dve_out, last.dve + wo_m1.end[2])
            products(m2_last, last, 2 * L)


_INS = ['x', 'src', 'dst', 'node_vec1', 'L0_gnn_W1', 'L0_gnn_b1', 'L0_gnn_W2', 'L0_gnn_b2', 'L0_gnn_eps',
        'L1_gnn_f_w1', 'L1_gnn_f_b1', 'L1_gnn_f_w2', 'L1_gnn_f_b2', 'L1_gnn_s1_w', 'L1_gnn_s1_b', 'L1_gnn_b1_w',
        'L1_gnn_b1_b', 'L1_gnn_wq', 'L1_gnn_bq', 'L1_gnn_wk', 'L1_gnn_bk', 'L1_gnn_wv', 'L1_gnn_bv', 'L1_gnn_wo',
        'L1_gnn_bo', 'L1_gnn_s2_w', 'L1_gnn_s2_b', 'L1_gnn_b2_w', 'L1_gnn_b2_b', 'L1_gnn_m_w1', 'L1_gnn_m_b1',
        'L1_gnn_m_w2', 'L1_gnn_m_b2']


def kernel(**inputs):
    import numpy as _np
    import concourse.bacc as _bacc
    from concourse import mybir as _mybir
    from concourse.bass_utils import run_bass_kernel_spmd as _run

    nc = _bacc.Bacc("TRN2", target_bir_lowering=False, num_devices=1)
    arrays, args = {}, []
    for name in _INS:
        a = _np.ascontiguousarray(inputs[name])
        arrays[f"in_{name}_dram"] = a
        args.append(nc.dram_tensor(f"in_{name}_dram", a.shape, _mybir.dt.from_np(a.dtype), kind="ExternalInput").ap())
    args.append(nc.dram_tensor("out_dram", (N, D), F32, kind="ExternalOutput").ap())
    gnn_kernel(nc, *args)
    r = _run(nc, [arrays], core_ids=[0])
    return r.results[0]["out_dram"]
```

```python
from contextlib import ExitStack

import numpy as np

import concourse.bass as bass
from concourse import mybir

ALU = mybir.AluOpType
ACT = mybir.ActivationFunctionType
AX = mybir.AxisListType
F32 = mybir.dt.float32
F32R = mybir.dt.float32r
BF16 = mybir.dt.bfloat16
F16 = mybir.dt.float16
I32 = mybir.dt.int32

P = 128
N = 1250
D = 512
E = 21250
H1 = 1024
L = 4
H = 4
KD = D // P
NT = -(-N // P)
NP = NT * P
ET = 125
NE = E // ET
HOT = 4
NEP = 2 * NE + 4
NOTHING = -1e30
LOWEST = -1e29
EPS = 1e-5
BANK = 512
ROUND = 12582912.0
TWO_PI = (6.28125, 0.0019353071693331003, 1.0253131677018246e-11)
GROUPS = [(0, 512), (512, 512), (1024, N - 1024)]
TILES_OF = [range(0, 4), range(4, 8), range(8, NT)]
NG = NT // 2
UNITS = [(g, h, s) for g in range(NG) for h in range(H) for s in range(2)]


def rows(t):
    return min(P, N - t * P)


ON_SCALAR = ("XT", "H", "M1", "T", "K")
ON_VECTOR = ("NB", "C1", "C2", "Y", "WO", "FS", "FB", "T", "M2", "Q", "K", "V")
STEPS = ("W", "OS", "QP", "N0", "SIN", "EXP", "AV", "S0")
MASK_PLACE = (0, 1, 2, 3, 4, 0, 2, 3, 4, 0)


def after(jobs, job, step):
    n = jobs.index(job) + 1
    return jobs[:n] + [step] + jobs[n:]


def l0_jobs():
    jobs = [("XT", t, 0) for t in range(NT)]
    jobs += [("NB", m, g) for g in range(3) for m in range(KD)]
    jobs += [("H", m, g) for g in range(3) for m in range(H1 // P)]
    for job, step in ((("H", 0, 2), "C2"), (("H", 1, 1), "C1")):
        for g in (2, 1, 0):
            jobs = after(jobs, job, (step, g, 0))
    jobs = after(jobs, ("H", 7, 0), ("SIN", 0, 0))
    jobs = after(jobs, ("H", 3, 1), ("EXP", 0, 0))
    return jobs


def turned_and_dense(product, dense, weights):
    jobs = []
    for i in range(NT + 1):
        mine = [(product, i, 0)] if i < NT else []
        if product != "Y":
            jobs += mine
        elif i >= 1:
            jobs.append(("N0", i - 1, 0))
        if i >= 1:
            jobs += [("FS", i - 1, 0), ("FB", i - 1, 0)]
        if i == 4:
            jobs.append(("W", weights, 0))
        if i >= 3:
            jobs.append(("T", i - 3, 0))
        if product == "Y":
            jobs += mine
    jobs += [(dense, m, 0) for m in range(KD)]
    jobs += [("T", NT - 2, 0), ("T", NT - 1, 0)]
    jobs += [(dense, m, g) for g in (1, 2) for m in range(KD)]
    return jobs


def wo_m1_jobs():
    jobs = after(turned_and_dense("WO", "M1", "M1"), ("WO", 0, 0), ("AV", 0, 0))
    jobs = [("OS", t, 0) for t in range(2)] + jobs
    for t in range(2, NT):
        jobs.insert(jobs.index(("WO", t - 2, 0)), ("OS", t, 0))
    return after(jobs, ("M1", 1, 1), ("W", "M2", 0))


def qkv_jobs(product):
    jobs = turned_and_dense(product, "Q", "Q")
    jobs = after(jobs, ("Q", 1, 1), ("W", "K", 0))
    jobs += [("K", m, g) for g in range(3) for m in range(KD)]
    jobs = after(jobs, ("K", KD - 1, 1), ("W", "V", 0))
    jobs += [("V", t, 0) for t in range(NT)]
    jobs = after(jobs, ("V", NT - 3, 0), ("S0", 0, 0))
    for gh in range(2):
        jobs = after(jobs, ("V", 2 + gh, 0), ("QP", gh, 0))
    return jobs


def m2_last_jobs():
    return [("M2", t, 0) for t in range(NT)]


class Counts:

    def __init__(self, jobs, before=None):
        self.jobs, self.products, self.before = jobs, [], before
        first = before.next_bank if before else 0
        self.made, self.act_out, self.dve_out, self.bank = {}, {}, {}, {}
        made, act, dve = before.end if before else (0, 0, 0)
        for kind, a, b in jobs:
            if kind in ON_SCALAR:
                act += 1
                self.act_out[kind, a, b] = act
            if kind in ON_VECTOR:
                dve += 1
                self.dve_out[kind, a, b] = dve
            if kind in ON_SCALAR or kind in ON_VECTOR:
                made += 1
                self.made[kind, a, b] = made
                self.bank[kind, a, b] = (first + len(self.products)) % 8
                self.products.append((kind, a, b))
        self.end = (made, act, dve)
        self.next_bank = (first + len(self.products)) % 8

    def eight_before(self, n):
        if n >= 8:
            return self.products[n - 8], self
        if self.before:
            return self.before.products[n - 8], self.before
        return None, self


class Now:

    def __init__(self, made, act, dve, block):
        self.made, self.act, self.dve, self.block = made, act, dve, block


def gnn_kernel(nc, x_in, src, dst, noise, W1, b1, W2, b2, eps0, f_w1, f_b1, f_w2, f_b2, s1_w, s1_b,
               b1_w, b1_b, wq, bq, wk, bk, wv, bv, wo, bo, s2_w, s2_b, b2_w, b2_b, m_w1, m_b1,
               m_w2, m_b2, out):
    l0 = Counts(l0_jobs())
    qkv0 = Counts(qkv_jobs("Y"), l0)
    wo_m1 = Counts(wo_m1_jobs())
    m2_qkv = Counts(qkv_jobs("M2"), wo_m1)
    m2_last = Counts(m2_last_jobs(), wo_m1)
    start, per = qkv0.end, m2_qkv.end
    for counted in (qkv0, m2_qkv):
        assert all(counted.bank["V", t, 0] > 2 for t in range(NT - 3, NT))
    U = len(UNITS)
    GH = NG * H

    def now(i, eng=None):
        values = [i * per[n] + start[n] for n in range(3)]
        if eng is not None:
            values = [eng.snap(value) for value in values]
        return Now(*values, i)

    def y_stats(t):
        return 2 * t

    def n0_stats(t):
        return 2 * t + 1

    zero_now = Now(0, 0, 0, -1)
    last = now(L - 1)

    W_IN_BLOCK = {"WO": 3, "M1": 4, "M2": 5, "Q": 6, "K": 7, "V": 8}

    def w_index(kind, block):
        return 6 * block + W_IN_BLOCK[kind]

    def w_parts(kind, block):
        return (6 + KD - 1) * block + W_IN_BLOCK[kind] + 1 + (KD - 1) * (W_IN_BLOCK[kind] >= W_IN_BLOCK["WO"])

    def w_place(kind):
        return (W_IN_BLOCK[kind] + 1) % 2

    def w_loads(kind, block):
        c = W_IN_BLOCK[kind]
        return 3 * block + ((c + 1) // 2 if c % 2 else c // 2 + 1)

    x_first = nc.dram_tensor("x_first", (NT * P, D), F32, kind="Internal").ap()
    mask_dram = nc.dram_tensor("mask_dram", (NT, P, NP), F32, kind="Internal").ap()

    with ExitStack() as ctx:
        def sb(name, shape, dt=F32):
            return ctx.enter_context(nc.sbuf_tensor(name, shape, dt))

        def sem(name):
            return ctx.enter_context(nc.semaphore(name))

        ident = sb("ident", [P, P])
        rep = sb("rep", [P, P])
        stat6 = sb("stat6", [P, NT, 6])
        mv = sb("mv", [P, NT, 2])
        rstd = sb("rstd", [P, NT])
        ve = sb("ve", [P, NT])
        half = sb("half", [P, 1])
        small = sb("small", [P, 2, 4])
        eps1 = sb("eps1", [P, 1])
        table = sb("table", [1, NT + 1], I32)
        col_bias = sb("col_bias", [P, 3, KD])
        l0_bias = sb("l0_bias", [P, H1 // P])
        f_bias = sb("f_bias", [16, 2])

        SLAB = [("x", 20480), ("cond", 5024), ("q", 20480), ("kh", 40960), ("v", 20480), ("yp", 40960),
                ("q_parts", 4096), ("s_first", 5120), ("w", 32768), ("y", 6144), ("film", 4096), ("film_raw", 4096), ("row_bias", 6144)]
        base = -(-nc.sbuf_base // 32) * 32
        sb("slab", [P, sum(n for _, n in SLAB) // 4 + 8])
        offset = {}
        for name, size in SLAB:
            offset[name] = base
            base += size

        def at(part, plus, name, shape, dt=F32):
            return nc.alloc_sbuf_tensor_at(name, shape, dt, offset=offset[part] + plus)

        x = at("x", 0, "x", [P, NT, D])
        cond = at("cond", 0, "cond", [96, N], F32R)
        q = at("q", 0, "q", [P, KD, N])
        kh = at("kh", 0, "kh", [P, 2, KD, NP], F32R)
        v = at("v", 0, "v", [P, NT, D])
        yT = at("yp", 0, "yT", [P, 2, KD, N], F32R)
        pT = at("yp", 0, "pT", [P, 2, NT + 1, 2 * P])
        masks = [at("y", 0, "mask_y", [P, NP]), at("w", 0, "mask_w", [P, NP])] + [
            at("yp", 22528 + 5120 * n, f"mask_{n}", [P, NP]) for n in range(3)]
        q_parts = at("q_parts", 0, "q_parts", [P, 2, 2, 2 * P], F32R)
        w = at("w", 0, "w", [P, 2, 2, KD, D], F32R)
        w_raw = at("w", 0, "w_raw", [P, 2, 2, KD, D])
        s = at("w", 16384, "s", [P, 2, NP])
        s_first = at("s_first", 0, "s_first", [P, NP])

        def s_of(u):
            return s[0:rows(u % 2 + 2 * UNITS[u][0]), u % 2, :] if u else s_first[:]

        y = at("y", 0, "y", [P, 3, D])
        film = at("film", 0, "film", [96, 2 * D], F32R)
        film_raw = at("film_raw", 0, "film_raw_t", [96, 2 * D])
        row_bias = at("row_bias", 0, "row_bias_t", [P, 3, D])
        relu_out = v[:, 0:2, :]
        counts = at("kh", 0, "counts", [P, NT, NP])
        phase = at("yp", 20480, "phase", [64, 2, N])
        xT = at("q", 0, "xT", [P, KD, N])
        x_high = at("w", 0, "x_high", [P, NT, D], F32R)
        x_low = at("x", 0, "x_low", [P, NT, D], F32R)
        mask_out = at("yp", 20480, "mask_out", [P, 2, NP])
        mask_log = at("yp", 30720, "mask_log", [P, 2, NP])
        hidden = at("kh", 0, "hidden", [P, H1 // P, N])
        w1_l0 = at("w", 20480, "w1_l0", [P, KD, H1])
        w2_l0 = at("w", 0, "w2_l0", [P, H1 // P, D])
        x1 = at("v", 0, "x1", [P, NT, D])
        iota_n = at("yp", 0, "iota_n", [P, NP], F16)
        hot = at("yp", 2560, "hot", [P, HOT, NP + P], BF16)
        idx_rows = at("yp", 14848, "idx_rows", [P, 4, ET], I32)
        idx_f = at("yp", 16896, "idx_f", [P, 4, ET])
        span = at("yp", 18944, "span", [P, 4, NT])
        tl = at("yp", 19200, "tl", [NT, 2, NE])
        tl_iota = at("yp", 20608, "tl_iota", [NT, NE])
        tl_i32 = at("yp", 21504, "tl_i32", [NT, NE], I32)
        parts = at("yp", 24896, "parts", [1, 3, NT])
        most = at("yp", 25024, "most", [1, 1])
        spans = at("yp", 24832, "spans", [P, 4])
        bounds = at("yp", 24576, "bounds", [NT, 4])
        edge_of = at("yp", 24640, "edge_of", [NT, 2])
        edge_of_i = at("yp", 24672, "edge_of_i", [NT, 2], I32)
        earlier = at("yp", 24704, "earlier", [NT, NT])
        rel = at("v", 0, "rel", [NT, 3, NE])
        emb = at("v", 0, "emb", [64, KD, N])
        edge = at("film", 0, "edge", [ET, 2, NEP])
        f_mats = at("q_parts", 0, "f_mats", [64, 32])
        ps = ctx.enter_context(nc.psum_tensor("ps", [P, 8, BANK], F32))
        ps_flat = ps[:].rearrange("p b c -> p (b c)")

        idx_in, x_in_s, small_in, noise_in = sem("idx_in"), sem("x_loaded"), sem("small_in"), sem("noise_in")
        w1_in, w2_in, b2_in = sem("w1_in"), sem("w2_in"), sem("b2_in")
        consts = sem("consts")
        idx_t, tiles_s = sem("idx_transposed"), sem("edge_tables")
        bounds_ready, bounds_turned = sem("bounds_ready"), sem("bounds_turned")
        dv = sem("dve_step")
        hot_ready, hot_used = sem("hot_ready"), sem("hot_used")
        counts_out = sem("counts_out")
        cond_dve, cond_act = sem("cond_dve"), sem("cond_act")
        made = sem("product_made")
        act_out, dve_out = sem("copied_by_scalar"), sem("copied_by_vector")
        stat_s, mv_ready, rstd_ready, ve_s, biased = (
            sem("stats_made"), sem("mean_var_ready"), sem("rstd_ready"), sem("ve"), sem("bias_added"))
        x_high_done, x_split, x_whole = sem("x_high"), sem("x_split"), sem("x_whole_again")
        l0_twice, l0_ready = sem("x_twice"), sem("l0_normed")
        mask_ln, mask_dve, mask_ready = sem("mask_ln"), sem("mask_dve"), sem("mask_ready")
        mask_saved = [sem(f"mask_saved_{n}") for n in range(2)]
        mask_in = [sem(f"mask_in_{n}") for n in range(5)]
        padded, tails_clear = sem("padding_cleared"), sem("tails_clear")
        w_in = [sem("w_in_first"), sem("w_in_second")]
        w_high, w_ready = sem("w_high"), sem("w_ready")
        bqk_in, mb1_in, film_in = sem("bq_bk_in"), sem("m_b1_in"), sem("film_in")
        bv_in, bo_in, mb2_in = sem("bv_in"), sem("bo_in"), sem("m_b2_in")
        film_hi, film_ready = sem("film_high"), sem("film_ready")
        q_high, q_ready = sem("q_high"), sem("q_ready")
        o_high, o_ready = sem("o_high"), sem("o_ready")
        h_high, h_ready = sem("h_high"), sem("h_ready")
        scored, masked, negm_s, exp_done = sem("scored"), sem("masked"), sem("neg_max"), sem("exp_done")
        den_s, rep_ready = sem("denominator"), sem("reciprocal_spread")
        turned, pT_out, summed, head_out = sem("turned"), sem("weights_out"), sem("summed"), sem("head_out")
        x1_saved, x1_in, x1_late, added = sem("x1_saved"), sem("x1_in"), sem("x1_late"), sem("x1_added")
        y_out, out_s = sem("y_out"), sem("out_written")
        passed = sem("passed_waits")
        block = ctx.enter_context(nc.Block())

        EXACT = 4096
        CONSTS = 11
        QUADS_AT, BEFORE_AT = 2 ** 8, 2 ** 14
        TILES_DONE = 13

        def edge_tiles(eng, j):
            packed = eng.value_load(table[0:1, bass.ds(j, 1)], min_val=0, max_val=2 ** 24 - 1)
            first = eng.snap(packed & (QUADS_AT - 1)).with_bounds(min_val=0, max_val=NE - 1)
            quads = eng.snap((packed >> 8) & (BEFORE_AT // QUADS_AT - 1)).with_bounds(min_val=1, max_val=NE // HOT + 1)
            before = eng.snap(packed >> 14).with_bounds(min_val=0, max_val=NT * (NE // HOT + 1))
            return first, quads, before

        @block.sync
        def _(sp):
            for a, ind in enumerate((src, dst)):
                r = ind.rearrange("(t e) -> t e", e=ET)
                sp.dma_start(idx_rows[:, 2 * a, :], r[0:P]).then_inc(idx_in, 16)
                sp.dma_start(idx_rows[0:NE - P, 2 * a + 1, :], r[P:NE]).then_inc(idx_in, 16)
            sp.dma_start(x[:, 0:NT - 1, :], x_in[0:(NT - 1) * P].rearrange("(t p) d -> p t d", p=P)).then_inc(x_in_s, 16)
            sp.dma_start(x[0:rows(NT - 1), NT - 1, :], x_in[(NT - 1) * P:N]).then_inc(x_in_s, 16)
            sp.dma_start(f_mats[0:64, 0:16], f_w1[:, :]).then_inc(small_in, 16)
            sp.dma_start(f_mats[0:16, 16:32], f_w2[:, :]).then_inc(small_in, 16)
            sp.dma_start(f_bias[:, 0:1], f_b1.rearrange("(p o) -> p o", o=1)).then_inc(small_in, 16)
            sp.dma_start(f_bias[:, 1:2], f_b2.rearrange("(p o) -> p o", o=1)).then_inc(small_in, 16)
            sp.dma_start(eps1[:], eps0.rearrange("(o n) -> o n", o=1).broadcast_to([P, 1])).then_inc(small_in, 16)
            sp.dma_start(l0_bias[:], b1.rearrange("(m p) -> p m", p=P), allow_slow_non_contiguous=True).then_inc(small_in, 16)
            sp.dma_start(w1_l0[:], W1.rearrange("(k p) n -> p k n", p=P)).then_inc(w1_in, 16)
            sp.dma_start(row_bias[:, 2, :], b2.rearrange("(o n) -> o n", o=1).broadcast_to([P, D])).then_inc(b2_in, 16)

            def load_col(n, b, i, s_):
                sp.dma_start(col_bias[:, n, :], b[i].rearrange("(m p) -> p m", p=P),
                             allow_slow_non_contiguous=True).then_inc(s_, 16)

            def load_row(n, b, i, s_):
                sp.dma_start(row_bias[:, n, :], b[bass.ds(i, 1)].broadcast_to([P, D])).then_inc(s_, 16)

            def load_film(i, sw, sb_, bw, bb):
                for c, (wt, bt) in enumerate(((sw, sb_), (bw, bb))):
                    for r in range(3):
                        sp.dma_start(film_raw[32 * r:32 * r + 16, c * D:(c + 1) * D], wt[i]).then_inc(film_in, 16)
                        sp.dma_start(film_raw[32 * r + 16:32 * r + 17, c * D:(c + 1) * D], bt[bass.ds(i, 1)]).then_inc(film_in, 16)

            def load_w(kind, wt, i):
                p = w_place(kind)
                sp.dma_start(w_raw[:, p, 1, :, :], wt[i].rearrange("(k p) n -> p k n", p=P)).then_inc(w_in[p], 16)

            load_col(0, bq, 0, bqk_in)
            load_col(1, bk, 0, bqk_in)
            load_col(2, m_b1, 0, mb1_in)
            load_row(0, bv, 0, bv_in)
            load_row(1, bo, 0, bo_in)
            for t in range(NT):
                sp.wait_ge(mask_ready, t + 1)
                sp.dma_start(mask_dram[t], mask_out[:, t % 2, :]).then_inc(mask_saved[t % 2], 16)
            for n in range(2):
                sp.wait_ge(mask_saved[n], 16 * NT // 2)
            sp.dma_start(phase[0:32, 0, :], noise.rearrange("n o -> o n").broadcast_to([32, N])).then_inc(noise_in, 16)
            sp.wait_ge(padded, 2)
            load_film(0, s1_w, s1_b, b1_w, b1_b)
            sp.wait_ge(x_whole, NT)
            sp.dma_start(w2_l0[:], W2.rearrange("(k p) n -> p k n", p=P)).then_inc(w2_in, 16)
            sp.wait_ge(made, l0.end[0])
            load_w("Q", wq, 0)
            sp.wait_ge(l0_twice, 2 * NT)
            load_row(2, m_b2, 0, mb2_in)
            for t in range(NT):
                sp.wait_ge(l0_ready, t + 1)
                sp.dma_start(x_first[t * P:t * P + rows(t)], x[0:rows(t), t, :]).then_inc(x1_saved, 16)
            load_w("K", wk, 0)

            def load_mask(t):
                sp.dma_start(masks[MASK_PLACE[t]][:], mask_dram[t]).then_inc(mask_in[MASK_PLACE[t]], 16)

            def attention_loads(jl, c, i):
                sp.wait_ge(made, c.made + jl.made["Q", KD - 1, 2])
                load_w("V", wv, i)
                load_mask(0)
                sp.wait_ge(made, c.made + jl.made["K", KD - 1, 2])
                load_w("WO", wo, i)
                load_mask(1)

            attention_loads(qkv0, zero_now, 0)

            def block_loads(c, more):
                i = c.block
                sp.wait_ge(film_ready, 2 * i + 1)
                load_film(i, s2_w, s2_b, b2_w, b2_b)
                sp.wait_ge(made, c.made)
                for t in range(2, NT):
                    if t >= 5:
                        old = max(n for n in range(t) if MASK_PLACE[n] == MASK_PLACE[t])
                        sp.wait_ge(masked, i * U + UNITS.index((old // 2, H - 1, old % 2)) + 1)
                    load_mask(t)
                sp.wait_ge(turned, i * U + U)
                load_w("M1", m_w1, i)
                if more:
                    sp.wait_ge(biased, i * 2 * NT + NT)
                    load_row(0, bv, i + 1, bv_in)
                    load_row(1, bo, i + 1, bo_in)
                    load_col(0, bq, i + 1, bqk_in)
                    load_col(1, bk, i + 1, bqk_in)
                    sp.wait_ge(film_ready, 2 * i + 2)
                    load_film(i + 1, s1_w, s1_b, b1_w, b1_b)
                sp.wait_ge(made, c.made + wo_m1.made["WO", NT - 1, 0])
                load_w("M2", m_w2, i)
                if more:
                    sp.wait_ge(made, c.made + wo_m1.made["M1", KD - 1, 2])
                    load_w("Q", wq, i + 1)
                    sp.wait_ge(biased, i * 2 * NT + 2 * NT)
                    sp.wait_ge(h_ready, (i + 1) * 3 * KD)
                    load_row(2, m_b2, i + 1, mb2_in)
                    load_col(2, m_b1, i + 1, mb1_in)
                    sp.wait_ge(made, c.made + m2_qkv.made["M2", NT - 1, 0])
                    load_w("K", wk, i + 1)
                    attention_loads(m2_qkv, c, i + 1)

            with sp.Fori(0, L - 1) as i:
                block_loads(now(i, sp), True)
            block_loads(last, False)
            sp.wait_ge(x1_saved, 16 * NT)
            for t in (*range(2, NT), 0, 1):
                if t == 2:
                    sp.wait_ge(summed, L * GH)
                elif t == 0:
                    sp.wait_ge(h_ready, L * 3 * KD)
                sp.dma_start(x1[0:rows(t), t, :], x_first[t * P:t * P + rows(t)]).then_inc(x1_in if t >= 2 else x1_late, 16)
            for t in range(NT):
                sp.wait_ge(y_out, t + 1)
                sp.dma_start(out[t * P:t * P + rows(t)], x[0:rows(t), t, :]).then_inc(out_s, 16)
            sp.wait_ge(out_s, 16 * NT)

        @block.gpsimd
        def _(pool):
            nc.gpsimd.memset(ident[:], 0.0).then_inc(consts, 1)
            nc.gpsimd.memset(half[:], -0.5).then_inc(consts, 1)
            nc.gpsimd.memset(edge[:, 0, :], -1.0).then_inc(consts, 1)
            nc.gpsimd.memset(edge[:, 1, :], -1.0).then_inc(consts, 1)
            pool.wait_ge(consts, 4)
            nc.gpsimd.affine_select(out=ident[:], in_=ident[:], compare_op=ALU.not_equal, fill=1.0, base=0,
                                    pattern=[[-1, P]], channel_multiplier=1).then_inc(consts, 1)
            nc.gpsimd.iota(iota_n[:], [[1, NP]], base=0, channel_multiplier=0,
                           allow_small_or_imprecise_dtypes=True).then_inc(consts, 1)
            nc.gpsimd.iota(tl_i32[:], [[1, NE]], base=0, channel_multiplier=0).then_inc(consts, 1)
            nc.gpsimd.iota(edge_of_i[:], [[P, 2]], base=0, channel_multiplier=P).then_inc(consts, 1)
            nc.gpsimd.memset(earlier[:], 1.0).then_inc(consts, 1)
            pool.wait_ge(consts, CONSTS - 2)
            nc.gpsimd.affine_select(out=earlier[:], in_=earlier[:], compare_op=ALU.is_gt, fill=0.0, base=0,
                                    pattern=[[1, NT]], channel_multiplier=-1).then_inc(consts, 1)
            nc.gpsimd.iota(rep[0:32, 0:1].bitcast(I32), [[0, 1]], base=1, channel_multiplier=1).then_inc(consts, 1)

            def rstd_of(t, n):
                R = rows(t)
                pool.wait_ge(mv_ready, n + 1)
                pool.sem_inc(passed)
                nc.gpsimd.tensor_scalar(ve[0:R, t:t + 1], mv[0:R, t, 1:2], EPS, None, ALU.add).then_inc(ve_s, 1)
                pool.wait_ge(ve_s, n + 1)
                nc.gpsimd.tensor_tensor(rstd[0:R, t:t + 1], ve[0:R, t:t + 1], half[0:R, :], ALU.pow).then_inc(rstd_ready, 1)

            def split_film(n):
                pool.wait_ge(film_in, (n + 1) * 12 * 16)
                pool.sem_inc(passed)
                nc.gpsimd.tensor_copy(film[:], film_raw[:]).then_inc(film_hi, 1)
                pool.wait_ge(film_hi, n + 1)
                nc.gpsimd.tensor_tensor(film[64:96, :], film_raw[64:96, :], film[64:96, :].bitcast(F32),
                                        ALU.subtract).then_inc(film_ready, 1)
                pool.wait_ge(film_ready, n + 1)

            nc.gpsimd.memset(film_raw[:], 0.0).then_inc(padded, 1)
            pool.wait_ge(padded, 1)
            nc.gpsimd.affine_select(out=film_raw[0:32, 0:D], in_=film_raw[0:32, 0:D], compare_op=ALU.not_equal, fill=1.0,
                                    base=-17, pattern=[[0, D]], channel_multiplier=1).then_inc(padded, 1)

            pool.wait_ge(made, l0.made["XT", NT - 1, 0])
            pool.wait_ge(x_high_done, 2)
            for R, t0, t1 in ((P, 0, NT - 1), (rows(NT - 1), NT - 1, NT)):
                nc.gpsimd.tensor_tensor(x_low[0:R, t0:t1, :], x[0:R, t0:t1, :], x_high[0:R, t0:t1, :].bitcast(F32),
                                        ALU.subtract).then_inc(x_split, 1)

            pool.wait_ge(made, l0.made["NB", KD - 1, 2])
            pool.wait_ge(x_in_s, 32)
            pool.wait_ge(b2_in, 16)
            for t in range(NT):
                xt = x[0:rows(t), t, :]
                nc.gpsimd.tensor_tensor(xt, x_low[0:rows(t), t, :].bitcast(F32), x_high[0:rows(t), t, :].bitcast(F32),
                                        ALU.add).then_inc(x_whole, 1)
            for t in range(NT):
                xt = x[0:rows(t), t, :]
                if t == 0:
                    pool.wait_ge(x_whole, NT)
                nc.gpsimd.tensor_tensor(xt, xt, xt, ALU.add).then_inc(l0_twice, 1)
                pool.wait_ge(l0_twice, 2 * t + 1)
                nc.gpsimd.tensor_tensor(xt, xt, row_bias[0:rows(t), 2, :], ALU.add).then_inc(l0_twice, 1)
            split_film(0)
            for t in range(NT):
                rstd_of(t, y_stats(t))
                rstd_of(t, n0_stats(t))

            def add_bias(t, jl, c, row):
                R = rows(t)
                pool.wait_ge(dve_out, c.dve + jl.dve_out["FS", t, 0])
                nc.gpsimd.tensor_tensor(x[0:R, t, :], x[0:R, t, :], row_bias[0:R, row, :], ALU.add).then_inc(biased, 1)

            pool.wait_ge(x1_saved, 16 * NT)
            pool.wait_ge(bo_in, 16)
            for t in range(NT):
                add_bias(t, qkv0, zero_now, 1)

            def split_head_outputs(t, i):
                tile = slice(t * P, t * P + rows(t))
                pool.wait_ge(o_high, i * NT + t + 1)
                nc.gpsimd.tensor_tensor(kh[:, 1, :, tile], q[:, :, tile], kh[:, 0, :, tile].bitcast(F32),
                                        ALU.subtract).then_inc(o_ready, 1)

            def pool_block(c, more):
                i = c.block
                pool.wait_ge(made, c.made)
                split_film(2 * i + 1)
                pool.wait_ge(mb2_in, i * 16 + 16)
                split_head_outputs(0, i)
                split_head_outputs(1, i)
                for t in range(NT + 1):
                    if t + 2 < NT:
                        split_head_outputs(t + 2, i)
                    if t < NT:
                        rstd_of(t, (2 * i + 2) * NT + t)
                    if t >= 1:
                        add_bias(t - 1, wo_m1, c, 2)
                if more:
                    pool.wait_ge(made, c.made + wo_m1.made["FB", NT - 1, 0])
                    split_film(2 * i + 2)
                    pool.wait_ge(bo_in, i * 16 + 32)
                    for t in range(NT + 1):
                        if t < NT:
                            rstd_of(t, (2 * i + 3) * NT + t)
                        if t >= 1:
                            add_bias(t - 1, m2_qkv, c, 1)

            with pool.Fori(0, L - 1) as i:
                pool_block(now(i, pool), True)
            pool_block(last, False)
            for t in (*range(2, NT), 0, 1):
                R = rows(t)
                if t == 2:
                    pool.wait_ge(x1_in, 16 * (NT - 2))
                elif t == 0:
                    pool.wait_ge(x1_late, 32)
                pool.wait_ge(biased, 2 * L * NT)
                nc.gpsimd.tensor_tensor(x[0:R, t, :], x[0:R, t, :], x1[0:R, t, :], ALU.add).then_inc(added, 1)
            for t in range(NT):
                rstd_of(t, (2 * L + 1) * NT + t)

        @block.scalar
        def _(act):
            for t in range(NT):
                R = rows(t)
                act.wait_ge(made, l0.made["XT", t, 0])
                nc.scalar.copy(xT[:, :, t * P:t * P + R],
                               ps[:, l0.bank["XT", t, 0], :].rearrange("p (k r) -> p k r", r=P)[:, :, 0:R]).then_inc(act_out, 1)
            act.wait_ge(x_in_s, 32)
            for R, t0, t1 in ((P, 0, NT - 1), (rows(NT - 1), NT - 1, NT)):
                nc.scalar.copy(x_high[0:R, t0:t1, :], x[0:R, t0:t1, :]).then_inc(x_high_done, 1)
            act.wait_ge(tiles_s, TILES_DONE)
            with act.Fori(0, NT // 2) as jj:
                for place in range(2):
                    j = act.snap(jj * 2 + place)
                    _, quads, before = edge_tiles(act, j)
                    act.wait_ge(hot_used, (before + quads) * HOT + HOT)
                    nc.scalar.copy(counts[:, :, bass.ds(j * P, P)],
                                   ps_flat[:, BANK * 3 * place:BANK * 3 * place + NP].rearrange("p (i d) -> p i d", d=P)
                                   ).then_inc(counts_out, 1)
            for t in range(NT):
                act.wait_ge(mask_dve, 2 * t + 1)
                nc.scalar.activation(mask_log[:, t % 2, :], mask_log[:, t % 2, :], ACT.Ln).then_inc(mask_ln, 1)
            for kind, a, b in l0.jobs:
                if kind == "SIN":
                    act.wait_ge(cond_dve, 2)
                    nc.scalar.activation(phase[0:32, 0, :], emb[0:32, 0, :], ACT.Sin).then_inc(cond_act, 1)
                    nc.scalar.activation(phase[32:64, 0, :], emb[0:32, 1, :], ACT.Sin).then_inc(cond_act, 1)
                if kind == "EXP":
                    act.wait_ge(cond_dve, 3)
                    nc.scalar.activation(emb[0:16, 1, :], emb[0:16, 0, :], ACT.Exp, scale=-1.0).then_inc(cond_act, 1)
                if kind != "H":
                    continue
                if (a, b) == (0, 0):
                    act.wait_ge(mask_ready, NT)
                act.wait_ge(made, l0.made[kind, a, b])
                c0, cn = GROUPS[b]
                nc.scalar.activation(hidden[:, a, c0:c0 + cn], ps[:, l0.bank[kind, a, b], 0:cn], ACT.Relu,
                                     bias=l0_bias[:, a:a + 1]).then_inc(act_out, 1)

            def q_part(gh, i, queries_out=None):
                g, h = gh // H, gh % H
                wd = rows(2 * g) + rows(2 * g + 1)
                if gh < 2:
                    act.wait_ge(dve_out, queries_out)
                else:
                    act.wait_ge(scored, i * U + 2 * gh - 2)
                nc.scalar.copy(q_parts[:, gh % 2, 0, 0:wd], q[:, h, g * 2 * P:g * 2 * P + wd]).then_inc(q_high, 1)

            def split_head_outputs(t, i):
                R = rows(t)
                act.wait_ge(head_out, i * GH + (t // 2 + 1) * H)
                nc.scalar.copy(kh[:, 0, :, t * P:t * P + R], q[:, :, t * P:t * P + R]).then_inc(o_high, 1)

            def exp(u, i):
                g, h, k = UNITS[u]
                R = rows(2 * g + k)
                act.wait_ge(negm_s, i * U + u + 1)
                nc.scalar.activation(s_of(u), s_of(u), ACT.Exp, bias=small[0:R, u % 2, 1:2],
                                     accum_out=small[0:R, u % 2, 2:3]).then_inc(exp_done, 1)

            def products(jl, c, norm):
                for kind, a, b in jl.jobs:
                    if kind == "S0":
                        exp(0, c.block + 1)
                    if kind == "QP":
                        q_part(a, c.block + 1, c.dve + jl.dve_out["Q", KD - 1, 2])
                    elif kind == "W":
                        p = w_place(a)
                        n = w_index(a, c.block)
                        act.wait_ge(w_in[p], w_loads(a, c.block) * 16)
                        nc.scalar.copy(w[:, p, 0, :, :], w_raw[:, p, 1, :, :]).then_inc(w_high, 1)
                    elif kind == "OS":
                        if a >= 2:
                            split_head_outputs(a, c.block)
                    elif kind in ON_SCALAR:
                        act.wait_ge(made, c.made + jl.made[kind, a, b])
                        bank = ps[:, jl.bank[kind, a, b], :]
                        if kind == "T":
                            R = rows(a)
                            nc.scalar.copy(yT[:, 0, :, a * P:a * P + R],
                                           bank.rearrange("p (k r) -> p k r", r=P)[:, :, 0:R]).then_inc(act_out, 1)
                        elif kind == "K":
                            c0, cn = GROUPS[b]
                            if (a, b) == (0, 0):
                                act.wait_ge(bqk_in, c.block * 32 + 64)
                            nc.scalar.activation(kh[:, 0, a, c0:c0 + cn], bank[:, 0:cn], ACT.Identity,
                                                 bias=col_bias[:, 1, a:a + 1]).then_inc(act_out, 1)
                        else:
                            c0, cn = GROUPS[b]
                            n = b * KD + a
                            if n == 0:
                                act.wait_ge(mb1_in, c.block * 16 + 16)
                            if n >= 2:
                                act.wait_ge(h_ready, c.block * 3 * KD + n - 1)
                            nc.scalar.activation(relu_out[:, n % 2, 0:cn], bank[:, 0:cn], ACT.Relu,
                                                 bias=col_bias[:, 2, a:a + 1]).then_inc(act_out, 1)
                            act.wait_ge(act_out, c.act + jl.act_out[kind, a, b])
                            nc.scalar.copy(kh[:, 0, a, c0:c0 + cn], relu_out[:, n % 2, 0:cn]).then_inc(h_high, 1)

            def attention(c):
                i = c.block

                for u, (g, h, k) in enumerate(UNITS):
                    gh = u // 2
                    if k == 1 and gh + 2 < GH:
                        q_part(gh + 2, i)
                    if u + 1 < U:
                        exp(u + 1, i)
                    if u == U - 1:
                        act.wait_ge(scored, i * U + U)
                        split_head_outputs(0, i)
                        split_head_outputs(1, i)
                    R = rows(2 * g + k)
                    act.wait_ge(turned, i * U + u + 1)
                    if gh >= 2 and k == 0:
                        act.wait_ge(head_out, i * GH + gh - 1)
                    turn = ps_flat[:, 3 * BANK:3 * BANK + (NT + 1) * P].rearrange("p (t r) -> p t r", r=P)
                    nc.scalar.copy(pT[:, gh % 2, :, k * P:k * P + R], turn[:, :, 0:R]).then_inc(pT_out, 1)
                    if 0 <= u - U // 2 < KD:
                        p, k = w_place("WO"), u - U // 2
                        act.wait_ge(w_in[p], w_loads("WO", i) * 16)
                        nc.scalar.copy(w[:, p, 0, k, :], w_raw[:, p, 1, k, :]).then_inc(w_high, 1)

            products(qkv0, zero_now, 0)
            with act.Fori(0, L - 1) as i:
                c = now(i, act)
                attention(c)
                products(wo_m1, c, 2 * i + 1)
                products(m2_qkv, c, 2 * i + 2)
            attention(last)
            products(wo_m1, last, 2 * L - 1)

        @block.vector
        def _(dve):
            step = [0]

            def chain(ins):
                step[0] += 1
                ins.then_inc(dv, 1)
                dve.wait_ge(dv, step[0])

            dve.wait_ge(consts, CONSTS)
            dve.wait_ge(idx_in, 64)
            for a in range(2):
                nc.vector.tensor_copy(idx_f[:, 2 * a, :], idx_rows[:, 2 * a, :]).then_inc(tiles_s, 1)
                nc.vector.tensor_copy(idx_f[0:NE - P, 2 * a + 1, :], idx_rows[0:NE - P, 2 * a + 1, :]).then_inc(tiles_s, 1)
            dve.wait_ge(tiles_s, 4)
            for a, R in ((0, P), (1, NE - P)):
                chain(nc.vector.tensor_reduce(spans[0:R, 2 * a:2 * a + 1], idx_f[0:R, 2 + a, :], AX.X, ALU.min))
                chain(nc.vector.tensor_reduce(spans[0:R, 2 * a + 1:2 * a + 2], idx_f[0:R, 2 + a, :], AX.X, ALU.max))
                for n in (2 * a, 2 * a + 1):
                    nc.vector.tensor_copy(span[0:R, n, :], spans[0:R, n:n + 1].broadcast_to([R, NT])).then_inc(tiles_s, 1)
            dve.wait_ge(idx_t, 1)
            nc.vector.tensor_copy(edge[:, 0, 0:NE], ps[0:ET, 0, 0:NE]).then_inc(tiles_s, 1)
            nc.vector.tensor_copy(edge[:, 1, 0:NE], ps[0:ET, 1, 0:NE]).then_inc(tiles_s, 1)
            for a in range(2):
                nc.vector.tensor_copy(tl[:, a, :], ps[0:NT, 2 + a, 0:NE]).then_inc(tiles_s, 1)
            chain(nc.vector.tensor_copy(tl_iota[:], tl_i32[:]))
            chain(nc.vector.tensor_copy(edge_of[:], edge_of_i[:]))
            dve.wait_ge(tiles_s, 12)
            nc.vector.tensor_scalar(rel[:, 0, :], tl[:, 1, :], edge_of[:, 0:1], None, ALU.is_ge)
            chain(nc.vector.tensor_scalar(rel[:, 1, :], tl[:, 0, :], edge_of[:, 1:2], None, ALU.is_lt))
            chain(nc.vector.tensor_tensor(rel[:, 0], rel[:, 0], rel[:, 1], ALU.mult))
            chain(nc.vector.scalar_tensor_tensor(rel[:, 2], rel[:, 0], -1024.0, tl_iota[:], ALU.mult, ALU.add))
            chain(nc.vector.scalar_tensor_tensor(rel[:, 1], tl_iota[:], 1.0, rel[:, 0], ALU.add, ALU.mult))
            first_tile, beyond, some = bounds[:, 0:1], bounds[:, 1:2], bounds[:, 2:3]
            chain(nc.vector.tensor_reduce(beyond, rel[:, 1], AX.X, ALU.max))
            chain(nc.vector.tensor_reduce(first_tile, rel[:, 2], AX.X, ALU.min))
            chain(nc.vector.tensor_scalar(some, first_tile, 0.0, 1024.0, ALU.is_lt, ALU.mult))
            chain(nc.vector.tensor_tensor(first_tile, first_tile, some, ALU.add))
            chain(nc.vector.tensor_scalar(beyond, beyond, 1.0, None, ALU.max))
            chain(nc.vector.scalar_tensor_tensor(first_tile, beyond, -1.0, first_tile, ALU.add, ALU.min))
            chain(nc.vector.tensor_tensor(beyond, beyond, first_tile, ALU.subtract))
            chain(nc.vector.tensor_scalar(beyond, beyond, 0.25, 0.375, ALU.mult, ALU.add))
            nc.vector.tensor_scalar(beyond, beyond, ROUND, ROUND, ALU.add, ALU.subtract).then_inc(bounds_ready, 1)
            dve.wait_ge(bounds_turned, 1)
            chain(nc.vector.tensor_copy(parts[:], ps[0:1, 4, 0:3 * NT].rearrange("p (a j) -> p a j", j=NT)))
            chain(nc.vector.scalar_tensor_tensor(parts[:, 0, :], parts[:, 1, :], float(QUADS_AT), parts[:, 0, :],
                                                 ALU.mult, ALU.add))
            chain(nc.vector.tensor_reduce(most[:], parts[:, 1, :], AX.X, ALU.max))
            chain(nc.vector.tensor_copy(table[:, NT:NT + 1], most[:]))
            nc.vector.scalar_tensor_tensor(table[:, 0:NT], parts[:, 2, :], float(BEFORE_AT), parts[:, 0, :],
                                           ALU.mult, ALU.add).then_inc(tiles_s, 1)
            dve.wait_ge(small_in, 16 * 6)
            chain(nc.vector.tensor_scalar(eps1[:], eps1[:], 1.0, None, ALU.add))
            dve.wait_ge(tiles_s, TILES_DONE)
            dve.sem_inc(hot_used, HOT)
            with dve.Fori(0, NT // 2) as jj:
                blocks = [(dve.snap((jj * 2 + n) * P), *edge_tiles(dve, jj * 2 + n)) for n in range(2)]
                for block_start, first, quads, before in blocks:
                    with dve.Fori(0, quads) as k:
                        t = dve.snap(first + k * HOT)
                        n = dve.snap((before + k) * HOT)
                        for m in range(HOT):
                            dve.wait_ge(hot_used, n + m + 1)
                            nc.vector.tensor_scalar(hot[0:ET, m, 0:NP], iota_n[0:ET], edge[:, 0, bass.ds(t + m, 1)], None,
                                                    ALU.is_equal)
                            nc.vector.tensor_scalar(hot[0:ET, m, NP:NP + P], iota_n[0:ET, bass.ds(block_start, P)],
                                                    edge[:, 1, bass.ds(t + m, 1)], None, ALU.is_equal).then_inc(hot_ready, 1)

            def stats_begin(t):
                nc.vector.bn_stats(stat6[0:rows(t), t, :], x[0:rows(t), t, :]).then_inc(stat_s, 1)

            def stats_end(t, n):
                R = rows(t)
                dve.wait_ge(stat_s, n + 1)
                dve.sem_inc(passed)
                nc.vector.bn_aggr(mv[0:R, t, :], stat6[0:R, t, :]).then_inc(mv_ready, 1)

            def stats(t, n):
                stats_begin(t)
                stats_end(t, n)

            def mask_tile(t):
                if t == 0:
                    dve.wait_ge(counts_out, NT + 2)
                if t >= 2:
                    dve.wait_ge(mask_saved[t % 2], 16 * (t // 2))
                nc.vector.tensor_scalar(mask_log[:, t % 2, :], counts[:, t, :], 1.0, None, ALU.max).then_inc(mask_dve, 1)
                nc.vector.tensor_scalar(mask_out[:, t % 2, :], counts[:, t, :], 0.5, NOTHING, ALU.is_lt,
                                        ALU.mult).then_inc(mask_dve, 1)
                dve.wait_ge(mask_dve, 2 * t + 2)
                dve.wait_ge(mask_ln, t + 1)
                nc.vector.tensor_tensor(mask_out[:, t % 2, :], mask_out[:, t % 2, :], mask_log[:, t % 2, :],
                                        ALU.add).then_inc(mask_ready, 1)

            def noise_phases():
                freq = rep[0:32, 1:2]
                chain(nc.vector.tensor_copy(freq, rep[0:32, 0:1].bitcast(I32)))
                chain(nc.vector.tensor_scalar(freq, freq, float(np.float32(2.0 * np.pi / 16)), None, ALU.mult))
                dve.wait_ge(noise_in, 16)
                dve.wait_ge(made, l0.made["NB", KD - 1, 2])
                ph, kk = phase[0:32, 0, :], phase[0:32, 1, :]
                chain(nc.vector.tensor_scalar(ph, ph, freq, None, ALU.mult))
                chain(nc.vector.tensor_scalar(kk, ph, float(1.0 / (2.0 * np.pi)), ROUND, ALU.mult, ALU.add))
                chain(nc.vector.tensor_scalar(kk, kk, ROUND, None, ALU.subtract))
                for part in TWO_PI:
                    chain(nc.vector.scalar_tensor_tensor(ph, kk, -part, ph, ALU.mult, ALU.add))
                nc.vector.tensor_scalar(emb[0:32, 0, :], ph, 3.1415925, -3.1415925, ALU.min, ALU.max).then_inc(cond_dve, 1)
                dve.wait_ge(cond_dve, 1)
                chain(nc.vector.scalar_tensor_tensor(kk, emb[0:32, 0, :], -1.0, emb[0:32, 0, :], ALU.mult, ALU.max))
                nc.vector.tensor_scalar(emb[0:32, 1, :], kk, -1.0, float(np.pi / 2), ALU.mult, ALU.add).then_inc(cond_dve, 1)

            def silu():
                dve.wait_ge(dve_out, l0.dve_out["C1", 2, 0])
                dve.sem_inc(cond_dve, 1)
                dve.wait_ge(cond_act, 3)
                chain(nc.vector.tensor_scalar(emb[0:16, 1, :], emb[0:16, 1, :], 1.0, None, ALU.add))
                chain(nc.vector.reciprocal(emb[0:16, 1, :], emb[0:16, 1, :]))
                nc.vector.tensor_tensor(emb[0:16, 2, :], emb[0:16, 0, :], emb[0:16, 1, :], ALU.mult).then_inc(cond_dve, 1)
                chain(nc.vector.memset(emb[0:32, 3, :], 1.0))

            def condition_parts():
                dve.wait_ge(dve_out, l0.dve_out["C2", 2, 0])
                nc.vector.tensor_copy(cond[0:32, :], emb[0:32, 3, :]).then_inc(cond_dve, 1)
                dve.wait_ge(cond_dve, 5)
                nc.vector.tensor_copy(cond[64:96, :], emb[0:32, 3, :]).then_inc(cond_dve, 1)
                nc.vector.tensor_tensor(cond[32:64, :], emb[0:32, 3, :], cond[0:32, :].bitcast(F32),
                                        ALU.subtract).then_inc(cond_dve, 1)
                dve.wait_ge(cond_dve, 7)

            for kind, a, b in l0.jobs:
                if kind not in ON_VECTOR:
                    continue
                if kind == "NB" and b * KD + a < NT:
                    mask_tile(b * KD + a)
                c0, cn = GROUPS[b if kind == "NB" else a]
                if (kind, a, b) == ("C1", 0, 0):
                    noise_phases()
                dve.wait_ge(made, l0.made[kind, a, b])
                bank = ps[:, l0.bank[kind, a, b], :]
                if kind == "NB":
                    if (a, b) == (0, 0):
                        dve.wait_ge(act_out, l0.act_out["XT", NT - 1, 0])
                    nc.vector.scalar_tensor_tensor(q[:, a, c0:c0 + cn], xT[:, a, c0:c0 + cn], eps1[:, 0:1],
                                                   bank[:, 0:cn], ALU.mult, ALU.add).then_inc(dve_out, 1)
                elif kind == "C1":
                    nc.vector.tensor_scalar(emb[0:16, 0, c0:c0 + cn], bank[0:16, 0:cn], f_bias[:, 0:1], None,
                                            ALU.add).then_inc(dve_out, 1)
                    if a == 2:
                        silu()
                else:
                    nc.vector.tensor_scalar(emb[0:16, 3, c0:c0 + cn], bank[0:16, 0:cn], f_bias[:, 1:2], None,
                                            ALU.add).then_inc(dve_out, 1)
                    if a == 2:
                        condition_parts()
            nc.vector.memset(v[:, NT - 1, :], 0.0).then_inc(tails_clear, 1)

            def q_part(gh, i):
                g, h = gh // H, gh % H
                wd = rows(2 * g) + rows(2 * g + 1)
                dve.wait_ge(q_high, i * GH + gh + 1)
                nc.vector.tensor_tensor(q_parts[:, gh % 2, 1, 0:wd], q[:, h, g * 2 * P:g * 2 * P + wd],
                                        q_parts[:, gh % 2, 0, 0:wd].bitcast(F32), ALU.subtract).then_inc(q_ready, 1)

            def mask(u, i):
                g, h, k = UNITS[u]
                t = 2 * g + k
                R = rows(t)
                if h == 0:
                    loads = MASK_PLACE.count(MASK_PLACE[t])
                    nth = MASK_PLACE[:t + 1].count(MASK_PLACE[t])
                    dve.wait_ge(mask_in[MASK_PLACE[t]], i * 16 * loads + 16 * nth)
                dve.wait_ge(scored, i * U + u + 1)
                if u >= 2:
                    dve.wait_ge(turned, i * U + u - 1)
                dve.sem_inc(passed)
                nc.vector.tensor_tensor_reduce(s_of(u), ps_flat[0:R, 0:NP], masks[MASK_PLACE[t]][0:R, :],
                                               1.0, LOWEST, ALU.add, ALU.max, small[0:R, u % 2, 0:1]).then_inc(masked, 1)
                dve.wait_ge(masked, i * U + u + 1)
                nc.vector.tensor_scalar(small[0:R, u % 2, 1:2], small[0:R, u % 2, 0:1], -1.0, None,
                                        ALU.mult).then_inc(negm_s, 1)

            def head_output(gh, i):
                g, h = gh // H, gh % H
                wd = rows(2 * g) + rows(2 * g + 1)
                dve.wait_ge(summed, i * GH + gh + 1)
                dve.wait_ge(pT_out, i * U + 2 * gh + 2)
                nc.vector.tensor_tensor(q[:, h, g * 2 * P:g * 2 * P + wd], ps[:, 6 + gh % 2, 0:wd],
                                        pT[:, gh % 2, NT, 0:wd], ALU.mult).then_inc(head_out, 1)

            def products(jl, c, norm):
                before = (norm + 1) * NT
                for kind, a, b in jl.jobs:
                    R = rows(a) if kind in ("Y", "N0", "T", "V", "WO", "M2") else P
                    if kind == "W":
                        p = w_place(a)
                        n = w_index(a, c.block)
                        dve.wait_ge(w_high, w_parts(a, c.block))
                        nc.vector.tensor_tensor(w[:, p, 1, :, :], w_raw[:, p, 1, :, :], w[:, p, 0, :, :].bitcast(F32),
                                                ALU.subtract).then_inc(w_ready, 1)
                        continue
                    if kind == "AV":
                        head_output(GH - 1, c.block)
                        continue
                    if kind == "S0":
                        mask(0, c.block + 1)
                        continue
                    if kind == "OS":
                        continue
                    if kind == "QP":
                        q_part(a, c.block + 1)
                        continue
                    if kind == "N0":
                        dve.wait_ge(rstd_ready, y_stats(a) + 1)
                        nc.vector.tensor_scalar(x[0:R, a, :], x[0:R, a, :], mv[0:R, a, 0:1], rstd[0:R, a:a + 1],
                                                ALU.subtract, ALU.mult).then_inc(l0_ready, 1)
                        dve.wait_ge(l0_ready, a + 1)
                        stats(a, n0_stats(a))
                        if a == NT - 1:
                            nc.vector.memset(kh[:, :, :, N:NP].bitcast(F32), 0.0).then_inc(tails_clear, 1)
                            dve.wait_ge(tails_clear, 2)
                        continue
                    if kind == "M1":
                        c0, cn = GROUPS[b]
                        n = b * KD + a
                        dve.wait_ge(h_high, c.block * 3 * KD + n + 1)
                        nc.vector.tensor_tensor(kh[:, 1, a, c0:c0 + cn], relu_out[:, n % 2, 0:cn],
                                                kh[:, 0, a, c0:c0 + cn].bitcast(F32), ALU.subtract).then_inc(h_ready, 1)
                        continue
                    if kind == "FS":
                        norm_tile(jl, c, before + a if jl is not qkv0 else n0_stats(a), a,
                                  None if jl is qkv0 or a == NT - 1 else before + a + 1)
                        continue
                    if kind == "FB":
                        continue
                    dve.wait_ge(made, c.made + jl.made[kind, a, b])
                    if kind in ("T", "K"):
                        dve.wait_ge(act_out, c.act + jl.act_out[kind, a, b])
                    bank = ps[:, jl.bank[kind, a, b], :]
                    mine = c.dve + jl.dve_out[kind, a, b]
                    if kind == "T":
                        turned_tile = bank.rearrange("p (k r) -> p k r", r=P)[:, :, 0:R]
                        high = yT[:, 0, :, a * P:a * P + R].bitcast(F32)
                        nc.vector.tensor_tensor(yT[:, 1, :, a * P:a * P + R], turned_tile, high,
                                                ALU.subtract).then_inc(dve_out, 1)
                    elif kind == "Q":
                        c0, cn = GROUPS[b]
                        if (a, b) == (0, 0):
                            dve.wait_ge(bqk_in, c.block * 32 + 64)
                        nc.vector.tensor_scalar(q[:, a, c0:c0 + cn], bank[:, 0:cn], col_bias[:, 0, a:a + 1],
                                                float(P ** -0.5), ALU.add, ALU.mult).then_inc(dve_out, 1)
                    elif kind == "K":
                        c0, cn = GROUPS[b]
                        nc.vector.scalar_tensor_tensor(kh[:, 1, a, c0:c0 + cn], bank[:, 0:cn], col_bias[:, 1, a:a + 1],
                                                       kh[:, 0, a, c0:c0 + cn].bitcast(F32), ALU.add,
                                                       ALU.subtract).then_inc(dve_out, 1)
                    elif kind == "V":
                        if a == 0:
                            dve.wait_ge(bv_in, c.block * 16 + 32)
                        nc.vector.tensor_tensor(v[0:R, a, :], bank[0:R, :], row_bias[0:R, 0, :],
                                                ALU.add).then_inc(dve_out, 1)
                    elif kind == "Y":
                        dve.wait_ge(l0_twice, 2 * a + 2)
                        nc.vector.tensor_tensor(x[0:R, a, :], bank[0:R, :], x[0:R, a, :], ALU.add).then_inc(dve_out, 1)
                        dve.wait_ge(dve_out, mine)
                        stats(a, y_stats(a))
                    else:
                        second = kind == "M2"
                        if jl is m2_last:
                            dve.wait_ge(added, (a - 2) % NT + 1)
                        dve.wait_ge(biased, (2 * c.block + second) * NT + a + 1)
                        nc.vector.tensor_tensor(x[0:R, a, :], bank[0:R, :], x[0:R, a, :], ALU.add).then_inc(dve_out, 1)
                        if jl is not m2_last and a >= 1:
                            continue
                        dve.wait_ge(dve_out, mine)
                        stats(a, (2 * c.block + 2 + second) * NT + a)
                        if jl is m2_last and a >= 1:
                            last_norm(a - 1)

            def last_norm(t):
                R = rows(t)
                dve.wait_ge(rstd_ready, (2 * L + 1) * NT + t + 1)
                nc.vector.tensor_scalar(x[0:R, t, :], x[0:R, t, :], mv[0:R, t, 0:1], rstd[0:R, t:t + 1],
                                        ALU.subtract, ALU.mult).then_inc(y_out, 1)

            def norm_tile(jl, c, n, a, n_next):
                R = rows(a)
                dve.wait_ge(rstd_ready, n + 1)
                dve.wait_ge(made, c.made + jl.made["FS", a, 0])
                if a >= 3:
                    dve.wait_ge(made, c.made + jl.made["T", a - 3, 0])
                nc.vector.scalar_tensor_tensor(y[0:R, a % 3, :], x[0:R, a, :], mv[0:R, a, 0:1],
                                               ps[0:R, jl.bank["FS", a, 0], :], ALU.subtract, ALU.mult).then_inc(dve_out, 1)
                if n_next is not None:
                    dve.wait_ge(dve_out, c.dve + jl.dve_out["FS", a, 0] - 1)
                    stats_begin(a + 1)
                dve.wait_ge(dve_out, c.dve + jl.dve_out["FS", a, 0])
                dve.wait_ge(made, c.made + jl.made["FB", a, 0])
                nc.vector.scalar_tensor_tensor(y[0:R, a % 3, :], y[0:R, a % 3, :], rstd[0:R, a:a + 1],
                                               ps[0:R, jl.bank["FB", a, 0], :], ALU.mult, ALU.add).then_inc(dve_out, 1)
                if n_next is not None:
                    stats_end(a + 1, n_next)

            def attention(c):
                i = c.block

                for u, (g, h, k) in enumerate(UNITS):
                    R = rows(2 * g + k)
                    dve.wait_ge(exp_done, i * U + u + 1)
                    nc.vector.tensor_scalar(small[0:R, u % 2, 2:3], small[0:R, u % 2, 2:3], 0.5, None,
                                            ALU.max).then_inc(den_s, 1)
                    dve.wait_ge(den_s, (i * U + u) * 2 + 1)
                    nc.vector.reciprocal(small[0:R, u % 2, 3:4], small[0:R, u % 2, 2:3]).then_inc(den_s, 1)
                    dve.wait_ge(den_s, (i * U + u) * 2 + 2)
                    if u >= 1:
                        dve.wait_ge(turned, i * U + u)
                    nc.vector.tensor_scalar(rep[0:R, :], ident[0:R, :], 0.0, small[0:R, u % 2, 3:4], ALU.mult,
                                            ALU.add).then_inc(rep_ready, 1)
                    if u + 1 < U:
                        mask(u + 1, i)
                    if k == 1 and u // 2 + 2 < GH:
                        q_part(u // 2 + 2, i)
                    if k == 1 and u >= 2:
                        head_output(u // 2 - 1, i)
                    if 1 <= u - U // 2 <= KD:
                        p, kk = w_place("WO"), u - U // 2 - 1
                        dve.wait_ge(w_high, w_parts("WO", i) - KD + 1 + kk)
                        nc.vector.tensor_tensor(w[:, p, 1, kk, :], w_raw[:, p, 1, kk, :], w[:, p, 0, kk, :].bitcast(F32),
                                                ALU.subtract).then_inc(w_ready, 1)

            products(qkv0, zero_now, 0)
            with dve.Fori(0, L - 1) as i:
                c = now(i, dve)
                attention(c)
                products(wo_m1, c, 2 * i + 1)
                products(m2_qkv, c, 2 * i + 2)
            attention(last)
            products(wo_m1, last, 2 * L - 1)
            products(m2_last, last, 2 * L)
            last_norm(NT - 1)

        @block.tensor
        def _(pe):
            mm = nc.tensor.matmul

            def bank_of(jl, key, c):
                old, its = jl.eight_before(jl.products.index(key))
                if old in its.dve_out:
                    pe.wait_ge(dve_out, c.dve + its.dve_out[old])
                elif old is not None:
                    pe.wait_ge(act_out, c.act + its.act_out[old])
                return ps[:, jl.bank[key], :]

            pe.wait_ge(consts, 6)
            pe.wait_ge(tiles_s, 8)
            for a in range(2):
                nc.tensor.transpose(ps[0:ET, a, 0:P], idx_f[:, 2 * a, :], ident[:])
                nc.tensor.transpose(ps[0:ET, a, P:NE], idx_f[0:NE - P, 2 * a + 1, :], ident[0:NE - P, 0:NE - P])
            for a in range(2):
                nc.tensor.transpose(ps[0:NT, 2 + a, 0:P], span[:, a, :], ident[:])
                mine = nc.tensor.transpose(ps[0:NT, 2 + a, P:NE], span[0:NE - P, 2 + a, :], ident[0:NE - P, 0:NE - P])
            mine.then_inc(idx_t, 1)
            pe.wait_ge(consts, CONSTS)
            pe.wait_ge(bounds_ready, 1)
            for a, (value, onto) in enumerate(((0, ident), (1, ident), (1, earlier))):
                mine = mm(ps[0:1, 4, a * NT:(a + 1) * NT], bounds[:, value:value + 1], onto[0:NT, 0:NT], start=True, stop=True)
            mine.then_inc(bounds_turned, 1)
            pe.wait_ge(tiles_s, TILES_DONE)
            pe.wait_ge(x_in_s, 32)
            for t in range(NT):
                R = rows(t)
                bank = bank_of(l0, ("XT", t, 0), zero_now)
                for k in range(KD):
                    mine = nc.tensor.transpose(bank[:, k * P:k * P + R], x[0:R, t, k * P:(k + 1) * P], ident[0:R, 0:R])
                mine.then_inc(made, 1)
            pe.wait_ge(act_out, NT)
            def count_block(j, place, quads, before):
                pe.wait_ge(counts_out, j + 1)

                def quad(n, first):
                    for m in range(HOT):
                        pe.wait_ge(hot_ready, n + m + 1)
                        for i in range(NT):
                            c0 = place * 3 * BANK + i * P
                            mine = mm(ps_flat[:, c0:c0 + P], hot[0:ET, m, i * P:(i + 1) * P], hot[0:ET, m, NP:NP + P],
                                      start=first and m == 0 and i % 4 == 0, stop=True, skip_group_check=True)
                        mine.then_inc(hot_used, 1)

                quad(pe.snap(before * HOT), True)
                with pe.Fori(1, quads) as k:
                    quad(pe.snap((before + k) * HOT), False)

            pe.sem_inc(counts_out, 2)
            with pe.Fori(0, NT // 2) as jj:
                blocks = [edge_tiles(pe, jj * 2 + place)[1:] for place in range(2)]
                for place, (quads, before) in enumerate(blocks):
                    count_block(jj * 2 + place, place, quads, before)
            pe.wait_ge(counts_out, NT + 2)
            pe.wait_ge(x_split, 2)

            def neighbour_sums(left, right):
                for kind, a, b in l0.jobs:
                    if kind == "NB":
                        c0, cn = GROUPS[b]
                        bank = bank_of(l0, (kind, a, b), zero_now)
                        for n in range(2):
                            for k in range(NT):
                                R = rows(k)
                                mine = mm(bank[:, 0:cn], left[n](R, k)[:, a * P:(a + 1) * P], right(counts[0:R, k, c0:c0 + cn]),
                                          start=(n == 0 and k == 0), stop=(n == 1 and k == NT - 1))
                        mine.then_inc(made, 1)

            most_quads = pe.value_load(table[0:1, NT:NT + 1], min_val=1, max_val=NE // HOT + 1)
            with pe.If(most_quads <= EXACT // (HOT * ET)):
                neighbour_sums((lambda R, k: x_low[0:R, k, :], lambda R, k: x_high[0:R, k, :]), lambda part: part.bitcast(F32R))
            with pe.Else():
                neighbour_sums((lambda R, k: x_low[0:R, k, :].bitcast(F32), lambda R, k: x_high[0:R, k, :].bitcast(F32)),
                               lambda part: part)

            for kind, a, b in l0.jobs:
                if kind in STEPS or kind in ("XT", "NB"):
                    continue
                bank = bank_of(l0, (kind, a, b), zero_now)
                if kind == "C1":
                    pe.wait_ge(cond_act, 2)
                    pe.wait_ge(small_in, 16 * 6)
                    c0, cn = GROUPS[a]
                    mine = mm(bank[0:16, 0:cn], f_mats[0:64, 0:16], phase[0:64, 0, c0:c0 + cn], start=True, stop=True)
                elif kind == "C2":
                    pe.wait_ge(cond_dve, 4)
                    c0, cn = GROUPS[a]
                    mine = mm(bank[0:16, 0:cn], f_mats[0:16, 16:32], emb[0:16, 2, c0:c0 + cn], start=True, stop=True)
                elif kind == "H":
                    c0, cn = GROUPS[b]
                    if a == 0:
                        pe.wait_ge(w1_in, 16)
                        pe.wait_ge(dve_out, l0.dve_out["NB", KD - 1, b])
                    for k in range(KD):
                        mine = mm(bank[:, 0:cn], w1_l0[:, k, a * P:(a + 1) * P], q[:, k, c0:c0 + cn],
                                  start=(k == 0), stop=(k == KD - 1))
                mine.then_inc(made, 1)

            PARTS = ((1, 0), (0, 1), (0, 0))

            def three_passes(to, left, right, first=True, final=True):
                for n, (a, b) in enumerate(PARTS):
                    mine = mm(to, left(a), right(b), start=first and n == 0, stop=final and n == 2)
                return mine

            def scores(u, i):
                g, h, k = UNITS[u]
                R = rows(2 * g + k)
                gh = u // 2
                if k == 0:
                    pe.wait_ge(q_ready, i * GH + gh + 1)
                if u >= 1:
                    pe.wait_ge(masked, i * U + u)
                for b, (c0, cn) in enumerate(((0, 512), (512, 512), (1024, 256))):
                    mine = three_passes(ps[0:R, b, 0:cn], lambda n: q_parts[:, gh % 2, n, k * P:k * P + R],
                                        lambda n: kh[:, n, h, c0:c0 + cn])
                mine.then_inc(scored, 1)

            def weigh(gh, part, i):
                g, h = gh // H, gh % H
                wd = rows(2 * g) + rows(2 * g + 1)
                if part == 0:
                    pe.wait_ge(pT_out, i * U + 2 * gh + 2)
                    if gh >= 2:
                        pe.wait_ge(head_out, i * GH + gh - 1)
                for t in range(5 * part, 5 * part + 5):
                    mine = mm(ps[:, 6 + gh % 2, 0:wd], v[:, t, h * P:(h + 1) * P], pT[:, gh % 2, t, 0:wd],
                              start=(t == 0), stop=(t == NT - 1))
                if part == 1:
                    mine.then_inc(summed, 1)

            def products(jl, c, norm):
                for kind, a, b in jl.jobs:
                    if kind == "AV":
                        for part in range(2):
                            weigh(GH - 1, part, c.block)
                    if kind == "S0":
                        pe.wait_ge(dve_out, c.dve + jl.dve_out["V", NT - 4, 0])
                        pe.wait_ge(tails_clear, 2)
                        scores(0, c.block + 1)
                    if kind in STEPS:
                        continue
                    if kind == "WO" and a == 2:
                        pe.wait_ge(head_out, c.block * GH + GH)
                    bank = bank_of(jl, (kind, a, b), c)
                    if kind in ("FS", "FB"):
                        R = rows(a)
                        if a == 0 and kind == "FS":
                            pe.wait_ge(film_ready, norm + 1)
                            if jl is qkv0:
                                pe.wait_ge(cond_dve, 7)
                        c0 = 0 if kind == "FS" else D
                        mine = mm(bank[0:R, :], cond[:, a * P:a * P + R], film[:, c0:c0 + D], start=True, stop=True)
                    elif kind == "Y":
                        R = rows(a)
                        if a == 0:
                            pe.wait_ge(w2_in, 16)
                        pe.wait_ge(act_out, l0.act_out["H", H1 // P - 1, min(a // 4, 2)])
                        for k in range(H1 // P):
                            mine = mm(bank[0:R, :], hidden[:, k, a * P:a * P + R], w2_l0[:, k, :], start=(k == 0),
                                      stop=(k == H1 // P - 1))
                    elif kind == "T":
                        R = rows(a)
                        pe.wait_ge(dve_out, c.dve + jl.dve_out["FB", a, 0])
                        for k in range(KD):
                            mine = nc.tensor.transpose(bank[:, k * P:k * P + R], y[0:R, a % 3, k * P:(k + 1) * P],
                                                       ident[0:R, 0:R])
                    elif kind in ("Q", "K", "M1"):
                        c0, cn = GROUPS[b]
                        p = w_place(kind)
                        if (a, b) == (0, 0):
                            pe.wait_ge(w_ready, w_parts(kind, c.block))
                        if a == 0 and kind != "K":
                            pe.wait_ge(dve_out, c.dve + jl.dve_out["T", TILES_OF[b][-1], 0])
                        for k in range(KD):
                            mine = three_passes(bank[:, 0:cn], lambda n: w[:, p, n, k, a * P:(a + 1) * P],
                                                lambda n: yT[:, n, k, c0:c0 + cn], k == 0, k == KD - 1)
                    else:
                        R = rows(a)
                        p = w_place(kind)
                        left = yT if kind == "V" else kh
                        if a == 0:
                            pe.wait_ge(w_ready, w_parts(kind, c.block))
                        if kind == "WO":
                            pe.wait_ge(o_ready, c.block * NT + a + 1)
                        if kind == "M2":
                            pe.wait_ge(h_ready, c.block * 3 * KD + KD * (min(a // 4, 2) + 1))
                        for k in range(KD):
                            mine = three_passes(bank[0:R, :], lambda n: left[:, n, k, a * P:a * P + R],
                                                lambda n: w[:, p, n, k, :], k == 0, k == KD - 1)
                    mine.then_inc(made, 1)

            def attention(c):
                i = c.block

                pe.wait_ge(dve_out, c.dve)
                for u, (g, h, k) in enumerate(UNITS):
                    R = rows(2 * g + k)
                    if u + 1 < U:
                        scores(u + 1, i)
                    if u >= 2:
                        weigh(u // 2 - 1, k, i)
                    pe.wait_ge(exp_done, i * U + u + 1)
                    pe.wait_ge(rep_ready, i * U + u + 1)
                    if u >= 1:
                        pe.wait_ge(pT_out, i * U + u)
                    turn = ps_flat[:, 3 * BANK:]
                    for t in range(NT):
                        nc.tensor.transpose(turn[:, t * P:t * P + R], s_of(u)[:, t * P:(t + 1) * P], ident[0:R, 0:R])
                    nc.tensor.transpose(turn[:, NT * P:NT * P + R], rep[0:R, :], ident[0:R, 0:R]).then_inc(turned, 1)

            products(qkv0, zero_now, 0)
            with pe.Fori(0, L - 1) as i:
                c = now(i, pe)
                attention(c)
                products(wo_m1, c, 2 * i + 1)
                products(m2_qkv, c, 2 * i + 2)
            attention(last)
            products(wo_m1, last, 2 * L - 1)
            products(m2_last, last, 2 * L)


_INS = ['x', 'src', 'dst', 'node_vec1', 'L0_gnn_W1', 'L0_gnn_b1', 'L0_gnn_W2', 'L0_gnn_b2', 'L0_gnn_eps',
        'L1_gnn_f_w1', 'L1_gnn_f_b1', 'L1_gnn_f_w2', 'L1_gnn_f_b2', 'L1_gnn_s1_w', 'L1_gnn_s1_b', 'L1_gnn_b1_w',
        'L1_gnn_b1_b', 'L1_gnn_wq', 'L1_gnn_bq', 'L1_gnn_wk', 'L1_gnn_bk', 'L1_gnn_wv', 'L1_gnn_bv', 'L1_gnn_wo',
        'L1_gnn_bo', 'L1_gnn_s2_w', 'L1_gnn_s2_b', 'L1_gnn_b2_w', 'L1_gnn_b2_b', 'L1_gnn_m_w1', 'L1_gnn_m_b1',
        'L1_gnn_m_w2', 'L1_gnn_m_b2']


def kernel(**inputs):
    import numpy as _np
    import concourse.bacc as _bacc
    from concourse import mybir as _mybir
    from concourse.bass_utils import run_bass_kernel_spmd as _run

    nc = _bacc.Bacc("TRN2", target_bir_lowering=False, num_devices=1)
    arrays, args = {}, []
    for name in _INS:
        a = _np.ascontiguousarray(inputs[name])
        arrays[f"in_{name}_dram"] = a
        args.append(nc.dram_tensor(f"in_{name}_dram", a.shape, _mybir.dt.from_np(a.dtype), kind="ExternalInput").ap())
    args.append(nc.dram_tensor("out_dram", (N, D), F32, kind="ExternalOutput").ap())
    gnn_kernel(nc, *args)
    r = _run(nc, [arrays], core_ids=[0])
    return r.results[0]["out_dram"]
```
